# Optimizing a Trainium2 kernel written in Bass

```python
import numpy as np
import jax
import jax.numpy as jnp

def _softmax(x, axis=-1):
    return jax.nn.softmax(x, axis=axis)

def _gelu(x):
    return jax.nn.gelu(x, approximate=True)

def _silu(x):
    return jax.nn.silu(x)

def _sigmoid(x):
    return jax.nn.sigmoid(x)

def _layernorm(x, axis=-1, eps=1e-05):
    m = jnp.mean(x, axis=axis, keepdims=True)
    v = jnp.var(x, axis=axis, keepdims=True)
    return (x - m) / jnp.sqrt(v + eps)

def _scatter_add(tgt, idx, src, axis=0):
    return tgt.at[idx].add(src)

def _segment_sum(src, seg, n):
    return jax.ops.segment_sum(src, seg, n)
kernel_name = 'mk_gnn_resnorm_d4_gnn_r32_fa9644'

def setup_inputs(seed: int=0):
    np.random.seed(seed)
    _w = jnp.asarray

    def _rec_inputs():
        import jax
        import jax.numpy as jnp
        _gk = jax.random.key(seed)
        x = -0.000202 + 1 * jax.random.normal(jax.random.fold_in(_gk, 1), (3125, 128), jnp.float32)
        src = jax.random.randint(jax.random.fold_in(_gk, 2), (50000,), 0, 3125, jnp.int32)
        dst = jax.random.randint(jax.random.fold_in(_gk, 3), (50000,), 0, 3125, jnp.int32)
        _o = jnp.argsort(dst, stable=True)
        src = src[_o]
        dst = dst[_o]
        edge_type_8 = jax.random.randint(jax.random.fold_in(_gk, 13), (50000,), 0, 8, jnp.int32)
        return (x, src, dst, edge_type_8)
    x, src, dst, edge_type_8 = _rec_inputs()

    def _L0_gnn_setup():
        import jax, jax.numpy as jnp
        import numpy as np
        N = 50000
        E = 25000
        IN = 128
        H = 4
        C = 32
        NEG_SLOPE = 0.2

        def gat_conv(x, src, dst, W, a_src, a_dst, bias):
            n = x.shape[0]
            h = (x @ W).reshape(n, H, C)
            alpha_src = jnp.einsum('nhc,hc->nh', h, a_src)
            alpha_dst = jnp.einsum('nhc,hc->nh', h, a_dst)
            e = jax.nn.leaky_relu(alpha_src[src] + alpha_dst[dst], NEG_SLOPE)
            emax = jax.ops.segment_max(e, dst, num_segments=n)
            emax = jnp.where(jnp.isfinite(emax), emax, 0.0)
            ex = jnp.exp(e - emax[dst])
            denom = jax.ops.segment_sum(ex, dst, num_segments=n)
            alpha = ex / denom[dst]
            msg = h[src] * alpha[:, :, None]
            out = jax.ops.segment_sum(msg, dst, num_segments=n)
            return out.reshape(n, H * C) + bias
        key = jax.random.key(seed)
        ks = jax.random.split(key, 20)
        inp = {'x': jax.random.normal(ks[0], (N, IN), dtype=jnp.float32), 'edge_index': jax.random.randint(ks[1], (2, E), 0, N, dtype=jnp.int64)}
        for i in range(4):
            k = jax.random.split(ks[2 + i], 4)
            inp[f'W{i + 1}'] = jax.random.normal(k[0], (IN, H * C), dtype=jnp.float32) * 0.08
            inp[f'as{i + 1}'] = jax.random.normal(k[1], (H, C), dtype=jnp.float32) * 0.08
            inp[f'ad{i + 1}'] = jax.random.normal(k[2], (H, C), dtype=jnp.float32) * 0.08
            inp[f'b{i + 1}'] = jnp.zeros((H * C,), dtype=jnp.float32)
        return inp
    _L0_gnn_all = _L0_gnn_setup()
    _L0_gnn_in = {k: v for k, v in _L0_gnn_all.items() if k in ('W1', 'as1', 'ad1', 'b1', 'W2', 'as2', 'ad2', 'b2', 'W3', 'as3', 'ad3', 'b3', 'W4', 'as4', 'ad4', 'b4')}
    del _L0_gnn_all

    def _L1_gnn_setup():
        import jax, jax.numpy as jnp
        import numpy as np
        N, E = (50000, 25000)
        IN, OUT, R, B = (128, 128, 8, 4)
        LN_EPS = 1e-05
        key = jax.random.key(seed)
        ks = jax.random.split(key, 9)
        x = jax.random.normal(ks[0], (N, IN), dtype=jnp.float32)
        edge_index = jax.random.randint(ks[1], (2, E), 0, N, dtype=jnp.int64)
        edge_type = jax.random.randint(ks[2], (E,), 0, R, dtype=jnp.int64)
        weight = jax.random.normal(ks[3], (B, IN, OUT), dtype=jnp.float32) * (2.0 / (IN + OUT)) ** 0.5
        alpha = jax.random.normal(ks[4], (R, B), dtype=jnp.float32) * (2.0 / (R + B)) ** 0.5
        bias = jnp.zeros((OUT,), dtype=jnp.float32)
        weight_self_loop = jax.random.normal(ks[5], (IN, OUT), dtype=jnp.float32) * (2.0 / (IN + OUT)) ** 0.5
        ln_gamma = jnp.ones((OUT,), dtype=jnp.float32)
        ln_beta = jnp.zeros((OUT,), dtype=jnp.float32)
        return {'x': x, 'edge_index': edge_index, 'edge_type': edge_type, 'weight': weight, 'alpha': alpha, 'bias': bias, 'weight_self_loop': weight_self_loop, 'ln_gamma': ln_gamma, 'ln_beta': ln_beta}
    _L1_gnn_all = _L1_gnn_setup()
    _L1_gnn_in = {k: v for k, v in _L1_gnn_all.items() if k in ('weight', 'alpha', 'bias', 'weight_self_loop', 'ln_gamma', 'ln_beta')}
    del _L1_gnn_all

    def _L2_gnn_setup():
        import jax, jax.numpy as jnp
        import numpy as np
        N = 3125
        E = 25000
        D = 128
        OUT = 128
        key = jax.random.key(seed)
        k = jax.random.split(key, 6)
        x = jax.random.normal(k[0], (N, D), dtype=jnp.float32)
        edge_index = jax.random.randint(k[1], (2, E), 0, N, dtype=jnp.int64)
        Wl = jax.random.normal(k[2], (D, OUT), dtype=jnp.float32) / np.sqrt(D)
        bl = jax.random.normal(k[3], (OUT,), dtype=jnp.float32) * 0.01
        Wr = jax.random.normal(k[4], (D, OUT), dtype=jnp.float32) / np.sqrt(D)
        br = jax.random.normal(k[5], (OUT,), dtype=jnp.float32) * 0.01
        return {'x': x, 'edge_index': edge_index, 'Wl': Wl, 'bl': bl, 'Wr': Wr, 'br': br}
    _L2_gnn_all = _L2_gnn_setup()
    _L2_gnn_in = {k: v for k, v in _L2_gnn_all.items() if k in ('Wl', 'bl', 'Wr', 'br')}
    del _L2_gnn_all

    def _L3_gnn_setup():
        import jax, jax.numpy as jnp
        import numpy as np
        N_NODES = 50000
        N_EDGES = 25000
        IN_FEAT = 128
        OUT_FEAT = 128
        key = jax.random.key(seed)
        k_h, k_src, k_dst, k_w, k_b = jax.random.split(key, 5)
        h = jax.random.normal(k_h, (N_NODES, IN_FEAT), dtype=jnp.float32)
        src = jax.random.randint(k_src, (N_EDGES,), 0, N_NODES, dtype=jnp.int64)
        dst = jax.random.randint(k_dst, (N_EDGES,), 0, N_NODES, dtype=jnp.int64)
        W = jax.random.normal(k_w, (OUT_FEAT, 2 * IN_FEAT), dtype=jnp.float32) / np.sqrt(2 * IN_FEAT)
        b = jax.random.normal(k_b, (OUT_FEAT,), dtype=jnp.float32) * 0.01
        return {'h': h, 'src': src, 'dst': dst, 'W': W, 'b': b}
    _L3_gnn_all = _L3_gnn_setup()
    _L3_gnn_in = {k: v for k, v in _L3_gnn_all.items() if k in ('W', 'b')}
    del _L3_gnn_all
    return {'x': x, 'src': src, 'dst': dst, 'edge_type_8': edge_type_8, 'L0_gnn_W1': _L0_gnn_in['W1'], 'L0_gnn_as1': _L0_gnn_in['as1'], 'L0_gnn_ad1': _L0_gnn_in['ad1'], 'L0_gnn_b1': _L0_gnn_in['b1'], 'L0_gnn_W2': _L0_gnn_in['W2'], 'L0_gnn_as2': _L0_gnn_in['as2'], 'L0_gnn_ad2': _L0_gnn_in['ad2'], 'L0_gnn_b2': _L0_gnn_in['b2'], 'L0_gnn_W3': _L0_gnn_in['W3'], 'L0_gnn_as3': _L0_gnn_in['as3'], 'L0_gnn_ad3': _L0_gnn_in['ad3'], 'L0_gnn_b3': _L0_gnn_in['b3'], 'L0_gnn_W4': _L0_gnn_in['W4'], 'L0_gnn_as4': _L0_gnn_in['as4'], 'L0_gnn_ad4': _L0_gnn_in['ad4'], 'L0_gnn_b4': _L0_gnn_in['b4'], 'L1_gnn_weight': _L1_gnn_in['weight'], 'L1_gnn_alpha': _L1_gnn_in['alpha'], 'L1_gnn_bias': _L1_gnn_in['bias'], 'L1_gnn_weight_self_loop': _L1_gnn_in['weight_self_loop'], 'L1_gnn_ln_gamma': _L1_gnn_in['ln_gamma'], 'L1_gnn_ln_beta': _L1_gnn_in['ln_beta'], 'L2_gnn_Wl': _L2_gnn_in['Wl'], 'L2_gnn_bl': _L2_gnn_in['bl'], 'L2_gnn_Wr': _L2_gnn_in['Wr'], 'L2_gnn_br': _L2_gnn_in['br'], 'L3_gnn_W': _L3_gnn_in['W'], 'L3_gnn_b': _L3_gnn_in['b']}

def reference(x, src, dst, edge_type_8, L0_gnn_W1, L0_gnn_as1, L0_gnn_ad1, L0_gnn_b1, L0_gnn_W2, L0_gnn_as2, L0_gnn_ad2, L0_gnn_b2, L0_gnn_W3, L0_gnn_as3, L0_gnn_ad3, L0_gnn_b3, L0_gnn_W4, L0_gnn_as4, L0_gnn_ad4, L0_gnn_b4, L1_gnn_weight, L1_gnn_alpha, L1_gnn_bias, L1_gnn_weight_self_loop, L1_gnn_ln_gamma, L1_gnn_ln_beta, L2_gnn_Wl, L2_gnn_bl, L2_gnn_Wr, L2_gnn_br, L3_gnn_W, L3_gnn_b):
    import jax
    import jax.numpy as jnp

    def _L0_gnn_ref(x, edge_index, W1, as1, ad1, b1, W2, as2, ad2, b2, W3, as3, ad3, b3, W4, as4, ad4, b4):
        import jax, jax.numpy as jnp
        import numpy as np
        N = 50000
        E = 25000
        IN = 128
        H = 4
        C = 32
        NEG_SLOPE = 0.2

        def gat_conv(x, src, dst, W, a_src, a_dst, bias):
            n = x.shape[0]
            h = (x @ W).reshape(n, H, C)
            alpha_src = jnp.einsum('nhc,hc->nh', h, a_src)
            alpha_dst = jnp.einsum('nhc,hc->nh', h, a_dst)
            e = jax.nn.leaky_relu(alpha_src[src] + alpha_dst[dst], NEG_SLOPE)
            emax = jax.ops.segment_max(e, dst, num_segments=n)
            emax = jnp.where(jnp.isfinite(emax), emax, 0.0)
            ex = jnp.exp(e - emax[dst])
            denom = jax.ops.segment_sum(ex, dst, num_segments=n)
            alpha = ex / denom[dst]
            msg = h[src] * alpha[:, :, None]
            out = jax.ops.segment_sum(msg, dst, num_segments=n)
            return out.reshape(n, H * C) + bias
        loops = jnp.arange(N, dtype=edge_index.dtype)
        src = jnp.concatenate([edge_index[0], loops])
        dst = jnp.concatenate([edge_index[1], loops])
        x1 = jax.nn.relu(gat_conv(x, src, dst, W1, as1, ad1, b1))
        x2 = jax.nn.relu(gat_conv(x1, src, dst, W2, as2, ad2, b2))
        x3 = jax.nn.relu(gat_conv(x2, src, dst, W3, as3, ad3, b3))
        x4 = gat_conv(x3, src, dst, W4, as4, ad4, b4)
        return x4

    def _L1_gnn_ref(x, edge_index, edge_type, weight, alpha, bias, weight_self_loop, ln_gamma, ln_beta):
        import jax, jax.numpy as jnp
        import numpy as np
        N, E = (50000, 25000)
        IN, OUT, R, B = (128, 128, 8, 4)
        LN_EPS = 1e-05
        n = x.shape[0]
        row, col = (edge_index[0], edge_index[1])
        ones = jnp.ones((edge_type.shape[0],), dtype=x.dtype)
        deg = jax.ops.segment_sum(ones, row, num_segments=n)
        inv_deg = jnp.where(deg > 0, 1.0 / deg, 0.0)
        ew = inv_deg[row]
        W = jnp.einsum('rb,bio->rio', alpha, weight)
        h = jnp.einsum('ni,rio->rno', x, W)
        msg = ew[:, None] * h[edge_type, col]
        agg = jax.ops.segment_sum(msg, row, num_segments=n)
        mu = jnp.mean(agg, axis=-1, keepdims=True)
        var = jnp.var(agg, axis=-1, keepdims=True)
        out = (agg - mu) / jnp.sqrt(var + LN_EPS) * ln_gamma + ln_beta
        out = out + bias
        out = out + x @ weight_self_loop
        return out

    def _L2_gnn_ref(x, edge_index, Wl, bl, Wr, br):
        import jax, jax.numpy as jnp
        import numpy as np
        N = 3125
        E = 25000
        D = 128
        OUT = 128
        n = x.shape[0]
        tgt = edge_index[0]
        nbr = edge_index[1]
        agg_sum = jax.ops.segment_sum(x[nbr], tgt, num_segments=n)
        deg = jax.ops.segment_sum(jnp.ones((edge_index.shape[1],), x.dtype), tgt, num_segments=n)
        agg = agg_sum / jnp.maximum(deg, 1.0)[:, None]
        out = jax.nn.relu(x @ Wl + bl + agg @ Wr + br)
        norm = jnp.linalg.norm(out, axis=1, keepdims=True) + 1e-06
        return out / norm

    def _L3_gnn_ref(h, src, dst, W, b):
        import jax, jax.numpy as jnp
        import numpy as np
        N_NODES = 50000
        N_EDGES = 25000
        IN_FEAT = 128
        OUT_FEAT = 128
        n = h.shape[0]
        msg = h[src]
        agg = jax.ops.segment_sum(msg, dst, num_segments=n)
        deg = jax.ops.segment_sum(jnp.ones((dst.shape[0],), dtype=h.dtype), dst, num_segments=n)
        h_N = agg / jnp.maximum(deg, 1.0)[:, None]
        h_total = jnp.concatenate([h, h_N], axis=1)
        return h_total @ W.T + b
    edge_index = jnp.stack([src, dst])
    x = _layernorm(x + _L0_gnn_ref(x, edge_index, L0_gnn_W1, L0_gnn_as1, L0_gnn_ad1, L0_gnn_b1, L0_gnn_W2, L0_gnn_as2, L0_gnn_ad2, L0_gnn_b2, L0_gnn_W3, L0_gnn_as3, L0_gnn_ad3, L0_gnn_b3, L0_gnn_W4, L0_gnn_as4, L0_gnn_ad4, L0_gnn_b4), axis=-1)
    x = _layernorm(x + _L1_gnn_ref(x, edge_index, edge_type_8, L1_gnn_weight, L1_gnn_alpha, L1_gnn_bias, L1_gnn_weight_self_loop, L1_gnn_ln_gamma, L1_gnn_ln_beta), axis=-1)
    x = _layernorm(x + _L2_gnn_ref(x, edge_index, L2_gnn_Wl, L2_gnn_bl, L2_gnn_Wr, L2_gnn_br), axis=-1)
    x = _layernorm(x + _L3_gnn_ref(x, src, dst, L3_gnn_W, L3_gnn_b), axis=-1)
    return x

_drawn_inputs = setup_inputs


def setup_inputs(seed=0):
    import zlib

    import numpy as np

    out = dict(_drawn_inputs(seed))
    spreads = {'L0_gnn_b1': (0.0, 0.286),
     'L0_gnn_b2': (0.0, 0.28),
     'L0_gnn_b3': (0.0, 0.1),
     'L0_gnn_b4': (0.0, 0.1),
     'L1_gnn_bias': (0.0, 0.1),
     'L1_gnn_ln_gamma': (1.0, 0.2),
     'L1_gnn_ln_beta': (0.0, 0.1)}
    factors = {'L0_gnn_W1': 5.194,
     'L0_gnn_as1': 6.323,
     'L0_gnn_ad1': 8.0,
     'L0_gnn_as2': 8.0,
     'L0_gnn_ad2': 8.0,
     'L0_gnn_as3': 8.0,
     'L0_gnn_ad3': 8.0,
     'L0_gnn_as4': 8.0,
     'L0_gnn_ad4': 8.0,
     'L2_gnn_bl': 64.0,
     'L2_gnn_br': 64.0,
     'L3_gnn_b': 6.935}
    for name, (base, spread) in spreads.items():
        noise = np.random.default_rng([zlib.crc32(name.encode()), seed]).standard_normal(out[name].shape)
        drawn = base * np.exp(spread * noise) if base else spread * noise
        out[name] = jnp.asarray(drawn.astype(out[name].dtype))
    for name, factor in factors.items():
        out[name] = (out[name] * factor).astype(out[name].dtype)
    return out
```

```python
import concourse.bass as bass
from concourse import mybir
from contextlib import ExitStack

F32 = mybir.dt.float32
F16 = mybir.dt.float16
I32 = mybir.dt.int32
ALU = mybir.AluOpType
ACT = mybir.ActivationFunctionType
AX = mybir.AxisListType

N = 3125
D = 128
L = 125
G = N // L
E = 50000
P = 128
HEADS, C = 4, 32
REL = 8
BASES = 4
LP = 125
CE = E // LP
B = 8
BODY = 2 * B


def up(n, m):
    return -(-n // m) * m


CIN = up(G + CE, BODY)
ES = E + N
CMID = up(up(ES, P) // P, BODY)
KD = up((ES + G * (P - 1)) // P, BODY)
KS = up((E + G * (P - 1)) // P, BODY)
ROWS, RL = KD // 4, 4 * P

ROUND = 12582912.0
HALF = 0.498
MID = float(N // 2)
SELF = 2000.0
BIG = 1e30
ACC = G * D


class Signal:

    def __init__(self, sem):
        self.sem, self.base = sem, 0

    def at(self, n):
        return self.base + n


class Chain:

    def __init__(self, sem):
        self.sem, self.n = sem, 0

    def __call__(self, eng, ins):
        self.n += 1
        ins.then_inc(self.sem, 1)
        eng.wait_ge(self.sem, self.n)


class Kit:
    pass


def col(ap, n):
    return ap.unsqueeze(2).broadcast_to([ap.shape[0], ap.shape[1], n])


def row(ap, n):
    return ap.unsqueeze(1).broadcast_to([ap.shape[0], n, ap.shape[1]])


def constants(k):
    nc = k.nc
    with nc.Block() as block:
        @block.gpsimd
        def _(pool):
            ch = k.pool_step
            ch(pool, nc.gpsimd.memset(k.ones[:, :], 1.0))
            ch(pool, nc.gpsimd.memset(k.zeros[:, :], 0.0))
            ch(pool, nc.gpsimd.memset(k.ones16[:, :], 1.0))
            ch(pool, nc.gpsimd.iota(k.count[:, :], [[1, 512]], base=0, channel_multiplier=0,
                                    allow_small_or_imprecise_dtypes=True))
            ch(pool, nc.gpsimd.tensor_copy(k.count16[:, :], k.count[:, :]))
            ch(pool, nc.gpsimd.affine_select(out=k.ident[:, :], in_=k.ones[:, 0:P], compare_op=ALU.is_equal,
                                             fill=0.0, base=0, pattern=[[-1, P]], channel_multiplier=1))
            ch(pool, nc.gpsimd.affine_select(out=k.before[:, :], in_=k.ones[:, 0:P], compare_op=ALU.is_gt,
                                             fill=0.0, base=0, pattern=[[1, P]], channel_multiplier=-1))
            ch(pool, nc.gpsimd.tensor_copy(k.before16[:, :], k.before[:, :]))


def split(k, dve, node, group, local, n):
    nc, ch = k.nc, k.dve_step
    ch(dve, nc.vector.tensor_scalar(group, node, 1.0 / L, -0.496, ALU.mult, ALU.add))
    ch(dve, nc.vector.tensor_scalar(group, group, ROUND, -ROUND, ALU.add, ALU.add))
    ch(dve, nc.vector.scalar_tensor_tensor(local, group, -float(L), node, ALU.mult, ALU.add))


def read_edges(k, src, dst, kind):
    nc = k.nc
    with nc.Block() as block:
        @block.sync
        def _(sp):
            sp.dma_start(k.raw[:, 0, :], src.rearrange("(p c) -> p c", p=LP)).then_inc(k.loaded.sem, 16)
            sp.dma_start(k.raw[:, 1, :], dst.rearrange("(p c) -> p c", p=LP)).then_inc(k.loaded.sem, 16)
            sp.dma_start(k.raw[:, 2, :], kind.rearrange("(p c) -> p c", p=LP)).then_inc(k.loaded.sem, 16)

        @block.gpsimd
        def _(pool):
            nc.gpsimd.iota(k.dst[0:LP, 0:G], [[L, G]], base=0, channel_multiplier=1,
                           allow_small_or_imprecise_dtypes=True).then_inc(k.pool_done.sem, 1)

        @block.vector
        def _(dve):
            ch = k.dve_step
            fill = slice(G + CE, CIN)
            real = slice(G, G + CE)
            dve.wait_ge(k.pool_done.sem, k.pool_done.at(1))
            dve.wait_ge(k.loaded.sem, k.loaded.at(48))
            nc.vector.memset(k.dst[0:LP, fill], 0.0)
            nc.vector.tensor_copy(k.dst[0:LP, real], k.raw[:, 1, :])
            nc.vector.tensor_copy(k.src[0:LP, real], k.raw[:, 0, :])
            ch(dve, nc.vector.tensor_copy(k.kind[0:LP, real], k.raw[:, 2, :]))
            split(k, dve, k.dst[0:LP, 0:CIN], k.t0[0:LP, 0:CIN], k.key[0:LP, 0:CIN], CIN)
            ch(dve, nc.vector.memset(k.key[0:LP, fill], -1.0))
            nc.vector.tensor_scalar(k.va[0:LP, 0:CIN], k.dst[0:LP, 0:CIN], MID, None, ALU.subtract)
            nc.vector.tensor_scalar(k.vb[0:LP, real], k.src[0:LP, real], MID, None, ALU.subtract)
            ch(dve, nc.vector.memset(k.vb[0:LP, 0:G], SELF))
            ch(dve, nc.vector.memset(k.va[0:LP, fill], 0.0))
            ch(dve, nc.vector.memset(k.vb[0:LP, fill], 0.0))
    k.loaded.base += 48
    k.pool_done.base += 1


def place(k, parts, cols, digits, padded, chunks=0, group_row=None):
    nc = k.nc
    turns = cols // BODY
    key, tot, base = k.key, k.tot, k.basis

    def one_hots(dve, t, h):
        i = t * BODY + h * B
        return nc.vector.tensor_tensor(k.marks[h][0:parts, :, 0:digits], col(key[0:parts, bass.ds(i, B)], digits),
                                       row(k.count16[0:parts, 0:digits], B), ALU.is_equal)

    with nc.Block() as block:
        @block.vector
        def _(dve):
            dve.sem_inc(k.marks_free.sem, 2)
            with dve.Fori(0, turns) as t:
                for h in range(2):
                    dve.wait_ge(k.marks_free.sem, 2 * t + (k.marks_free.base + h + 1))
                    one_hots(dve, t, h).then_inc(k.marks_ready.sem, 1)

        @block.tensor
        def _(pe):
            pe.sem_inc(k.sums_free.sem, 2)
            with pe.Fori(0, turns) as t:
                for h in range(2):
                    pe.wait_ge(k.sums_free.sem, 2 * t + (k.sums_free.base + h + 1))
                    pe.wait_ge(k.marks_ready.sem, 2 * t + (k.marks_ready.base + h + 1))
                    for b in range(B):
                        last = nc.tensor.matmul(k.ps[0:digits, 512 * h + b:512 * h + b + 1],
                                                k.marks[h][0:parts, b, 0:digits], k.ones16[0:parts, 0:1],
                                                start=True, stop=True)
                    last.then_inc(k.marks_free.sem, 1)

        @block.scalar
        def _(act):
            with act.Fori(0, turns) as t:
                for h in range(2):
                    act.wait_ge(k.marks_free.sem, 2 * t + (k.marks_free.base + h + 3))
                    nc.scalar.copy(tot[0:digits, bass.ds(t * BODY + h * B, B)],
                                   k.ps[0:digits, 512 * h:512 * h + B]).then_inc(k.sums_free.sem, 1)
    k.marks_free.base += 2 + 2 * turns
    k.sums_free.base += 2 + 2 * turns
    k.marks_ready.base += 2 * turns

    with nc.Block() as block:
        @block.vector
        def _(dve):
            ch = k.dve_step
            ch(dve, nc.vector.memset(base[:, 0:cols], 0.0))
            ch(dve, nc.vector.tensor_tensor_scan(k.t0[0:digits, 0:cols], k.ones[0:digits, 0:cols],
                                                 tot[0:digits, 0:cols], 0.0, ALU.mult, ALU.add))
            size = k.small[0:digits, 0:1]
            ch(dve, nc.vector.tensor_copy(size, k.t0[0:digits, cols - 1:cols]))
            if padded:
                ch(dve, nc.vector.tensor_scalar(size, size, 1.0 / P, (P - 1.0) / P - HALF, ALU.mult, ALU.add))
                ch(dve, nc.vector.tensor_scalar(size, size, ROUND, -ROUND, ALU.add, ALU.add))
                ch(dve, nc.vector.tensor_scalar(size, size, float(P), None, ALU.mult))
            dve.sem_inc(k.dve_done.sem, 1)
            dve.wait_ge(k.pe_done.sem, k.pe_done.at(1))
            start = k.small[0:digits, 1:2]
            ch(dve, nc.vector.tensor_copy(start, k.ps[0:digits, 0:1]))
            ch(dve, nc.vector.scalar_tensor_tensor(base[0:digits, 0:cols], k.t0[0:digits, 0:cols], start,
                                                   tot[0:digits, 0:cols], ALU.add, ALU.subtract))
            if padded:
                end = k.small[0:digits, 2:3]
                ch(dve, nc.vector.tensor_tensor(end, start, size, ALU.add))
                ch(dve, nc.vector.tensor_scalar(end, end, 1.0 / P, None, ALU.mult))
                ch(dve, nc.vector.tensor_scalar(k.t0[0:digits, 0:chunks], k.count[0:digits, 0:chunks], end, None,
                                                ALU.is_ge))
                dve.sem_inc(k.dve_done.sem, 1)
                dve.wait_ge(k.pe_done.sem, k.pe_done.at(2))
                ch(dve, nc.vector.tensor_scalar(group_row, k.ps[0:1, 512:512 + chunks], float(G - 1), None,
                                                ALU.min))

        @block.tensor
        def _(pe):
            pe.wait_ge(k.dve_done.sem, k.dve_done.at(1))
            nc.tensor.matmul(k.ps[0:digits, 0:1], k.before[0:digits, 0:digits], k.small[0:digits, 0:1],
                             start=True, stop=True).then_inc(k.pe_done.sem, 1)
            if padded:
                pe.wait_ge(k.dve_done.sem, k.dve_done.at(2))
                nc.tensor.matmul(k.ps[0:1, 512:512 + chunks], k.ones[0:digits, 0:1], k.t0[0:digits, 0:chunks],
                                 start=True, stop=True).then_inc(k.pe_done.sem, 1)
    k.dve_done.base += 2 if padded else 1
    k.pe_done.base += 2 if padded else 1

    def ranks(h, b):
        at = 1024 * h + 512 * (b // 4) + 128 * (b % 4)
        return k.ps[0:parts, at:at + digits]

    with nc.Block() as block:
        @block.vector
        def _(dve):
            dve.sem_inc(k.marks_free.sem, 2)
            with dve.Fori(0, turns) as t:
                for h in range(2):
                    dve.wait_ge(k.marks_free.sem, 2 * t + (k.marks_free.base + h + 1))
                    one_hots(dve, t, h).then_inc(k.marks_ready.sem, 1)
                for h in range(2):
                    dve.wait_ge(k.pe_done.sem, 2 * t + (k.pe_done.base + h + 3))
                    at = k.ps[0:parts, 1024 * h:1024 * (h + 1)].rearrange("p (b d) -> p b d", d=128)
                    nc.vector.tensor_tensor(k.picked[h][0:parts, :, 0:digits], at[:, :, 0:digits],
                                            k.marks[h][0:parts, :, 0:digits], ALU.mult).then_inc(k.dve_done.sem, 1)
                    dve.wait_ge(k.dve_done.sem, 2 * t + (k.dve_done.base + h + 1))
                    nc.vector.tensor_reduce(k.pos[0:parts, bass.ds(t * BODY + h * B, B)],
                                            k.picked[h][0:parts, :, 0:digits], AX.X,
                                            ALU.add).then_inc(k.marks_free.sem, 1)

        @block.scalar
        def _(act):
            with act.Fori(0, turns) as t:
                for h in range(2):
                    act.wait_ge(k.pe_done.sem, 2 * t + (k.pe_done.base + h + 1))
                    nc.scalar.copy(k.begin[h][:, :], base[:, bass.ds(t * BODY + h * B, B)]).then_inc(k.act_done.sem, 1)

        @block.tensor
        def _(pe):
            pe.sem_inc(k.pe_done.sem, 2)
            with pe.Fori(0, turns) as t:
                for h in range(2):
                    pe.wait_ge(k.marks_ready.sem, 2 * t + (k.marks_ready.base + h + 1))
                    pe.wait_ge(k.act_done.sem, 2 * t + (k.act_done.base + h + 1))
                    for b in range(B):
                        nc.tensor.matmul(ranks(h, b), k.before16[0:parts, 0:parts], k.marks[h][0:parts, b, 0:digits],
                                         start=True, stop=False)
                        last = nc.tensor.matmul(ranks(h, b), k.begin[h][:, b:b + 1].broadcast_to([P, parts]),
                                                k.ident[:, 0:digits], start=False, stop=True)
                    last.then_inc(k.pe_done.sem, 1)
    k.marks_free.base += 2 + 2 * turns
    k.marks_ready.base += 2 * turns
    k.act_done.base += 2 * turns
    k.pe_done.base += 2 + 2 * turns
    k.dve_done.base += 2 * turns

    with nc.Block() as block:
        @block.vector
        def _(dve):
            ch = k.dve_step
            pos, chunk, lane = (x[0:parts, 0:cols] for x in (k.pos, k.chunk, k.lane))
            ch(dve, nc.vector.tensor_scalar(chunk, pos, 1.0 / P, -HALF, ALU.mult, ALU.add))
            ch(dve, nc.vector.tensor_scalar(chunk, chunk, ROUND, -ROUND, ALU.add, ALU.add))
            ch(dve, nc.vector.scalar_tensor_tensor(lane, chunk, -float(P), pos, ALU.mult, ALU.add))


def permute(k, parts, cols, chunks, out_a, out_b):
    nc = k.nc
    turns = cols // BODY
    with nc.Block() as block:
        @block.vector
        def _(dve):
            dve.sem_inc(k.marks_free.sem, 2)
            with dve.Fori(0, turns) as t:
                for h in range(2):
                    dve.wait_ge(k.marks_free.sem, 2 * t + (k.marks_free.base + h + 1))
                    for b in range(B):
                        i = t * BODY + (h * B + b)
                        lane, chunk = k.lane[0:parts, bass.ds(i, 1)], k.chunk[0:parts, bass.ds(i, 1)]
                        for n, v in enumerate((k.va, k.vb)):
                            nc.vector.tensor_scalar(k.to_lane[h][0:parts, b, n, :], k.count16[0:parts, 0:P], lane,
                                                    v[0:parts, bass.ds(i, 1)], ALU.is_equal, ALU.mult)
                        last = nc.vector.tensor_scalar(k.to_chunk[h][0:parts, b, 0:chunks],
                                                       k.count16[0:parts, 0:chunks], chunk, None, ALU.is_equal)
                    last.then_inc(k.marks_ready.sem, 1)
            dve.wait_ge(k.marks_free.sem, k.marks_free.at(2 + 2 * turns))
            k.dve_step(dve, nc.vector.tensor_copy(out_a, k.ps[:, 0:chunks]))
            k.dve_step(dve, nc.vector.tensor_copy(out_b, k.ps[:, 512:512 + chunks]))

        @block.tensor
        def _(pe):
            for n in range(2):
                nc.tensor.matmul(k.ps[:, 512 * n:512 * n + chunks], k.zeros[:, 0:P], k.zeros[:, 0:chunks],
                                 start=True, stop=False, skip_group_check=True)
            with pe.Fori(0, turns) as t:
                for h in range(2):
                    pe.wait_ge(k.marks_ready.sem, 2 * t + (k.marks_ready.base + h + 1))
                    for b in range(B):
                        for n in range(2):
                            last = nc.tensor.matmul(k.ps[:, 512 * n:512 * n + chunks], k.to_lane[h][0:parts, b, n, :],
                                                    k.to_chunk[h][0:parts, b, 0:chunks],
                                                    start=False, stop=False, skip_group_check=True)
                    last.then_inc(k.marks_free.sem, 1)
    k.marks_free.base += 2 + 2 * turns
    k.marks_ready.base += 2 * turns


def order_edges(k):
    nc = k.nc
    place(k, LP, CIN, L, False)
    permute(k, LP, CIN, CMID, k.va[:, 0:CMID], k.vb[:, 0:CMID])
    with nc.Block() as block:
        @block.gpsimd
        def _(pool):
            nc.gpsimd.affine_select(out=k.t2[:, 0:CMID], in_=k.ones[:, 0:CMID], compare_op=ALU.is_gt, fill=0.0,
                                    base=ES, pattern=[[-P, CMID]],
                                    channel_multiplier=-1).then_inc(k.pool_done.sem, 1)

        @block.vector
        def _(dve):
            ch = k.dve_step
            m = slice(0, CMID)
            node, valid, group, local, own = k.t0[:, m], k.t2[:, m], k.key[:, m], k.t3[:, m], k.t4[:, m]
            ch(dve, nc.vector.tensor_scalar(node, k.va[:, m], MID, None, ALU.add))
            split(k, dve, node, group, local, CMID)
            dve.wait_ge(k.pool_done.sem, k.pool_done.at(1))
            ch(dve, nc.vector.tensor_scalar(own, k.vb[:, m], SELF, None, ALU.is_equal))
            ch(dve, nc.vector.tensor_tensor(k.t5[:, m], k.va[:, m], k.vb[:, m], ALU.subtract))
            ch(dve, nc.vector.tensor_tensor(k.t5[:, m], k.t5[:, m], own, ALU.mult))
            ch(dve, nc.vector.tensor_tensor(k.vb[:, m], k.vb[:, m], k.t5[:, m], ALU.add))
            ch(dve, nc.vector.scalar_tensor_tensor(k.va[:, m], own, 128.0, local, ALU.mult, ALU.add))
            ch(dve, nc.vector.scalar_tensor_tensor(k.va[:, m], k.va[:, m], 1.0, valid, ALU.add, ALU.mult))
            ch(dve, nc.vector.tensor_tensor(k.vb[:, m], k.vb[:, m], valid, ALU.mult))
            ch(dve, nc.vector.scalar_tensor_tensor(group, group, 1.0, valid, ALU.add, ALU.mult))
            ch(dve, nc.vector.tensor_scalar(group, group, -1.0, None, ALU.add))
    k.pool_done.base += 1
    place(k, P, CMID, G, True, KD, k.tgroup[0:1, :])
    permute(k, P, CMID, KD, k.tself[:, :], k.t0[:, 0:KD])
    with nc.Block() as block:
        @block.vector
        def _(dve):
            ch = k.dve_step
            ch(dve, nc.vector.tensor_scalar(k.town[:, :], k.tself[:, :], 128.0, None, ALU.is_gt))
            ch(dve, nc.vector.scalar_tensor_tensor(k.tloc[:, :], k.town[:, :], -128.0, k.tself[:, :],
                                                   ALU.mult, ALU.add))
            ch(dve, nc.vector.tensor_scalar(k.t0[:, 0:KD], k.t0[:, 0:KD], MID, None, ALU.add))
            ch(dve, nc.vector.tensor_copy(k.tsrc[:, :], k.t0[:, 0:KD]))
            real, out = slice(G, G + CE), slice(0, CE)
            split(k, dve, k.src[0:LP, real], k.key[0:LP, out], k.va[0:LP, out], CE)
            ch(dve, nc.vector.scalar_tensor_tensor(k.va[0:LP, out], k.kind[0:LP, real], 128.0, k.va[0:LP, out],
                                                   ALU.mult, ALU.add))
            ch(dve, nc.vector.tensor_scalar(k.va[0:LP, out], k.va[0:LP, out], 1.0, None, ALU.add))
            ch(dve, nc.vector.tensor_scalar(k.vb[0:LP, out], k.dst[0:LP, real], MID, None, ALU.subtract))
    place(k, LP, CE, G, True, KS, k.sgroup[0:1, :])
    permute(k, LP, CE, KS, k.va[:, 0:KS], k.vb[:, 0:KS])
    with nc.Block() as block:
        @block.vector
        def _(dve):
            ch = k.dve_step
            m = slice(0, KS)
            ch(dve, nc.vector.tensor_scalar(k.t0[:, m], k.va[:, m], 1.0 / 128, -HALF, ALU.mult, ALU.add))
            ch(dve, nc.vector.tensor_scalar(k.t0[:, m], k.t0[:, m], ROUND, -ROUND, ALU.add, ALU.add))
            ch(dve, nc.vector.scalar_tensor_tensor(k.sloc[:, :], k.t0[:, m], -128.0, k.va[:, m], ALU.mult, ALU.add))
            ch(dve, nc.vector.tensor_scalar(k.vb[:, m], k.vb[:, m], MID, None, ALU.add))
            ch(dve, nc.vector.tensor_copy(k.sdst[:, :], k.vb[:, m]))
            ch(dve, nc.vector.scalar_tensor_tensor(k.vb[:, m], k.t0[:, m], float(N), k.vb[:, m], ALU.mult, ALU.add))
            ch(dve, nc.vector.tensor_copy(k.skind[:, :], k.vb[:, m]))



def load_parameters(k, p):
    nc = k.nc
    every = [(k.bias[i], p[f"L0_gnn_b{i + 1}"]) for i in range(4)]
    every += [(k.gamma, p["L1_gnn_ln_gamma"]), (k.beta, p["L1_gnn_ln_beta"]), (k.bias1, p["L1_gnn_bias"]),
              (k.bias2[0], p["L2_gnn_bl"]), (k.bias2[1], p["L2_gnn_br"]), (k.bias3, p["L3_gnn_b"])]
    loads = [(dst[:, :], src.unsqueeze(0).broadcast_to([P, D])) for dst, src in every]
    loads += [(k.w_gat[i][:, 0:D], p[f"L0_gnn_W{i + 1}"]) for i in range(4)]
    for i in range(4):
        for n, name in enumerate(("as", "ad")):
            loads.append((k.a_col[:, 2 * i + n:2 * i + n + 1],
                          p[f"L0_gnn_{name}{i + 1}"].rearrange("h c -> (h c)").unsqueeze(1)))
    loads += [(k.w_base[:, :, :], p["L1_gnn_weight"].rearrange("b i o -> i b o")),
              (k.alpha[:, :], p["L1_gnn_alpha"].rearrange("r b -> (r b)").unsqueeze(0).broadcast_to([P, REL * BASES])),
              (k.w_self[:, :], p["L1_gnn_weight_self_loop"]), (k.w_l[:, :], p["L2_gnn_Wl"]),
              (k.w_r[:, :], p["L2_gnn_Wr"]), (k.w_cat[:, :], p["L3_gnn_W"]),
              (k.x[:, :, :], p["x"].rearrange("(g l) f -> l g f", l=L))]
    with nc.Block() as block:
        @block.sync
        def _(sp):
            for to, what in loads:
                sp.dma_start(to, what).then_inc(k.loaded.sem, 16)
            sp.wait_ge(k.loaded.sem, k.loaded.at(16 * len(loads)))
    k.loaded.base += 16 * len(loads)


def prepare_weights(k):
    nc = k.nc
    with nc.Block() as block:
        @block.gpsimd
        def _(pool):
            ch = k.pool_step
            ch(pool, nc.gpsimd.affine_select(out=k.own[:, :], in_=k.ones[:, 0:HEADS], compare_op=ALU.is_ge, fill=0.0,
                                             base=0, pattern=[[-C, HEADS]], channel_multiplier=1))
            nc.gpsimd.affine_select(out=k.own[:, :], in_=k.own[:, :], compare_op=ALU.is_ge, fill=0.0, base=C - 1,
                                    pattern=[[C, HEADS]], channel_multiplier=-1).then_inc(k.pool_done.sem, 1)

        @block.tensor
        def _(pe):
            for i in range(4):
                nc.tensor.transpose(k.ps[:, 512 * i:512 * i + P], k.w_gat[i][:, 0:D], k.ident[:, :])
            for n in range(2):
                last = nc.tensor.transpose(k.ps[:, 2048 + 512 * n:2048 + 512 * n + P], k.w_cat[:, n * D:(n + 1) * D],
                                           k.ident[:, :])
            last.then_inc(k.pe_done.sem, 1)
            pe.wait_ge(k.dve_done.sem, k.dve_done.at(1))
            for i in range(4):
                last = nc.tensor.matmul(k.ps[:, 512 * i + 256:512 * i + 256 + 2 * HEADS], k.w_t[:, i, :],
                                        k.a_wide[:, i, :, :].rearrange("p n h -> p (n h)"), start=True, stop=True)
            last.then_inc(k.pe_done.sem, 1)

        @block.vector
        def _(dve):
            ch = k.dve_step
            dve.wait_ge(k.pool_done.sem, k.pool_done.at(1))
            for i in range(4):
                for n in range(2):
                    ch(dve, nc.vector.tensor_scalar(k.a_wide[:, i, n, :], k.own[:, :],
                                                    k.a_col[:, 2 * i + n:2 * i + n + 1], None, ALU.mult))
            dve.wait_ge(k.pe_done.sem, k.pe_done.at(1))
            for i in range(4):
                ch(dve, nc.vector.tensor_copy(k.w_t[:, i, :], k.ps[:, 512 * i:512 * i + P]))
            for n in range(2):
                ch(dve, nc.vector.tensor_copy(k.w_cat_t[:, n, :], k.ps[:, 2048 + 512 * n:2048 + 512 * n + P]))
            dve.sem_inc(k.dve_done.sem, 1)
            for r in range(REL):
                w = k.w_rel[:, r * D:(r + 1) * D]
                for b in range(BASES):
                    a = k.alpha[:, r * BASES + b:r * BASES + b + 1]
                    if b == 0:
                        ch(dve, nc.vector.tensor_scalar(w, k.w_base[:, b, :], a, None, ALU.mult))
                    else:
                        ch(dve, nc.vector.scalar_tensor_tensor(w, k.w_base[:, b, :], a, w, ALU.mult, ALU.add))
            dve.wait_ge(k.pe_done.sem, k.pe_done.at(2))
            for i in range(4):
                ch(dve, nc.vector.tensor_copy(k.w_gat[i][:, D:D + 2 * HEADS],
                                              k.ps[:, 512 * i + 256:512 * i + 256 + 2 * HEADS]))
    k.pool_done.base += 1
    k.pe_done.base += 2
    k.dve_done.base += 1


def transposed_lists(k):
    nc = k.nc
    first, last, pen = k.m_first, k.m_last, k.m_pen
    with nc.Block() as block:
        @block.tensor
        def _(pe):
            pe.wait_ge(k.dve_done.sem, k.dve_done.at(1))
            for n, x in enumerate((k.town, k.pen)):
                v = x[:, :].rearrange("p (r j) -> p j r", j=4)
                for j in range(4):
                    at = 512 * n + P * j
                    done = nc.tensor.transpose(k.ps[0:ROWS, at:at + P], v[:, j, :], k.ident[:, :])
            done.then_inc(k.pe_done.sem, 1)
            pe.wait_ge(k.dve_done.sem, k.dve_done.at(2))
            nc.tensor.matmul(k.ps[0:ROWS, 1024:1025], k.shift[0:ROWS, 0:ROWS], first[:, 0:1], start=True,
                             stop=True).then_inc(k.pe_done.sem, 1)
            pe.wait_ge(k.dve_done.sem, k.dve_done.at(3))
            for n in range(2):
                done = nc.tensor.matmul(k.ps[0:HEADS, 1536 + P * n:1536 + P * n + ROWS],
                                        k.small[0:ROWS, n:n + 1].broadcast_to([ROWS, HEADS]),
                                        k.ident[0:ROWS, 0:ROWS], start=True, stop=True)
            done.then_inc(k.pe_done.sem, 1)

        @block.gpsimd
        def _(pool):
            nc.gpsimd.affine_select(out=k.shift[:, :], in_=k.ones[:, 0:P], compare_op=ALU.is_equal, fill=0.0,
                                    base=-1, pattern=[[-1, P]], channel_multiplier=1).then_inc(k.pool_done.sem, 1)

        @block.vector
        def _(dve):
            ch = k.dve_step
            ch(dve, nc.vector.tensor_scalar(k.pen[:, :], k.tloc[:, :], 0.0, -BIG, ALU.is_equal, ALU.mult))
            dve.sem_inc(k.dve_done.sem, 1)
            dve.wait_ge(k.pe_done.sem, k.pe_done.at(1))
            ch(dve, nc.vector.tensor_copy(first[:, :], k.ps[0:ROWS, 0:512]))
            ch(dve, nc.vector.tensor_copy(pen[:, :], k.ps[0:ROWS, 512:1024]))
            dve.wait_ge(k.pool_done.sem, k.pool_done.at(1))
            dve.sem_inc(k.dve_done.sem, 1)
            ch(dve, nc.vector.tensor_copy(last[:, 0:RL - 1], first[:, 1:RL]))
            dve.wait_ge(k.pe_done.sem, k.pe_done.at(2))
            ch(dve, nc.vector.tensor_copy(last[:, RL - 1:RL], k.ps[0:ROWS, 1024:1025]))
            ch(dve, nc.vector.tensor_reduce(k.small[0:ROWS, 0:1], first[:, :], AX.X, ALU.max))
            ch(dve, nc.vector.tensor_reduce(k.small[0:ROWS, 1:2], last[:, :], AX.X, ALU.max))
            dve.sem_inc(k.dve_done.sem, 1)
            ch(dve, nc.vector.tensor_scalar(k.m_reset[:, :], first[:, :], -BIG, None, ALU.mult))
            ch(dve, nc.vector.tensor_scalar(k.m_keep[:, :], first[:, :], -1.0, 1.0, ALU.mult, ALU.add))
            ch(dve, nc.vector.tensor_scalar(k.m_reset_b[:, :], last[:, :], -BIG, None, ALU.mult))
            one = k.ones[0:ROWS, 0:RL]
            ch(dve, nc.vector.tensor_tensor_scan(k.m_seen[:, :], one, first[:, :], 0.0, ALU.mult, ALU.max))
            ch(dve, nc.vector.tensor_tensor_scan(k.m_seen_b[:, ::-1], one, last[:, ::-1], 0.0, ALU.mult, ALU.max))
            ch(dve, nc.vector.tensor_scalar(k.m_open[:, :], k.m_seen[:, :], -1.0, 1.0, ALU.mult, ALU.add))
            ch(dve, nc.vector.tensor_scalar(k.m_seen[:, :], k.m_seen[:, :], -BIG, None, ALU.mult))
            ch(dve, nc.vector.tensor_scalar(k.m_seen_b[:, :], k.m_seen_b[:, :], -BIG, None, ALU.mult))
            dve.wait_ge(k.pe_done.sem, k.pe_done.at(3))
            has = [k.ps[0:HEADS, 1536 + P * n:1536 + P * n + ROWS] for n in range(2)]
            ch(dve, nc.vector.tensor_scalar(k.row_mask[:, 0, :], has[0], -BIG, None, ALU.mult))
            ch(dve, nc.vector.tensor_scalar(k.row_mask[:, 1, :], has[1], -BIG, None, ALU.mult))
            ch(dve, nc.vector.tensor_scalar(k.row_mask[:, 2, :], has[0], -1.0, 1.0, ALU.mult, ALU.add))
    k.dve_done.base += 3
    k.pe_done.base += 3
    k.pool_done.base += 1


TILES = 5


def products(k, x, jobs):
    nc = k.nc
    turns, J = G // TILES, len(jobs)
    stores = sum(TILES for _, out in jobs if out is None)
    items = [(b, j) for b in range(TILES) for j in range(J)]

    def turned(b):
        at = 512 * (b // 4) + P * (b % 4)
        return k.ps[:, at:at + L]

    def result(n, width):
        at = 512 * (2 + n % 5)
        return k.ps[0:L, at:at + width]

    with nc.Block() as block:
        @block.scalar
        def _(act):
            with act.Fori(0, turns) as t:
                for b in range(TILES):
                    act.wait_ge(k.turned.sem, TILES * t + (k.turned.base + b + 1))
                    nc.scalar.copy(k.xs[b][:, :], x[:, bass.ds(t * TILES + b, 1), :].rearrange(
                        "p a f -> p (a f)")).then_inc(k.act_done.sem, 1)
                for b in range(TILES):
                    act.wait_ge(k.turned.sem, TILES * t + (k.turned.base + 2 * TILES))
                    act.wait_ge(k.multiplied.sem, TILES * J * t + (k.multiplied.base + J * b + J))
                    nc.scalar.copy(k.xt[b][:, :], turned(b)).then_inc(k.act_done.sem, 1)

        @block.tensor
        def _(pe):
            pe.sem_inc(k.turned.sem, TILES)
            pe.sem_inc(k.multiplied.sem, TILES * J)
            with pe.Fori(0, turns) as t:
                for b in range(TILES):
                    pe.wait_ge(k.act_done.sem, 2 * TILES * t + (k.act_done.base + b + 1))
                    nc.tensor.transpose(turned(b), k.xs[b][:, :], k.ident[0:L, 0:L]).then_inc(k.turned.sem, 1)
                for n, (b, j) in enumerate(items):
                    if j == 0:
                        pe.wait_ge(k.act_done.sem, 2 * TILES * t + (k.act_done.base + TILES + b + 1))
                    pe.wait_ge(k.taken.sem, TILES * J * t + (k.taken.base + n + 1))
                    nc.tensor.matmul(result(n, jobs[j][0].shape[1]), k.xt[b][:, :], jobs[j][0], start=True,
                                     stop=True).then_inc(k.multiplied.sem, 1)

        @block.vector
        def _(dve):
            dve.sem_inc(k.taken.sem, 5)
            if stores:
                dve.sem_inc(k.tabled.sem, 16 * stores)
            with dve.Fori(0, turns) as t:
                if stores:
                    dve.wait_ge(k.tabled.sem, t * (16 * stores) + (k.tabled.base + 16 * stores))
                for n, (b, j) in enumerate(items):
                    rhs, out = jobs[j]
                    width = rhs.shape[1]
                    to = k.stage[b][j][:, :] if out is None else \
                        out[:, bass.ds(t * TILES + b, 1), 0:width].rearrange("p a f -> p (a f)")
                    dve.wait_ge(k.multiplied.sem, TILES * J * t + (k.multiplied.base + TILES * J + n + 1))
                    nc.vector.tensor_copy(to, result(n, width)).then_inc(k.taken.sem, 1)

        if stores:
            @block.sync
            def _(sp):
                table = k.table_rel.rearrange("(r n) f -> n r f", n=N)
                with sp.Fori(0, turns) as t:
                    for n, (b, j) in enumerate(items):
                        if jobs[j][1] is None:
                            sp.wait_ge(k.taken.sem, TILES * J * t + (k.taken.base + 5 + n + 1))
                            sp.dma_start(table[bass.ds((t * TILES + b) * L, L), 4 * j:4 * j + 4, :],
                                         k.stage[b][j][:, :].rearrange("p (r f) -> p r f", r=4)
                                         ).then_inc(k.tabled.sem, 16)
                sp.wait_ge(k.tabled.sem, k.tabled.at(16 * stores * (turns + 1)))
    k.turned.base += TILES * (turns + 1)
    k.multiplied.base += TILES * J * (turns + 1)
    k.act_done.base += 2 * TILES * turns
    k.taken.base += TILES * J * turns + 5
    if stores:
        k.tabled.base += 16 * stores * (turns + 1)


def store_table(k, pairs):
    nc = k.nc
    with nc.Block() as block:
        @block.sync
        def _(sp):
            for to, what in pairs:
                sp.dma_start(to.rearrange("(g l) f -> l g f", l=L), what).then_inc(k.stored.sem, 16)
            sp.wait_ge(k.stored.sem, k.stored.at(16 * len(pairs)))
    k.stored.base += 16 * len(pairs)


def gather(k, pool, table, width, turns):
    nc = k.nc
    with pool.Fori(0, turns) as t:
        for h in range(2):
            pool.wait_ge(k.index_ready.sem, 2 * t + (k.index_ready.base + h + 1))
            pool.sem_inc(k.pool_turn.sem, 1)
            for b in range(B):
                nc.gpsimd.indirect_dma_start(
                    k.rows[h][:, b, 0:width], None, table,
                    bass.IndirectOffsetOnAxis(ap=k.index[h][:, b:b + 1], axis=0)).then_inc(k.gathered[h].sem, 16)


def node_scores(k):
    nc = k.nc
    turns = KD // BODY
    with nc.Block() as block:
        @block.scalar
        def _(act):
            with act.Fori(0, turns) as t:
                for h in range(2):
                    act.wait_ge(k.rows_free.sem, 2 * t + (k.rows_free.base + h + 1))
                    nc.scalar.copy(k.index[h][:, :], k.tsrc[:, bass.ds(t * BODY + h * B, B)]).then_inc(
                        k.index_ready.sem, 1)

        @block.gpsimd
        def _(pool):
            gather(k, pool, k.table_score, 2 * HEADS, turns)

        @block.vector
        def _(dve):
            dve.sem_inc(k.rows_free.sem, 2)
            with dve.Fori(0, turns) as t:
                for h in range(2):
                    dve.wait_ge(k.gathered[h].sem, t * (16 * B) + (k.gathered[h].base + 16 * B))
                    nc.vector.tensor_copy(k.score[:, bass.ds(t * BODY + h * B, B), :],
                                          k.rows[h][:, :, 0:2 * HEADS]).then_inc(k.rows_free.sem, 1)
    k.rows_free.base += 2 + 2 * turns
    k.index_ready.base += 2 * turns
    for h in range(2):
        k.gathered[h].base += 16 * B * turns


def edge_weights(k):
    nc = k.nc
    src, own, fwd, bwd, tmp, = k.s_src, k.s_own, k.s_fwd, k.s_bwd, k.s_tmp
    with nc.Block() as block:
        @block.tensor
        def _(pe):
            v = k.score[:, :, :].rearrange("p (r j) e -> p e j r", j=4)
            for e in range(2 * HEADS):
                for j in range(4):
                    at = RL * e + P * j
                    last = nc.tensor.transpose(k.ps[0:ROWS, at:at + P], v[:, e, j, :], k.ident[:, :])
            last.then_inc(k.pe_done.sem, 1)
            pe.wait_ge(k.dve_done.sem, k.dve_done.at(1))
            for q in range(3):
                last = nc.tensor.transpose(k.ps[0:HEADS, P * q:P * q + ROWS], k.ends[:, q, :],
                                           k.ident[0:ROWS, 0:ROWS])
            last.then_inc(k.pe_done.sem, 1)
            pe.wait_ge(k.dve_done.sem, k.dve_done.at(2))
            for q in range(3):
                s = 1 if q == 1 else 0
                last = nc.tensor.transpose(k.ps[0:ROWS, 512 + HEADS * q:512 + HEADS * (q + 1)],
                                           k.carry_row[:, q, s:s + ROWS], k.ident[0:HEADS, 0:HEADS])
            last.then_inc(k.pe_done.sem, 1)
            pe.wait_ge(k.act_done.sem, k.act_done.at(1))
            for e in range(HEADS):
                for j in range(4):
                    at = RL * (4 + e) + P * j
                    last = nc.tensor.transpose(k.ps[:, at:at + ROWS], tmp[:, e, P * j:P * (j + 1)],
                                               k.ident[0:ROWS, 0:ROWS])
            last.then_inc(k.pe_done.sem, 1)

        @block.scalar
        def _(act):
            act.wait_ge(k.dve_done.sem, k.dve_done.at(3))
            nc.scalar.activation(tmp, tmp, ACT.Exp).then_inc(k.act_done.sem, 1)

        @block.vector
        def _(dve):
            ch = k.dve_step
            heads = range(HEADS)
            dve.wait_ge(k.pe_done.sem, k.pe_done.at(1))
            got = k.ps[0:ROWS, :].rearrange("p (e j) -> p e j", j=RL)
            ch(dve, nc.vector.tensor_tensor(src, got[:, 0:HEADS, :], row(k.m_pen[:, :], HEADS), ALU.add))
            ch(dve, nc.vector.tensor_tensor(own, got[:, HEADS:, :], row(k.m_first[:, :], HEADS), ALU.mult))
            for h in heads:
                nc.vector.tensor_tensor_scan(fwd[:, h, :], k.m_reset[:, :], src[:, h, :], -BIG, ALU.add, ALU.max)
                nc.vector.tensor_tensor_scan(bwd[:, h, ::-1], k.m_reset_b[:, ::-1], src[:, h, ::-1], -BIG, ALU.add,
                                             ALU.max)
                ch(dve, nc.vector.tensor_tensor_scan(tmp[:, h, :], k.m_keep[:, :], own[:, h, :], 0.0, ALU.mult,
                                                     ALU.add))
            nc.vector.tensor_copy(k.ends[:, 0, :], fwd[:, :, RL - 1])
            nc.vector.tensor_copy(k.ends[:, 1, :], bwd[:, :, 0])
            ch(dve, nc.vector.tensor_copy(k.ends[:, 2, :], tmp[:, :, RL - 1]))
            dve.sem_inc(k.dve_done.sem, 1)
            nc.vector.memset(k.carry_row[:, 0, 0:1], -BIG)
            nc.vector.memset(k.carry_row[:, 1, ROWS:ROWS + 1], -BIG)
            ch(dve, nc.vector.memset(k.carry_row[:, 2, 0:1], 0.0))
            dve.wait_ge(k.pe_done.sem, k.pe_done.at(2))
            end = [k.ps[0:HEADS, P * q:P * q + ROWS] for q in range(3)]
            nc.vector.tensor_tensor_scan(k.carry_row[:, 0, 1:ROWS + 1], k.row_mask[:, 0, :], end[0], -BIG, ALU.add,
                                         ALU.max)
            nc.vector.tensor_tensor_scan(k.carry_row[:, 1, 0:ROWS][:, ::-1], k.row_mask[:, 1, ::-1], end[1][:, ::-1],
                                         -BIG, ALU.add, ALU.max)
            ch(dve, nc.vector.tensor_tensor_scan(k.carry_row[:, 2, 1:ROWS + 1], k.row_mask[:, 2, :], end[2], 0.0,
                                                 ALU.mult, ALU.add))
            dve.sem_inc(k.dve_done.sem, 1)
            dve.wait_ge(k.pe_done.sem, k.pe_done.at(3))
            ch(dve, nc.vector.tensor_copy(k.carry[:, :], k.ps[0:ROWS, 512:512 + 3 * HEADS]))
            for h in heads:
                c = [k.carry[:, HEADS * q + h:HEADS * q + h + 1] for q in range(3)]
                nc.vector.scalar_tensor_tensor(fwd[:, h, :], k.m_seen[:, :], c[0], fwd[:, h, :], ALU.add, ALU.max)
                nc.vector.scalar_tensor_tensor(bwd[:, h, :], k.m_seen_b[:, :], c[1], bwd[:, h, :], ALU.add, ALU.max)
                ch(dve, nc.vector.scalar_tensor_tensor(own[:, h, :], k.m_open[:, :], c[2], tmp[:, h, :], ALU.mult,
                                                       ALU.add))
            ch(dve, nc.vector.tensor_tensor(fwd, fwd, bwd, ALU.max))
            ch(dve, nc.vector.tensor_tensor(fwd, fwd, own, ALU.add))
            ch(dve, nc.vector.scalar_tensor_tensor(fwd, fwd, 0.2, fwd, ALU.mult, ALU.max))
            ch(dve, nc.vector.tensor_tensor(tmp, src, own, ALU.add))
            ch(dve, nc.vector.scalar_tensor_tensor(tmp, tmp, 0.2, tmp, ALU.mult, ALU.max))
            ch(dve, nc.vector.tensor_tensor(tmp, tmp, fwd, ALU.subtract))
            dve.sem_inc(k.dve_done.sem, 1)
            dve.wait_ge(k.pe_done.sem, k.pe_done.at(4))
            back = k.ps[:, RL * 4:].rearrange("p (e j r) -> p e j r", e=HEADS, j=4)
            ch(dve, nc.vector.tensor_copy(k.expo[:, :, :].rearrange("p (r j) e -> p e j r", j=4),
                                          back[:, :, :, 0:ROWS]))
    k.pe_done.base += 4
    k.dve_done.base += 3
    k.act_done.base += 1


def aggregate(k, table, index, label, group, chunks, weigh, count):
    nc = k.nc
    turns = chunks // BODY
    with nc.Block() as block:
        @block.scalar
        def _(act):
            with act.Fori(0, turns) as t:
                for h in range(2):
                    act.wait_ge(k.rows_free.sem, 2 * t + (k.rows_free.base + h + 1))
                    nc.scalar.copy(k.index[h][:, :], index[:, bass.ds(t * BODY + h * B, B)]).then_inc(
                        k.index_ready.sem, 1)

        @block.gpsimd
        def _(pool):
            gather(k, pool, table, D, turns)

        @block.vector
        def _(dve):
            with dve.Fori(0, turns) as t:
                for h in range(2):
                    i = t * BODY + h * B
                    dve.wait_ge(k.rows_free.sem, 2 * t + (k.rows_free.base + h + 1))
                    last = nc.vector.tensor_tensor(k.member[h][:, :, :], col(label[:, bass.ds(i, B)], L),
                                                   row(k.count[:, 1:L + 1], B), ALU.is_equal)
                    if weigh:
                        nc.vector.tensor_copy(k.share[h][:, :], k.expo[:, bass.ds(i, B), :].rearrange(
                            "p b e -> p (b e)")).then_inc(k.dve_done.sem, 1)
                    dve.wait_ge(k.gathered[h].sem, t * (16 * B) + (k.gathered[h].base + 16 * B))
                    if weigh:
                        dve.wait_ge(k.dve_done.sem, 2 * t + (k.dve_done.base + h + 1))
                        last = nc.vector.tensor_tensor(
                            k.message[h][:, :].rearrange("p (b c) -> p b c", c=C),
                            k.rows[h][:, :, :].rearrange("p b (e c) -> p (b e) c", c=C),
                            col(k.share[h][:, :], C), ALU.mult)
                        last.then_inc(k.marks_ready.sem, 1)
                    else:
                        last.then_inc(k.marks_ready.sem, 1)

        @block.tensor
        def _(pe):
            for n in range(7):
                last = nc.tensor.matmul(k.ps[:, 512 * n:512 * (n + 1)], k.zeros[:, 0:P], k.zeros[:, :], start=True,
                                        stop=False, skip_group_check=True)
            last.then_inc(k.rows_free.sem, 2)
            with pe.Fori(0, turns) as t:
                for h in range(2):
                    i = t * BODY + h * B
                    pe.wait_ge(k.marks_ready.sem, 2 * t + (k.marks_ready.base + h + 1))
                    pe.wait_ge(k.gathered[h].sem, t * (16 * B) + (k.gathered[h].base + 16 * B))
                    for b in range(B):
                        g = pe.value_load(group[0:1, bass.ds(i + b, 1)], min_val=0, max_val=G - 1)
                        one = k.member[h][:, b, :]
                        what = k.message[h][:, b * D:(b + 1) * D] if weigh else k.rows[h][:, b, :]
                        last = nc.tensor.matmul(k.ps[0:L, bass.ds(g * D, D)], one, what, start=False, stop=False,
                                                skip_group_check=True)
                        if weigh:
                            last = nc.tensor.matmul(k.ps[0:L, bass.ds(g * HEADS + ACC, HEADS)], one,
                                                    k.share[h][:, b * HEADS:(b + 1) * HEADS], start=False,
                                                    stop=False, skip_group_check=True)
                        if count:
                            last = nc.tensor.matmul(k.ps[0:L, bass.ds(g + ACC, 1)], one, k.ones[:, 0:1], start=False,
                                                    stop=False, skip_group_check=True)
                    last.then_inc(k.rows_free.sem, 1)
    k.rows_free.base += 2 + 2 * turns
    k.index_ready.base += 2 * turns
    k.marks_ready.base += 2 * turns
    if weigh:
        k.dve_done.base += 2 * turns
    for h in range(2):
        k.gathered[h].base += 16 * B * turns


def sums(k):
    return k.ps[0:L, 0:ACC].rearrange("p (g f) -> p g f", f=D)


def on_vector(k, steps):
    nc = k.nc
    with nc.Block() as block:
        @block.vector
        def _(dve):
            steps(lambda ins: k.dve_step(dve, ins))


def attention_result(k, i, relu):
    nc = k.nc

    def steps(do):
        do(nc.vector.reciprocal(k.r100[:, :], k.ps[0:L, ACC:ACC + G * HEADS]))
        do(nc.vector.tensor_tensor(k.y[:, :, :].rearrange("p g (e c) -> p (g e) c", c=C),
                                   k.ps[0:L, 0:ACC].rearrange("p (a c) -> p a c", c=C), col(k.r100[:, :], C),
                                   ALU.mult))
        do(nc.vector.tensor_tensor(k.y[:, :, :], k.y[:, :, :], row(k.bias[i][0:L, :], G), ALU.add))
        if relu:
            do(nc.vector.tensor_scalar(k.y[:, :, :], k.y[:, :, :], 0.0, None, ALU.max))
    on_vector(k, steps)


def root(k, power, add_in, add_out):
    nc = k.nc
    with nc.Block() as block:
        @block.vector
        def _(dve):
            ch = k.dve_step
            ch(dve, nc.vector.tensor_scalar(k.r25[:, :], k.r25[:, :], power, add_in, ALU.mult, ALU.add))
            dve.sem_inc(k.dve_done.sem, 1)
            dve.wait_ge(k.act_done.sem, k.act_done.at(1))
            if add_out:
                ch(dve, nc.vector.tensor_scalar(k.r25[:, :], k.r25[:, :], add_out, None, ALU.add))
            ch(dve, nc.vector.reciprocal(k.r25[:, :], k.r25[:, :]))

        @block.scalar
        def _(act):
            act.wait_ge(k.dve_done.sem, k.dve_done.at(1))
            nc.scalar.activation(k.r25[:, :], k.r25[:, :], ACT.Sqrt).then_inc(k.act_done.sem, 1)
    k.dve_done.base += 1
    k.act_done.base += 1


def layer_norm(k, x, tmp, out):
    nc = k.nc

    def before(do):
        do(nc.vector.tensor_reduce(k.r25[:, :], x, AX.X, ALU.add))
        do(nc.vector.tensor_scalar(k.r25[:, :], k.r25[:, :], 1.0 / D, None, ALU.mult))
        do(nc.vector.tensor_tensor(x, x, col(k.r25[:, :], D), ALU.subtract))
        do(nc.vector.tensor_tensor(tmp, x, x, ALU.mult))
        do(nc.vector.tensor_reduce(k.r25[:, :], tmp, AX.X, ALU.add))
    on_vector(k, before)
    root(k, 1.0 / D, 1e-5, 0.0)
    on_vector(k, lambda do: do(nc.vector.tensor_tensor(out, x, col(k.r25[:, :], D), ALU.mult)))


def add_and_norm(k, what):
    nc = k.nc
    on_vector(k, lambda do: do(nc.vector.tensor_tensor(k.x[:, :, :], k.x[:, :, :], what, ALU.add)))
    layer_norm(k, k.x[:, :, :], k.z[:, :, :], k.x[:, :, :])


def mean_of_neighbours(k, out):
    nc = k.nc
    on_vector(k, lambda do: do(nc.vector.tensor_tensor(out, sums(k), col(k.degree[:, :], D), ALU.mult)))


def take_degree(k):
    nc = k.nc

    def steps(do):
        do(nc.vector.tensor_scalar(k.degree[:, :], k.ps[0:L, ACC:ACC + G], 1.0, None, ALU.max))
        do(nc.vector.reciprocal(k.degree[:, :], k.degree[:, :]))
    on_vector(k, steps)


def layers(k, out):
    nc = k.nc
    x, y, z, w = (t[:, :, :] for t in (k.x, k.y, k.z, k.w))

    for i in range(4):
        products(k, k.x if i == 0 else k.y, [(k.w_gat[i][:, :], k.h)])
        store_table(k, [(k.table, k.h[:, :, 0:D]), (k.table_score, k.h[:, :, D:])])
        node_scores(k)
        edge_weights(k)
        aggregate(k, k.table, k.tsrc, k.tloc, k.tgroup, KD, True, False)
        attention_result(k, i, i < 3)
    add_and_norm(k, y)

    products(k, k.x, [(k.w_rel[:, 0:512], None), (k.w_rel[:, 512:1024], None), (k.w_self[:, :], k.w)])
    aggregate(k, k.table_rel, k.skind, k.sloc, k.sgroup, KS, False, True)
    take_degree(k)
    mean_of_neighbours(k, y)
    layer_norm(k, y, z, y)

    def relations(do):
        do(nc.vector.tensor_tensor(y, y, row(k.gamma[0:L, :], G), ALU.mult))
        do(nc.vector.tensor_tensor(y, y, row(k.beta[0:L, :], G), ALU.add))
        do(nc.vector.tensor_tensor(y, y, row(k.bias1[0:L, :], G), ALU.add))
        do(nc.vector.tensor_tensor(y, y, w, ALU.add))
    on_vector(k, relations)
    add_and_norm(k, y)

    store_table(k, [(k.table, x)])
    aggregate(k, k.table, k.sdst, k.sloc, k.sgroup, KS, False, False)
    mean_of_neighbours(k, y)
    products(k, k.x, [(k.w_l[:, :], k.w)])
    products(k, k.y, [(k.w_r[:, :], k.z)])

    def joined(do):
        do(nc.vector.tensor_tensor(w, w, row(k.bias2[0][0:L, :], G), ALU.add))
        do(nc.vector.tensor_tensor(w, w, z, ALU.add))
        do(nc.vector.tensor_tensor(w, w, row(k.bias2[1][0:L, :], G), ALU.add))
        do(nc.vector.tensor_scalar(w, w, 0.0, None, ALU.max))
        do(nc.vector.tensor_tensor(z, w, w, ALU.mult))
        do(nc.vector.tensor_reduce(k.r25[:, :], z, AX.X, ALU.add))
    on_vector(k, joined)
    root(k, 1.0, 0.0, 1e-6)
    on_vector(k, lambda do: do(nc.vector.tensor_tensor(w, w, col(k.r25[:, :], D), ALU.mult)))
    add_and_norm(k, w)

    store_table(k, [(k.table, x)])
    aggregate(k, k.table, k.tsrc, k.tself, k.tgroup, KD, False, True)
    take_degree(k)
    mean_of_neighbours(k, y)
    products(k, k.x, [(k.w_cat_t[:, 0, :], k.w)])
    products(k, k.y, [(k.w_cat_t[:, 1, :], k.z)])

    def ended(do):
        do(nc.vector.tensor_tensor(w, w, z, ALU.add))
        do(nc.vector.tensor_tensor(w, w, row(k.bias3[0:L, :], G), ALU.add))
    on_vector(k, ended)
    add_and_norm(k, w)
    store_table(k, [(out, x)])


def gnn_kernel(nc, p, out):
    k = Kit()
    k.nc = nc
    with ExitStack() as ctx:
        def sb(name, shape, dt=F32, c=ctx):
            return c.enter_context(nc.sbuf_tensor(name, shape, dt))

        def signal(name):
            return Signal(ctx.enter_context(nc.semaphore(name)))

        k.loaded, k.stored, k.tabled = signal("loaded"), signal("stored"), signal("tabled")
        k.dve_done, k.pe_done, k.act_done = signal("dve_done"), signal("pe_done"), signal("act_done")
        k.pool_done, k.pool_turn = signal("pool_done"), signal("pool_turn")
        k.marks_free, k.marks_ready, k.sums_free = signal("marks_free"), signal("marks_ready"), signal("sums_free")
        k.turned, k.multiplied, k.taken = signal("turned"), signal("multiplied"), signal("taken")
        k.index_ready, k.rows_free = signal("index_ready"), signal("rows_free")
        k.gathered = [signal("gathered0"), signal("gathered1")]
        k.pool_step = Chain(ctx.enter_context(nc.semaphore("pool_step")))
        k.dve_step = Chain(ctx.enter_context(nc.semaphore("dve_step")))
        k.ps = ctx.enter_context(nc.psum_tensor("ps", [P, 4096], F32))

        k.ones, k.zeros, k.count = sb("ones", [P, 512]), sb("zeros", [P, 512]), sb("count", [P, 512])
        k.ones16, k.count16 = sb("ones16", [P, 1], F16), sb("count16", [P, 512], F16)
        k.ident, k.before, k.before16 = sb("ident", [P, P]), sb("before", [P, P]), sb("before16", [P, P], F16)
        k.small = sb("small", [P, 16])
        k.tself, k.tloc, k.town = (sb(name, [P, KD]) for name in ("tself", "tloc", "town"))
        k.tsrc, k.tgroup = sb("tsrc", [P, KD], I32), sb("tgroup", [1, KD], I32)
        k.sloc, k.sdst, k.skind = sb("sloc", [P, KS]), sb("sdst", [P, KS], I32), sb("skind", [P, KS], I32)
        k.sgroup = sb("sgroup", [1, KS], I32)

        constants(k)
        with ExitStack() as sorting:
            k.raw = sb("raw", [LP, 3, CE], I32, sorting)
            k.src, k.dst, k.kind, k.key, k.va, k.vb, k.pos, k.chunk, k.lane, k.tot, k.basis = (
                sb(name, [P, KD], F32, sorting) for name in ("src", "dst", "kind", "key", "va", "vb", "pos", "chunk",
                                                             "lane", "tot", "basis"))
            k.t0, k.t2, k.t3, k.t4, k.t5 = (sb(f"t{i}", [P, KD], F32, sorting) for i in (0, 2, 3, 4, 5))
            k.begin = [sb(f"begin{h}", [P, B], F32, sorting) for h in range(2)]
            k.marks = [sb(f"marks{h}", [P, B, L], F16, sorting) for h in range(2)]
            k.picked = [sb(f"picked{h}", [P, B, L], F32, sorting) for h in range(2)]
            k.to_lane = [sb(f"to_lane{h}", [P, B, 2, P], F16, sorting) for h in range(2)]
            k.to_chunk = [sb(f"to_chunk{h}", [P, B, KD], F16, sorting) for h in range(2)]
            read_edges(k, p["src"], p["dst"], p["edge_type_8"])
            order_edges(k)

        k.bias = [sb(f"bias_gat{i}", [P, D]) for i in range(4)]
        k.gamma, k.beta, k.bias1 = sb("gamma", [P, D]), sb("beta", [P, D]), sb("bias_rel", [P, D])
        k.bias2, k.bias3 = [sb("bias_l", [P, D]), sb("bias_r", [P, D])], sb("bias_cat", [P, D])
        k.w_gat = [sb(f"w_gat{i}", [P, D + 2 * HEADS]) for i in range(4)]
        k.w_t, k.a_col, k.a_wide = sb("w_t", [P, 4, D]), sb("a_col", [P, 8]), sb("a_wide", [P, 4, 2, HEADS])
        k.own = sb("own", [P, HEADS])
        k.w_base, k.alpha, k.w_rel = sb("w_base", [P, BASES, D]), sb("alpha", [P, REL * BASES]), sb("w_rel", [P, REL * D])
        k.w_self, k.w_l, k.w_r = sb("w_self", [P, D]), sb("w_l", [P, D]), sb("w_r", [P, D])
        k.w_cat, k.w_cat_t = sb("w_cat", [P, 2 * D]), sb("w_cat_t", [P, 2, D])
        k.x, k.y, k.z, k.w = (sb(n, [L, G, D]) for n in ("x", "y", "z", "w"))
        k.h = sb("h", [L, G, D + 2 * HEADS])
        k.r25, k.r100, k.degree = sb("r25", [L, G]), sb("r100", [L, G * HEADS]), sb("degree", [L, G])
        k.score, k.expo = sb("score", [P, KD, 2 * HEADS]), sb("expo", [P, KD, HEADS])
        k.s_src, k.s_own, k.s_fwd = (t[0:ROWS, :, :].rearrange("p g f -> p (g f)")[:, 0:HEADS * RL].rearrange(
            "p (e j) -> p e j", e=HEADS) for t in (k.y, k.z, k.w))
        k.s_bwd = k.h[0:ROWS, :, :].rearrange("p g f -> p (g f)")[:, 0:HEADS * RL].rearrange(
            "p (e j) -> p e j", e=HEADS)
        k.s_tmp = sb("s_tmp", [ROWS, HEADS, RL])[:, :, :]
        k.m_first, k.m_last, k.m_pen, k.m_reset, k.m_keep, k.m_reset_b, k.m_seen, k.m_seen_b, k.m_open = (
            sb(f"m_{name}", [ROWS, RL]) for name in ("first", "last", "pen", "reset", "keep", "reset_b", "seen",
                                                     "seen_b", "open"))
        k.pen, k.shift = sb("pen", [P, KD]), sb("shift", [P, P])
        k.ends, k.carry = sb("ends", [ROWS, 3, HEADS]), sb("carry", [ROWS, 3 * HEADS])
        k.row_mask, k.carry_row = sb("row_mask", [HEADS, 3, ROWS]), sb("carry_row", [HEADS, 3, ROWS + 2])
        k.index = [sb(f"index{h}", [P, B], I32) for h in range(2)]
        k.rows = [sb(f"rows{h}", [P, B, D]) for h in range(2)]
        k.share = [sb(f"share{h}", [P, B * HEADS]) for h in range(2)]
        k.message = [sb(f"message{h}", [P, B * D]) for h in range(2)]
        k.member = [sb(f"member{h}", [P, B, L]) for h in range(2)]
        k.xs = [sb(f"xs{b}", [L, D]) for b in range(TILES)]
        k.xt = [sb(f"xt{b}", [D, L]) for b in range(TILES)]
        k.stage = [[k.score[0:L, :, :].rearrange("p c e -> p (c e)")[:, 512 * b:512 * (b + 1)],
                    (k.expo[0:L, :, :].rearrange("p c e -> p (c e)")[:, 512 * b:512 * (b + 1)] if b < 3 else
                     k.message[b - 3][0:L, 0:512])] for b in range(TILES)]
        k.table = nc.dram_tensor("table", [N, D], F32, kind="Internal").ap()
        k.table_score = nc.dram_tensor("table_score", [N, 2 * HEADS], F32, kind="Internal").ap()
        k.table_rel = nc.dram_tensor("table_rel", [REL * N, D], F32, kind="Internal").ap()

        load_parameters(k, p)
        prepare_weights(k)
        transposed_lists(k)
        layers(k, out)


_INS = ["x", "src", "dst", "edge_type_8"] + [f"L0_gnn_{n}{i}" for i in range(1, 5) for n in ("W", "as", "ad", "b")] + [
    "L1_gnn_weight", "L1_gnn_alpha", "L1_gnn_bias", "L1_gnn_weight_self_loop", "L1_gnn_ln_gamma", "L1_gnn_ln_beta",
    "L2_gnn_Wl", "L2_gnn_bl", "L2_gnn_Wr", "L2_gnn_br", "L3_gnn_W", "L3_gnn_b"]


def kernel(**inputs):
    import numpy as _np
    import concourse.bacc as _bacc
    from concourse import mybir as _mybir
    from concourse.bass_utils import run_bass_kernel_spmd as _run

    nc = _bacc.Bacc("TRN2", target_bir_lowering=False, num_devices=1)
    arrays, p = {}, {}
    for name in _INS:
        a = _np.ascontiguousarray(inputs[name])
        arrays[f"in_{name}_dram"] = a
        p[name] = nc.dram_tensor(f"in_{name}_dram", a.shape, _mybir.dt.from_np(a.dtype), kind="ExternalInput").ap()
    out = nc.dram_tensor("out_0_dram", (N, D), _mybir.dt.float32, kind="ExternalOutput").ap()
    gnn_kernel(nc, p, out)
    r = _run(nc, [arrays], core_ids=[0])
    return r.results[0]["out_0_dram"]
```

```python
import concourse.bass as bass
from concourse import mybir
from contextlib import ExitStack

F32 = mybir.dt.float32
F16 = mybir.dt.float16
BF16 = mybir.dt.bfloat16
I32 = mybir.dt.int32
ALU = mybir.AluOpType
ACT = mybir.ActivationFunctionType
AX = mybir.AxisListType

N = 3125
D = 128
L = 125
G = N // L
E = 50000
P = 128
HEADS, C = 4, 32
REL = 8
BASES = 4
LP = 125
CE = E // LP
B = 8
BODY = 2 * B
RING = 4


def up(n, m):
    return -(-n // m) * m


CIN = up(G + CE, BODY)
ES = E + N
CMID = up(up(ES, P) // P, BODY)
KD = up((ES + G * (P - 1)) // P, RING * B)
KS = up((E + G * (P - 1)) // P, RING * B)
ROWS, RL = KD // 4, 4 * P

ROUND = 12582912.0
HALF = 0.498
MID = float(N // 2)
SELF = 2000.0
BIG = 1e30
ACC = G * D
COLUMNS = ((D, 0), (3 * HEADS, ACC), (1, ACC), (3 * HEADS, 0))
TO_ACC, TO_WEIGHTS, TO_COUNT, TO_SCORES = range(4)
BESIDE = 26
KEPT = 20


class Signal:

    def __init__(self, sem):
        self.sem, self.base = sem, 0

    def at(self, n):
        return self.base + n


class Chain:

    def __init__(self, sem):
        self.sem, self.n = sem, 0

    def __call__(self, eng, ins):
        self.n += 1
        ins.then_inc(self.sem, 1)
        eng.wait_ge(self.sem, self.n)


class Kit:
    pass


def col(ap, n):
    return ap.unsqueeze(2).broadcast_to([ap.shape[0], ap.shape[1], n])


def row(ap, n):
    return ap.unsqueeze(1).broadcast_to([ap.shape[0], n, ap.shape[1]])


def constants(k):
    nc = k.nc
    with nc.Block() as block:
        @block.gpsimd
        def _(pool):
            ch = k.pool_step
            ch(pool, nc.gpsimd.memset(k.ones[:, :], 1.0))
            ch(pool, nc.gpsimd.memset(k.zeros[:, :], 0.0))
            ch(pool, nc.gpsimd.memset(k.ones16[:, :], 1.0))
            ch(pool, nc.gpsimd.iota(k.count[:, :], [[1, 512]], base=0, channel_multiplier=0,
                                    allow_small_or_imprecise_dtypes=True))
            ch(pool, nc.gpsimd.tensor_copy(k.count16[:, :], k.count[:, :]))
            ch(pool, nc.gpsimd.affine_select(out=k.ident[:, :], in_=k.ones[:, 0:P], compare_op=ALU.is_equal,
                                             fill=0.0, base=0, pattern=[[-1, P]], channel_multiplier=1))
            ch(pool, nc.gpsimd.affine_select(out=k.before[:, :], in_=k.ones[:, 0:P], compare_op=ALU.is_gt,
                                             fill=0.0, base=0, pattern=[[1, P]], channel_multiplier=-1))
            ch(pool, nc.gpsimd.tensor_copy(k.before16[:, :], k.before[:, :]))


def split(k, dve, node, group, local, n):
    nc, ch = k.nc, k.dve_step
    ch(dve, nc.vector.tensor_scalar(group, node, 1.0 / L, -0.496, ALU.mult, ALU.add))
    ch(dve, nc.vector.tensor_scalar(group, group, ROUND, -ROUND, ALU.add, ALU.add))
    ch(dve, nc.vector.scalar_tensor_tensor(local, group, -float(L), node, ALU.mult, ALU.add))


def read_edges(k, src, dst, kind):
    nc = k.nc
    with nc.Block() as block:
        @block.sync
        def _(sp):
            sp.dma_start(k.raw[:, 0, :], src.rearrange("(p c) -> p c", p=LP)).then_inc(k.loaded.sem, 16)
            sp.dma_start(k.raw[:, 1, :], dst.rearrange("(p c) -> p c", p=LP)).then_inc(k.loaded.sem, 16)
            sp.dma_start(k.raw[:, 2, :], kind.rearrange("(p c) -> p c", p=LP)).then_inc(k.loaded.sem, 16)
            for n in range(2):
                sp.dma_start(k.by_source.rearrange("(p c) v -> p (c v)", p=P)[:, n * KS:(n + 1) * KS],
                             k.zeros[:, 0:KS]).then_inc(k.stored.sem, 16)
            sp.wait_ge(k.stored.sem, k.stored.at(32))

        @block.gpsimd
        def _(pool):
            nc.gpsimd.iota(k.dst[0:LP, 0:G], [[L, G]], base=0, channel_multiplier=1,
                           allow_small_or_imprecise_dtypes=True).then_inc(k.pool_done.sem, 1)

        @block.vector
        def _(dve):
            ch = k.dve_step
            fill = slice(G + CE, CIN)
            real = slice(G, G + CE)
            dve.wait_ge(k.pool_done.sem, k.pool_done.at(1))
            dve.wait_ge(k.loaded.sem, k.loaded.at(48))
            nc.vector.memset(k.dst[0:LP, fill], 0.0)
            nc.vector.tensor_copy(k.dst[0:LP, real], k.raw[:, 1, :])
            nc.vector.tensor_copy(k.src[0:LP, real], k.raw[:, 0, :])
            ch(dve, nc.vector.tensor_copy(k.kind[0:LP, real], k.raw[:, 2, :]))
            out = slice(0, CE)
            split(k, dve, k.src[0:LP, real], k.key[0:LP, out], k.t0[0:LP, out], CE)
            ch(dve, nc.vector.scalar_tensor_tensor(k.t0[0:LP, out], k.kind[0:LP, real], 128.0, k.t0[0:LP, out],
                                                   ALU.mult, ALU.add))
            ch(dve, nc.vector.tensor_scalar(k.pair[:, :, 0], k.t0[0:LP, out], 1.0, None, ALU.add))
            ch(dve, nc.vector.tensor_copy(k.pair[:, :, 1], k.dst[0:LP, real]))
    k.loaded.base += 48
    k.stored.base += 32
    k.pool_done.base += 1


def target_keys(k):
    nc = k.nc
    fill = slice(G + CE, CIN)
    real = slice(G, G + CE)
    with nc.Block() as block:
        @block.vector
        def _(dve):
            ch = k.dve_step
            ch(dve, nc.vector.scalar_tensor_tensor(k.t0[0:LP, 0:CE], k.lane[0:LP, 0:CE], float(KS),
                                                   k.chunk[0:LP, 0:CE], ALU.mult, ALU.add))
            ch(dve, nc.vector.tensor_copy(k.row_of[:, :], k.t0[0:LP, 0:CE]))
            split(k, dve, k.dst[0:LP, 0:CIN], k.t0[0:LP, 0:CIN], k.key[0:LP, 0:CIN], CIN)
            ch(dve, nc.vector.memset(k.key[0:LP, fill], -1.0))
            nc.vector.tensor_scalar(k.va[0:LP, 0:CIN], k.dst[0:LP, 0:CIN], MID, None, ALU.subtract)
            nc.vector.tensor_scalar(k.vb[0:LP, real], k.src[0:LP, real], MID, None, ALU.subtract)
            ch(dve, nc.vector.memset(k.vb[0:LP, 0:G], SELF))
            ch(dve, nc.vector.memset(k.va[0:LP, fill], 0.0))
            ch(dve, nc.vector.memset(k.vb[0:LP, fill], 0.0))


def place(k, parts, cols, digits, padded, chunks=0, group_row=None):
    nc = k.nc
    turns = cols // BODY
    key, tot, base = k.key, k.tot, k.basis

    def one_hots(dve, t, h):
        i = t * BODY + h * B
        return nc.vector.tensor_tensor(k.marks[h][0:parts, :, 0:digits], col(key[0:parts, bass.ds(i, B)], digits),
                                       row(k.count16[0:parts, 0:digits], B), ALU.is_equal)

    with nc.Block() as block:
        @block.vector
        def _(dve):
            dve.sem_inc(k.marks_free.sem, 2)
            with dve.Fori(0, turns) as t:
                for h in range(2):
                    dve.wait_ge(k.marks_free.sem, 2 * t + (k.marks_free.base + h + 1))
                    one_hots(dve, t, h).then_inc(k.marks_ready.sem, 1)

        @block.tensor
        def _(pe):
            pe.sem_inc(k.sums_free.sem, 2)
            with pe.Fori(0, turns) as t:
                for h in range(2):
                    pe.wait_ge(k.sums_free.sem, 2 * t + (k.sums_free.base + h + 1))
                    pe.wait_ge(k.marks_ready.sem, 2 * t + (k.marks_ready.base + h + 1))
                    for b in range(B):
                        last = nc.tensor.matmul(k.ps[0:digits, 512 * h + b:512 * h + b + 1],
                                                k.marks[h][0:parts, b, 0:digits], k.ones16[0:parts, 0:1],
                                                start=True, stop=True)
                    last.then_inc(k.marks_free.sem, 1)

        @block.scalar
        def _(act):
            with act.Fori(0, turns) as t:
                for h in range(2):
                    act.wait_ge(k.marks_free.sem, 2 * t + (k.marks_free.base + h + 3))
                    nc.scalar.copy(tot[0:digits, bass.ds(t * BODY + h * B, B)],
                                   k.ps[0:digits, 512 * h:512 * h + B]).then_inc(k.sums_free.sem, 1)
    k.marks_free.base += 2 + 2 * turns
    k.sums_free.base += 2 + 2 * turns
    k.marks_ready.base += 2 * turns

    with nc.Block() as block:
        @block.vector
        def _(dve):
            ch = k.dve_step
            ch(dve, nc.vector.memset(base[:, 0:cols], 0.0))
            ch(dve, nc.vector.tensor_tensor_scan(k.t0[0:digits, 0:cols], k.ones[0:digits, 0:cols],
                                                 tot[0:digits, 0:cols], 0.0, ALU.mult, ALU.add))
            size = k.small[0:digits, 0:1]
            ch(dve, nc.vector.tensor_copy(size, k.t0[0:digits, cols - 1:cols]))
            if padded:
                ch(dve, nc.vector.tensor_scalar(size, size, 1.0 / P, (P - 1.0) / P - HALF, ALU.mult, ALU.add))
                ch(dve, nc.vector.tensor_scalar(size, size, ROUND, -ROUND, ALU.add, ALU.add))
                ch(dve, nc.vector.tensor_scalar(size, size, float(P), None, ALU.mult))
            dve.sem_inc(k.dve_done.sem, 1)
            dve.wait_ge(k.pe_done.sem, k.pe_done.at(1))
            start = k.small[0:digits, 1:2]
            ch(dve, nc.vector.tensor_copy(start, k.ps[0:digits, 0:1]))
            ch(dve, nc.vector.scalar_tensor_tensor(base[0:digits, 0:cols], k.t0[0:digits, 0:cols], start,
                                                   tot[0:digits, 0:cols], ALU.add, ALU.subtract))
            if padded:
                end = k.small[0:digits, 2:3]
                ch(dve, nc.vector.tensor_tensor(end, start, size, ALU.add))
                ch(dve, nc.vector.tensor_scalar(end, end, 1.0 / P, None, ALU.mult))
                ch(dve, nc.vector.tensor_scalar(k.t0[0:digits, 0:chunks], k.count[0:digits, 0:chunks], end, None,
                                                ALU.is_ge))
                dve.sem_inc(k.dve_done.sem, 1)
                dve.wait_ge(k.pe_done.sem, k.pe_done.at(2))
                ch(dve, nc.vector.tensor_scalar(k.t0[0:1, 0:chunks], k.ps[0:1, 512:512 + chunks], float(G - 1), None,
                                                ALU.min))
                for n, (step, start) in enumerate(COLUMNS):
                    ch(dve, nc.vector.tensor_scalar(group_row[32 * n:32 * n + 1, :], k.t0[0:1, 0:chunks],
                                                    float(step), float(start), ALU.mult, ALU.add))

        @block.tensor
        def _(pe):
            pe.wait_ge(k.dve_done.sem, k.dve_done.at(1))
            nc.tensor.matmul(k.ps[0:digits, 0:1], k.before[0:digits, 0:digits], k.small[0:digits, 0:1],
                             start=True, stop=True).then_inc(k.pe_done.sem, 1)
            if padded:
                pe.wait_ge(k.dve_done.sem, k.dve_done.at(2))
                nc.tensor.matmul(k.ps[0:1, 512:512 + chunks], k.ones[0:digits, 0:1], k.t0[0:digits, 0:chunks],
                                 start=True, stop=True).then_inc(k.pe_done.sem, 1)
    k.dve_done.base += 2 if padded else 1
    k.pe_done.base += 2 if padded else 1

    H = B // 2

    def ranks(h, n):
        return k.ps[0:parts, 1024 * h + 512 * n:1024 * h + 512 * n + H * digits].rearrange("p (b d) -> p b d", b=H)

    with nc.Block() as block:
        @block.vector
        def _(dve):
            dve.sem_inc(k.marks_free.sem, 2)
            with dve.Fori(0, turns) as t:
                for h in range(2):
                    i = t * BODY + h * B
                    dve.wait_ge(k.marks_free.sem, 2 * t + (k.marks_free.base + h + 1))
                    one_hots(dve, t, h).then_inc(k.marks_ready.sem, 1)
                for h in range(2):
                    i = t * BODY + h * B
                    dve.wait_ge(k.pe_done.sem, 2 * t + (k.pe_done.base + h + 3))
                    at = k.ps[0:parts, 1024 * h:1024 * (h + 1)].rearrange("p (n x) -> p n x", n=2)[
                        :, :, 0:H * digits].rearrange("p n (b d) -> p n b d", b=H)
                    nc.vector.tensor_tensor(
                        k.picked[h][0:parts, :, 0:digits].rearrange("p (n b) d -> p n b d", n=2), at,
                        k.marks[h][0:parts, :, 0:digits].rearrange("p (n b) d -> p n b d", n=2),
                        ALU.mult).then_inc(k.dve_done.sem, 1)
                    dve.wait_ge(k.dve_done.sem, 2 * t + (k.dve_done.base + h + 1))
                    nc.vector.tensor_reduce(k.pos[0:parts, bass.ds(i, B)], k.picked[h][0:parts, :, 0:digits],
                                            AX.X, ALU.add).then_inc(k.marks_free.sem, 1)

        @block.gpsimd
        def _(pool):
            with pool.Fori(0, turns) as t:
                for h in range(2):
                    i = t * BODY + h * B
                    pool.wait_ge(k.pe_done.sem, 2 * t + (k.pe_done.base + h + 1))
                    nc.gpsimd.tensor_tensor(k.begin[h][0:P, :, 0:digits], col(base[:, bass.ds(i, B)], digits),
                                            row(k.ident[:, 0:digits], B), ALU.mult).then_inc(k.pool_done.sem, 1)

        @block.tensor
        def _(pe):
            pe.sem_inc(k.pe_done.sem, 2)
            with pe.Fori(0, turns) as t:
                for h in range(2):
                    pe.wait_ge(k.marks_ready.sem, 2 * t + (k.marks_ready.base + h + 1))
                    pe.wait_ge(k.pool_done.sem, 2 * t + (k.pool_done.base + h + 1))
                    for n in range(2):
                        half = slice(n * H, (n + 1) * H)
                        nc.tensor.matmul(ranks(h, n), k.before16[0:parts, 0:parts],
                                         k.marks[h][0:parts, half, 0:digits], start=True, stop=False)
                        last = nc.tensor.matmul(ranks(h, n), k.ones[:, 0:parts], k.begin[h][:, half, 0:digits],
                                                start=False, stop=True)
                    last.then_inc(k.pe_done.sem, 1)
    k.marks_free.base += 2 + 2 * turns
    k.marks_ready.base += 2 * turns
    k.pool_done.base += 2 * turns
    k.pe_done.base += 2 + 2 * turns
    k.dve_done.base += 2 * turns

    with nc.Block() as block:
        @block.vector
        def _(dve):
            ch = k.dve_step
            pos, chunk, lane = (x[0:parts, 0:cols] for x in (k.pos, k.chunk, k.lane))
            ch(dve, nc.vector.tensor_scalar(chunk, pos, 1.0 / P, -HALF, ALU.mult, ALU.add))
            ch(dve, nc.vector.tensor_scalar(chunk, chunk, ROUND, -ROUND, ALU.add, ALU.add))
            ch(dve, nc.vector.scalar_tensor_tensor(lane, chunk, -float(P), pos, ALU.mult, ALU.add))


def permute(k, parts, cols, chunks, out_a, out_b, first, last):
    nc = k.nc
    turns = cols // BODY
    scatters = (last - first) // 2
    with nc.Block() as block:
        @block.scalar
        def _(act):
            def stage(t, h):
                cols = bass.ds((t * 2 + (first + h)) * B, B)
                nc.scalar.copy(k.at_row[h][:, :], k.row_of[:, cols]).then_inc(k.index_ready.sem, 1)
                nc.scalar.copy(k.at_pair[h][:, :, :], k.pair[:, cols, :]).then_inc(k.index_ready.sem, 1)

            for h in range(2):
                stage(0, h)
            with act.Fori(0, scatters - 1) as t:
                for h in range(2):
                    act.wait_ge(k.scattered[h].sem, t * (16 * B) + (k.scattered[h].base + 16 * B))
                    act.sem_inc(k.act_turn.sem, 1)
                    stage(t + 1, h)

        @block.gpsimd
        def _(pool):
            with pool.Fori(0, scatters) as t:
                for h in range(2):
                    pool.wait_ge(k.index_ready.sem, 4 * t + (k.index_ready.base + 2 * h + 2))
                    pool.sem_inc(k.pool_turn.sem, 1)
                    for b in range(B):
                        nc.gpsimd.indirect_dma_start(
                            k.by_source, bass.IndirectOffsetOnAxis(ap=k.at_row[h][:, b:b + 1], axis=0),
                            k.at_pair[h][:, b, :], None).then_inc(k.scattered[h].sem, 16)
            for h in range(2):
                pool.wait_ge(k.scattered[h].sem, k.scattered[h].at(16 * B * scatters))

        @block.vector
        def _(dve):
            dve.sem_inc(k.marks_free.sem, 2)
            with dve.Fori(0, turns) as t:
                for h in range(2):
                    dve.wait_ge(k.marks_free.sem, 2 * t + (k.marks_free.base + h + 1))
                    for b in range(B):
                        i = t * BODY + (h * B + b)
                        lane, chunk = k.lane[0:parts, bass.ds(i, 1)], k.chunk[0:parts, bass.ds(i, 1)]
                        for n, v in enumerate((k.va, k.vb)):
                            nc.vector.tensor_scalar(k.to_lane[h][0:parts, b, n, :], k.count16[0:parts, 0:P], lane,
                                                    v[0:parts, bass.ds(i, 1)], ALU.is_equal, ALU.mult)
                        last = nc.vector.tensor_scalar(k.to_chunk[h][0:parts, b, 0:chunks],
                                                       k.count16[0:parts, 0:chunks], chunk, None, ALU.is_equal)
                    last.then_inc(k.marks_ready.sem, 1)
            dve.wait_ge(k.marks_free.sem, k.marks_free.at(2 + 2 * turns))
            k.dve_step(dve, nc.vector.tensor_copy(out_a, k.ps[:, 0:chunks]))
            k.dve_step(dve, nc.vector.tensor_copy(out_b, k.ps[:, 512:512 + chunks]))

        @block.tensor
        def _(pe):
            for n in range(2):
                nc.tensor.matmul(k.ps[:, 512 * n:512 * n + chunks], k.zeros[:, 0:P], k.zeros[:, 0:chunks],
                                 start=True, stop=False, skip_group_check=True)
            with pe.Fori(0, turns) as t:
                for h in range(2):
                    pe.wait_ge(k.marks_ready.sem, 2 * t + (k.marks_ready.base + h + 1))
                    for b in range(B):
                        for n in range(2):
                            last = nc.tensor.matmul(k.ps[:, 512 * n:512 * n + chunks], k.to_lane[h][0:parts, b, n, :],
                                                    k.to_chunk[h][0:parts, b, 0:chunks],
                                                    start=False, stop=False, skip_group_check=True)
                    last.then_inc(k.marks_free.sem, 1)
    k.marks_free.base += 2 + 2 * turns
    k.marks_ready.base += 2 * turns
    k.index_ready.base += 4 * scatters
    for h in range(2):
        k.scattered[h].base += 16 * B * scatters


def order_edges(k):
    nc = k.nc
    place(k, LP, CE, G, True, KS, k.sgroup)
    target_keys(k)
    place(k, LP, CIN, L, False)
    permute(k, LP, CIN, CMID, k.va[:, 0:CMID], k.vb[:, 0:CMID], 0, BESIDE)
    with nc.Block() as block:
        @block.gpsimd
        def _(pool):
            nc.gpsimd.affine_select(out=k.t2[:, 0:CMID], in_=k.ones[:, 0:CMID], compare_op=ALU.is_gt, fill=0.0,
                                    base=ES, pattern=[[-P, CMID]],
                                    channel_multiplier=-1).then_inc(k.pool_done.sem, 1)

        @block.vector
        def _(dve):
            ch = k.dve_step
            m = slice(0, CMID)
            node, valid, group, local, own = k.t0[:, m], k.t2[:, m], k.key[:, m], k.t3[:, m], k.t4[:, m]
            ch(dve, nc.vector.tensor_scalar(node, k.va[:, m], MID, None, ALU.add))
            split(k, dve, node, group, local, CMID)
            dve.wait_ge(k.pool_done.sem, k.pool_done.at(1))
            ch(dve, nc.vector.tensor_scalar(own, k.vb[:, m], SELF, None, ALU.is_equal))
            ch(dve, nc.vector.tensor_tensor(k.t5[:, m], k.va[:, m], k.vb[:, m], ALU.subtract))
            ch(dve, nc.vector.tensor_tensor(k.t5[:, m], k.t5[:, m], own, ALU.mult))
            ch(dve, nc.vector.tensor_tensor(k.vb[:, m], k.vb[:, m], k.t5[:, m], ALU.add))
            ch(dve, nc.vector.scalar_tensor_tensor(k.va[:, m], own, 128.0, local, ALU.mult, ALU.add))
            ch(dve, nc.vector.scalar_tensor_tensor(k.va[:, m], k.va[:, m], 1.0, valid, ALU.add, ALU.mult))
            ch(dve, nc.vector.tensor_tensor(k.vb[:, m], k.vb[:, m], valid, ALU.mult))
            ch(dve, nc.vector.scalar_tensor_tensor(group, group, 1.0, valid, ALU.add, ALU.mult))
            ch(dve, nc.vector.tensor_scalar(group, group, -1.0, None, ALU.add))
    k.pool_done.base += 1
    place(k, P, CMID, G, True, KD, k.tgroup)
    permute(k, P, CMID, KD, k.tself[:, :], k.t0[:, 0:KD], BESIDE, CE // B)
    with nc.Block() as block:
        @block.sync
        def _(sp):
            sp.dma_start(k.sorted_pair[:, :, :], k.by_source.rearrange("(p c) v -> p c v", p=P)).then_inc(
                k.loaded.sem, 16)

        @block.vector
        def _(dve):
            ch = k.dve_step
            ch(dve, nc.vector.tensor_scalar(k.t2[:, 0:KD], k.tself[:, :], 128.0, None, ALU.is_gt))
            ch(dve, nc.vector.scalar_tensor_tensor(k.tloc[:, :], k.t2[:, 0:KD], -128.0, k.tself[:, :],
                                                   ALU.mult, ALU.add))
            ch(dve, nc.vector.tensor_scalar(k.t0[:, 0:KD], k.t0[:, 0:KD], MID, None, ALU.add))
            ch(dve, nc.vector.tensor_copy(k.tsrc[:, :], k.t0[:, 0:KD]))
            dve.wait_ge(k.loaded.sem, k.loaded.at(16))
            m = slice(0, KS)
            place_kind, target = k.sorted_pair[:, :, 0], k.sorted_pair[:, :, 1]
            ch(dve, nc.vector.tensor_scalar(k.t0[:, m], place_kind, 1.0 / 128, -HALF, ALU.mult, ALU.add))
            ch(dve, nc.vector.tensor_scalar(k.t0[:, m], k.t0[:, m], ROUND, -ROUND, ALU.add, ALU.add))
            ch(dve, nc.vector.scalar_tensor_tensor(k.sloc[:, :], k.t0[:, m], -128.0, place_kind, ALU.mult, ALU.add))
            ch(dve, nc.vector.tensor_copy(k.sdst[:, :], target))
            ch(dve, nc.vector.scalar_tensor_tensor(k.t0[:, m], k.t0[:, m], float(N), target, ALU.mult, ALU.add))
            ch(dve, nc.vector.tensor_copy(k.skind[:, :], k.t0[:, m]))
    k.loaded.base += 16



def load(k, loads):
    nc = k.nc
    with nc.Block() as block:
        @block.sync
        def _(sp):
            for to, what in loads:
                sp.dma_start(to, what).then_inc(k.loaded.sem, 16)
            sp.wait_ge(k.loaded.sem, k.loaded.at(16 * len(loads)))
    k.loaded.base += 16 * len(loads)


def to_all(pairs):
    return [(dst[:, :], src.unsqueeze(0).broadcast_to([P, D])) for dst, src in pairs]


def load_attention(k, p):
    loads = to_all([(k.bias[i], p[f"L0_gnn_b{i + 1}"]) for i in range(4)])
    loads += [(k.w_gat[i][:, 0:D], p[f"L0_gnn_W{i + 1}"]) for i in range(4)]
    for i in range(4):
        for n, name in enumerate(("as", "ad")):
            loads.append((k.a_col[:, 2 * i + n:2 * i + n + 1],
                          p[f"L0_gnn_{name}{i + 1}"].rearrange("h c -> (h c)").unsqueeze(1)))
    load(k, loads)


def load_others(k, p):
    loads = to_all([(k.gamma, p["L1_gnn_ln_gamma"]), (k.beta, p["L1_gnn_ln_beta"]), (k.bias1, p["L1_gnn_bias"]),
                    (k.bias2[0], p["L2_gnn_bl"]), (k.bias2[1], p["L2_gnn_br"]), (k.bias3, p["L3_gnn_b"])])
    loads += [(k.x[:, :, :], p["x"].rearrange("(g l) f -> l g f", l=L)),
              (k.w_base[:, :, :], p["L1_gnn_weight"].rearrange("b i o -> i b o")),
              (k.alpha[:, :], p["L1_gnn_alpha"].rearrange("r b -> (r b)").unsqueeze(0).broadcast_to([P, REL * BASES])),
              (k.w_self[:, :], p["L1_gnn_weight_self_loop"]), (k.w_l[:, :], p["L2_gnn_Wl"]),
              (k.w_r[:, :], p["L2_gnn_Wr"]), (k.w_cat[:, :], p["L3_gnn_W"])]
    load(k, loads)


def prepare_attention(k):
    nc = k.nc
    with nc.Block() as block:
        @block.gpsimd
        def _(pool):
            ch = k.pool_step
            ch(pool, nc.gpsimd.affine_select(out=k.own[:, :], in_=k.ones[:, 0:HEADS], compare_op=ALU.is_ge, fill=0.0,
                                             base=0, pattern=[[-C, HEADS]], channel_multiplier=1))
            nc.gpsimd.affine_select(out=k.own[:, :], in_=k.own[:, :], compare_op=ALU.is_ge, fill=0.0, base=C - 1,
                                    pattern=[[C, HEADS]], channel_multiplier=-1).then_inc(k.pool_done.sem, 1)

        @block.tensor
        def _(pe):
            for i in range(4):
                last = nc.tensor.transpose(k.ps[:, 512 * i:512 * i + P], k.w_gat[i][:, 0:D], k.ident[:, :])
            last.then_inc(k.pe_done.sem, 1)
            pe.wait_ge(k.dve_done.sem, k.dve_done.at(1))
            for i in range(4):
                last = nc.tensor.matmul(k.ps[:, 512 * i + 256:512 * i + 256 + 2 * HEADS], k.w_t[:, i, :],
                                        k.a_wide[:, i, :, :].rearrange("p n h -> p (n h)"), start=True, stop=True)
            last.then_inc(k.pe_done.sem, 1)

        @block.vector
        def _(dve):
            ch = k.dve_step
            dve.wait_ge(k.pool_done.sem, k.pool_done.at(1))
            for i in range(4):
                for n in range(2):
                    ch(dve, nc.vector.tensor_scalar(k.a_wide[:, i, n, :], k.own[:, :],
                                                    k.a_col[:, 2 * i + n:2 * i + n + 1], None, ALU.mult))
            dve.wait_ge(k.pe_done.sem, k.pe_done.at(1))
            for i in range(4):
                ch(dve, nc.vector.tensor_copy(k.w_t[:, i, :], k.ps[:, 512 * i:512 * i + P]))
            dve.sem_inc(k.dve_done.sem, 1)
            dve.wait_ge(k.pe_done.sem, k.pe_done.at(2))
            for i in range(4):
                ch(dve, nc.vector.tensor_copy(k.w_gat[i][:, D:D + 2 * HEADS],
                                              k.ps[:, 512 * i + 256:512 * i + 256 + 2 * HEADS]))
    k.pool_done.base += 1
    k.pe_done.base += 2
    k.dve_done.base += 1


def prepare_others(k):
    nc = k.nc
    with nc.Block() as block:
        @block.tensor
        def _(pe):
            for n in range(2):
                last = nc.tensor.transpose(k.ps[:, 512 * n:512 * n + P], k.w_cat[:, n * D:(n + 1) * D],
                                           k.ident[:, :])
            last.then_inc(k.pe_done.sem, 1)

        @block.vector
        def _(dve):
            ch = k.dve_step
            for r in range(REL):
                w = k.w_rel[:, r * D:(r + 1) * D]
                for b in range(BASES):
                    a = k.alpha[:, r * BASES + b:r * BASES + b + 1]
                    if b == 0:
                        ch(dve, nc.vector.tensor_scalar(w, k.w_base[:, b, :], a, None, ALU.mult))
                    else:
                        ch(dve, nc.vector.scalar_tensor_tensor(w, k.w_base[:, b, :], a, w, ALU.mult, ALU.add))
            dve.wait_ge(k.pe_done.sem, k.pe_done.at(1))
            for n in range(2):
                ch(dve, nc.vector.tensor_copy(k.w_cat_t[:, n, :], k.ps[:, 512 * n:512 * n + P]))
    k.pe_done.base += 1


def transposed_lists(k):
    nc = k.nc
    first, last, pen = k.m_first, k.m_last, k.m_pen
    with nc.Block() as block:
        @block.sync
        def _(sp):
            sp.wait_ge(k.dve_done.sem, k.dve_done.at(2))
            sp.dma_start(k.place_list.rearrange("(r j) -> r j", j=RL), k.place_row[:, :]).then_inc(k.stored.sem, 16)
            sp.wait_ge(k.stored.sem, k.stored.at(16))

        @block.tensor
        def _(pe):
            pe.wait_ge(k.dve_done.sem, k.dve_done.at(1))
            for n, x in enumerate((k.town, k.pen, k.place_of)):
                v = x[:, :].rearrange("p (r j) -> p j r", j=4)
                for j in range(4):
                    at = 512 * n + P * j
                    done = nc.tensor.transpose(k.ps[0:ROWS, at:at + P], v[:, j, :], k.ident[:, :])
            done.then_inc(k.pe_done.sem, 1)
            pe.wait_ge(k.dve_done.sem, k.dve_done.at(3))
            nc.tensor.matmul(k.ps[0:ROWS, 1536:1537], k.shift[0:ROWS, 0:ROWS], first[:, 0:1], start=True,
                             stop=True).then_inc(k.pe_done.sem, 1)
            pe.wait_ge(k.dve_done.sem, k.dve_done.at(4))
            for n in range(2):
                done = nc.tensor.matmul(k.ps[0:HEADS, 2048 + P * n:2048 + P * n + ROWS],
                                        k.small[0:ROWS, n:n + 1].broadcast_to([ROWS, HEADS]),
                                        k.ident[0:ROWS, 0:ROWS], start=True, stop=True)
            done.then_inc(k.pe_done.sem, 1)

        @block.gpsimd
        def _(pool):
            nc.gpsimd.iota(k.self_count[:, :], [[0, 1]], base=0, channel_multiplier=1,
                           allow_small_or_imprecise_dtypes=True).then_inc(k.pool_done.sem, 1)
            nc.gpsimd.affine_select(out=k.shift[:, :], in_=k.ones[:, 0:P], compare_op=ALU.is_equal, fill=0.0,
                                    base=-1, pattern=[[-1, P]], channel_multiplier=1).then_inc(k.pool_done.sem, 1)

        @block.vector
        def _(dve):
            ch = k.dve_step
            ch(dve, nc.vector.memset(k.one16[:, :], 1.0))
            ch(dve, nc.vector.tensor_scalar(k.pen[:, :], k.tloc[:, :], 0.0, -BIG, ALU.is_equal, ALU.mult))
            ch(dve, nc.vector.tensor_scalar(k.town[:, :], k.tself[:, :], 128.0, None, ALU.is_gt))
            ch(dve, nc.vector.tensor_copy(k.node_of[:, :], k.tsrc[:, :]))
            split(k, dve, k.node_of[:, :], k.group_of[:, :], k.place_of[:, :], KD)
            dve.sem_inc(k.dve_done.sem, 1)
            dve.wait_ge(k.pe_done.sem, k.pe_done.at(1))
            ch(dve, nc.vector.tensor_copy(k.place_row[:, :], k.ps[0:ROWS, 1024:1536]))
            dve.sem_inc(k.dve_done.sem, 1)
            ch(dve, nc.vector.tensor_copy(first[:, :], k.ps[0:ROWS, 0:512]))
            ch(dve, nc.vector.tensor_copy(pen[:, :], k.ps[0:ROWS, 512:1024]))
            dve.wait_ge(k.pool_done.sem, k.pool_done.at(2))
            dve.sem_inc(k.dve_done.sem, 1)
            ch(dve, nc.vector.tensor_copy(last[:, 0:RL - 1], first[:, 1:RL]))
            dve.wait_ge(k.pe_done.sem, k.pe_done.at(2))
            ch(dve, nc.vector.tensor_copy(last[:, RL - 1:RL], k.ps[0:ROWS, 1536:1537]))
            ch(dve, nc.vector.tensor_reduce(k.small[0:ROWS, 0:1], first[:, :], AX.X, ALU.max))
            ch(dve, nc.vector.tensor_reduce(k.small[0:ROWS, 1:2], last[:, :], AX.X, ALU.max))
            dve.sem_inc(k.dve_done.sem, 1)
            ch(dve, nc.vector.tensor_scalar(k.m_reset[:, :], first[:, :], -BIG, None, ALU.mult))
            ch(dve, nc.vector.tensor_scalar(k.m_keep[:, :], first[:, :], -1.0, 1.0, ALU.mult, ALU.add))
            ch(dve, nc.vector.tensor_scalar(k.m_reset_b[:, :], last[:, :], -BIG, None, ALU.mult))
            one = k.ones[0:ROWS, 0:RL]
            ch(dve, nc.vector.tensor_tensor_scan(k.m_seen[:, :], one, first[:, :], 0.0, ALU.mult, ALU.max))
            ch(dve, nc.vector.tensor_tensor_scan(k.m_seen_b[:, ::-1], one, last[:, ::-1], 0.0, ALU.mult, ALU.max))
            ch(dve, nc.vector.tensor_scalar(k.m_open[:, :], k.m_seen[:, :], -1.0, 1.0, ALU.mult, ALU.add))
            ch(dve, nc.vector.tensor_scalar(k.m_seen[:, :], k.m_seen[:, :], -BIG, None, ALU.mult))
            ch(dve, nc.vector.tensor_scalar(k.m_seen_b[:, :], k.m_seen_b[:, :], -BIG, None, ALU.mult))
            dve.wait_ge(k.pe_done.sem, k.pe_done.at(3))
            has = [k.ps[0:HEADS, 2048 + P * n:2048 + P * n + ROWS] for n in range(2)]
            ch(dve, nc.vector.tensor_scalar(k.row_mask[:, 0, :], has[0], -BIG, None, ALU.mult))
            ch(dve, nc.vector.tensor_scalar(k.row_mask[:, 1, :], has[1], -BIG, None, ALU.mult))
            ch(dve, nc.vector.tensor_scalar(k.row_mask[:, 2, :], has[0], -1.0, 1.0, ALU.mult, ALU.add))
    k.stored.base += 16
    k.dve_done.base += 4
    k.pe_done.base += 3
    k.pool_done.base += 2


TILES = 5


def products(k, x, jobs):
    nc = k.nc
    turns, J = G // TILES, len(jobs)
    stores = sum(TILES for _, out in jobs if out is None)
    items = [(b, j) for b in range(TILES) for j in range(J)]

    def turned(b):
        at = 512 * (b // 4) + P * (b % 4)
        return k.ps[:, at:at + L]

    def result(n, width):
        at = 512 * (2 + n % 5)
        return k.ps[0:L, at:at + width]

    with nc.Block() as block:
        @block.scalar
        def _(act):
            with act.Fori(0, turns) as t:
                for b in range(TILES):
                    act.wait_ge(k.turned.sem, TILES * t + (k.turned.base + b + 1))
                    nc.scalar.copy(k.xs[b][:, :], x[:, bass.ds(t * TILES + b, 1), :].rearrange(
                        "p a f -> p (a f)")).then_inc(k.act_done.sem, 1)
                for b in range(TILES):
                    act.wait_ge(k.turned.sem, TILES * t + (k.turned.base + 2 * TILES))
                    act.wait_ge(k.multiplied.sem, TILES * J * t + (k.multiplied.base + J * b + J))
                    nc.scalar.copy(k.xt[b][:, :], turned(b)).then_inc(k.act_done.sem, 1)

        @block.tensor
        def _(pe):
            pe.sem_inc(k.turned.sem, TILES)
            pe.sem_inc(k.multiplied.sem, TILES * J)
            with pe.Fori(0, turns) as t:
                for b in range(TILES):
                    pe.wait_ge(k.act_done.sem, 2 * TILES * t + (k.act_done.base + b + 1))
                    nc.tensor.transpose(turned(b), k.xs[b][:, :], k.ident[0:L, 0:L]).then_inc(k.turned.sem, 1)
                for n, (b, j) in enumerate(items):
                    if j == 0:
                        pe.wait_ge(k.act_done.sem, 2 * TILES * t + (k.act_done.base + TILES + b + 1))
                    pe.wait_ge(k.taken.sem, TILES * J * t + (k.taken.base + n + 1))
                    nc.tensor.matmul(result(n, jobs[j][0].shape[1]), k.xt[b][:, :], jobs[j][0], start=True,
                                     stop=True).then_inc(k.multiplied.sem, 1)

        @block.vector
        def _(dve):
            dve.sem_inc(k.taken.sem, 5)
            if stores:
                dve.sem_inc(k.tabled.sem, 16 * stores)
            with dve.Fori(0, turns) as t:
                if stores:
                    dve.wait_ge(k.tabled.sem, t * (16 * stores) + (k.tabled.base + 16 * stores))
                for n, (b, j) in enumerate(items):
                    rhs, out = jobs[j]
                    width = rhs.shape[1]
                    to = k.stage[b][j][:, :] if out is None else \
                        out[:, bass.ds(t * TILES + b, 1), 0:width].rearrange("p a f -> p (a f)")
                    dve.wait_ge(k.multiplied.sem, TILES * J * t + (k.multiplied.base + TILES * J + n + 1))
                    nc.vector.tensor_copy(to, result(n, width)).then_inc(k.taken.sem, 1)

        if stores:
            @block.sync
            def _(sp):
                table = k.table_rel.rearrange("(r n) f -> n r f", n=N)
                with sp.Fori(0, turns) as t:
                    for n, (b, j) in enumerate(items):
                        if jobs[j][1] is None:
                            sp.wait_ge(k.taken.sem, TILES * J * t + (k.taken.base + 5 + n + 1))
                            sp.dma_start(table[bass.ds((t * TILES + b) * L, L), 4 * j:4 * j + 4, :],
                                         k.stage[b][j][:, :].rearrange("p (r f) -> p r f", r=4)
                                         ).then_inc(k.tabled.sem, 16)
                sp.wait_ge(k.tabled.sem, k.tabled.at(16 * stores * (turns + 1)))
    k.turned.base += TILES * (turns + 1)
    k.multiplied.base += TILES * J * (turns + 1)
    k.act_done.base += 2 * TILES * turns
    k.taken.base += TILES * J * turns + 5
    if stores:
        k.tabled.base += 16 * stores * (turns + 1)


def store_table(k, pairs):
    nc = k.nc
    with nc.Block() as block:
        @block.sync
        def _(sp):
            for to, what in pairs:
                sp.dma_start(to.rearrange("(g l) f -> l g f", l=L), what).then_inc(k.stored.sem, 16)
            sp.wait_ge(k.stored.sem, k.stored.at(16 * len(pairs)))
    k.stored.base += 16 * len(pairs)


def gather(k, pool, table, turns, ring, first):
    nc = k.nc
    with pool.Fori(0, turns) as t:
        for h in range(ring):
            pool.wait_ge(k.index_ready.sem, ring * t + (k.index_ready.base + first + h + 1))
            pool.wait_ge(k.rows_free.sem, ring * t + (k.rows_free.base + h + 1))
            pool.sem_inc(k.pool_turn.sem, 1)
            for b in range(B):
                nc.gpsimd.indirect_dma_start(
                    k.rows[h][:, b, :], None, table,
                    bass.IndirectOffsetOnAxis(ap=k.index[h][:, b:b + 1], axis=0)).then_inc(k.gathered[h].sem, 16)


def flat(ap):
    return ap.rearrange("p b f -> p (b f)")


def thirds(k, x, parts, do):
    nc = k.nc
    do(nc.vector.tensor_copy(parts[0], x))
    do(nc.vector.tensor_tensor(x, x, parts[0], ALU.subtract))
    do(nc.vector.tensor_copy(parts[1], x))
    do(nc.vector.tensor_tensor(parts[2], x, parts[1], ALU.subtract))




class Sweep:

    def __init__(self, k, body, turns, label, group, weigh, count, slots, kept_blocks=0):
        self.k, self.body, self.turns, self.label, self.group = k, body, turns, label, group
        self.weigh, self.count, self.slots, self.kept_blocks = weigh, count, slots, kept_blocks
        self.rings = sum(kind == "ring" for kind, _ in body)
        self.kepts = len(body) - self.rings
        assert self.rings % slots == 0 and len(body) % 2 == 0

    def chunk(self, t, n):
        kind, j = self.body[n]
        if kind == "kept":
            return t * (self.kepts * B) + j * B
        return t * (self.rings * B) + (self.kept_blocks + j) * B

    def rows(self, t, n):
        kind, j = self.body[n]
        if kind == "kept":
            return self.k.kept[:, bass.ds(self.chunk(t, n) * D, B * D)]
        return flat(self.k.rows[j % self.slots][:, :, :])

    def wait_rows(self, eng, t, n):
        kind, j = self.body[n]
        if kind == "ring":
            s = self.k.gathered[j % self.slots]
            per = self.rings // self.slots
            eng.wait_ge(s.sem, t * (16 * B * per) + (s.base + 16 * B * (j // self.slots + 1)))


def sweep_vector(k, dve, s):
    nc, N_ = k.nc, len(s.body)
    with dve.Fori(0, s.turns) as t:
        def last_part(n):
            u = n % 2
            dve.wait_ge(k.rounded.sem, t * (2 * N_) + (k.rounded.base + 2 * n + 2))
            nc.vector.tensor_tensor(k.parts[u][:, 2, :], s.rows(t, n), k.parts[u][:, 1, :],
                                    ALU.subtract).then_inc(k.marks_ready.sem, 1)
            if s.body[n][0] == "ring":
                dve.wait_ge(k.marks_ready.sem, t * N_ + (k.marks_ready.base + n + 1))
                dve.sem_inc(k.rows_free.sem, 1)

        for n in range(N_):
            u = n % 2
            i = s.chunk(t, n)
            s.wait_rows(dve, t, n)
            if s.weigh:
                x = s.rows(t, n).rearrange("p (a c) -> p a c", c=C)
                nc.vector.tensor_tensor(x, x, col(flat(k.expo[:, bass.ds(i, B), :]), C),
                                        ALU.mult).then_inc(k.weighed.sem, 1)
            if n:
                last_part(n - 1)
            dve.wait_ge(k.parts_free.sem, t * N_ + (k.parts_free.base + n + 1))
            nc.vector.tensor_tensor(k.member[u][:, :, :], col(s.label[:, bass.ds(i, B)], L),
                                    row(k.count16[:, 1:L + 1], B), ALU.is_equal)
            dve.wait_ge(k.rounded.sem, t * (2 * N_) + (k.rounded.base + 2 * n + 1))
            x = s.rows(t, n)
            nc.vector.tensor_tensor(x, x, k.parts[u][:, 0, :], ALU.subtract).then_inc(k.weighed.sem, 1)
        last_part(N_ - 1)


def sweep_scalar(k, act, s):
    nc, N_ = k.nc, len(s.body)
    with act.Fori(0, s.turns) as t:
        for n in range(N_):
            for part in range(2):
                if part == 0:
                    act.wait_ge(k.parts_free.sem, t * N_ + (k.parts_free.base + n + 1))
                if part == 0 and not s.weigh:
                    s.wait_rows(act, t, n)
                else:
                    steps = 2 if s.weigh else 1
                    act.wait_ge(k.weighed.sem, t * (steps * N_) + (k.weighed.base + steps * n + part + steps - 1))
                if s.body[n][0] == "kept":
                    act.sem_inc(k.act_turn.sem, 1)
                nc.scalar.copy(k.parts[n % 2][:, part, :], s.rows(t, n)).then_inc(k.rounded.sem, 1)


def sweep_tensor(k, pe, s):
    nc, N_ = k.nc, len(s.body)
    for n in range(7):
        last = nc.tensor.matmul(k.ps[:, 512 * n:512 * (n + 1)], k.zeros[:, 0:P], k.zeros[:, :], start=True,
                                stop=False, skip_group_check=True)
    last.then_inc(k.parts_free.sem, 2)
    with pe.Fori(0, s.turns) as t:
        for n in range(N_):
            u = n % 2
            i = s.chunk(t, n)
            pe.reg_load(k.acc_regs, s.group[0:1, bass.ds(i, B)])
            to_acc = [pe.snap(r, min_val=0, max_val=ACC - D) for r in k.acc_regs]
            if s.weigh or s.count:
                p = 32 * (TO_WEIGHTS if s.weigh else TO_COUNT)
                pe.reg_load(k.sum_regs, s.group[p:p + 1, bass.ds(i, B)])
                to_sum = [pe.snap(r, min_val=ACC, max_val=ACC + (G - 1) * 3 * HEADS) for r in k.sum_regs]
            pe.wait_ge(k.marks_ready.sem, t * N_ + (k.marks_ready.base + n + 1))
            for b in range(B):
                one = k.member[u][:, b, :]
                for part in range(3):
                    last = nc.tensor.matmul(k.ps[0:L, bass.ds(to_acc[b], D)], one,
                                            k.parts[u][:, part, b * D:(b + 1) * D], start=False, stop=False,
                                            skip_group_check=True)
                if s.weigh:
                    last = nc.tensor.matmul(k.ps[0:L, bass.ds(to_sum[b], 3 * HEADS)], one,
                                            k.share[:, bass.ds((i + b) * (3 * HEADS), 3 * HEADS)],
                                            start=False, stop=False, skip_group_check=True)
                if s.count:
                    last = nc.tensor.matmul(k.ps[0:L, bass.ds(to_sum[b], 1)], one, k.one16[:, 0:1],
                                            start=False, stop=False, skip_group_check=True)
            last.then_inc(k.parts_free.sem, 1)


def sweep_over(k, s):
    blocks = len(s.body) * s.turns
    k.parts_free.base += 2 + blocks
    k.marks_ready.base += blocks
    k.weighed.base += (2 if s.weigh else 1) * blocks
    k.rounded.base += 2 * blocks
    for h in range(s.slots):
        k.gathered[h].base += 16 * B * (s.rings * s.turns // s.slots)


def feed_indices(k, sp, index, start, turns, ring):
    def feed(t, h):
        sp.dma_start(k.index[h][:, :], index[:, bass.ds(t * (ring * B) + (start + h * B), B)]).then_inc(
            k.fed[h].sem, 16)
        sp.wait_ge(k.fed[h].sem, 16 * t + (k.fed[h].base + 16))
        sp.sem_inc(k.index_ready.sem, 1)

    for h in range(ring):
        feed(0, h)
    with sp.Fori(0, turns - 1) as t:
        for h in range(ring):
            sp.wait_ge(k.gathered[h].sem, t * (16 * B) + (k.gathered[h].base + 16 * B))
            feed(t + 1, h)
    for h in range(ring):
        k.fed[h].base += 16 * turns


def aggregate(k, table, index, label, group, chunks, count):
    nc = k.nc
    turns = chunks // (RING * B)
    s = Sweep(k, [("ring", h) for h in range(RING)], turns, label, group, False, count, RING)

    with nc.Block() as block:
        @block.sync
        def _(sp):
            sp.sem_inc(k.rows_free.sem, RING)
            feed_indices(k, sp, index, 0, turns, RING)

        @block.gpsimd
        def _(pool):
            gather(k, pool, table, turns, RING, 0)

        @block.scalar
        def _(act):
            sweep_scalar(k, act, s)

        @block.vector
        def _(dve):
            sweep_vector(k, dve, s)

        @block.tensor
        def _(pe):
            sweep_tensor(k, pe, s)
    sweep_over(k, s)
    k.rows_free.base += RING * (turns + 1)
    k.index_ready.base += RING * turns


SLOTS = 3
BODY_OF_ATTENTION = [("ring", 0), ("kept", 0), ("ring", 1), ("ring", 2), ("kept", 1), ("ring", 3), ("ring", 4),
                     ("kept", 2), ("ring", 5), ("ring", 6), ("kept", 3), ("ring", 7), ("kept", 4), ("ring", 8)]


def attention(k):
    nc = k.nc
    turns = KEPT // 5
    s = Sweep(k, BODY_OF_ATTENTION, turns, k.tloc, k.tgroup, True, False, SLOTS, KEPT)
    assert s.rings * turns + KEPT == KD // B and s.kepts * turns == KEPT
    look = KD // BODY
    blocks = KD // B

    with nc.Block() as block:
        @block.gpsimd
        def _(pool):
            keep_turns = KEPT // 2
            with pool.Fori(0, keep_turns) as t:
                for h in range(2):
                    pool.wait_ge(k.index_ready.sem, 2 * t + (k.index_ready.base + h + 1))
                    pool.sem_inc(k.pool_turn.sem, 1)
                    for b in range(B):
                        nc.gpsimd.indirect_dma_start(
                            k.rows[h][:, b, :], None, k.table,
                            bass.IndirectOffsetOnAxis(ap=k.index[h][:, b:b + 1], axis=0)).then_inc(
                                k.kept_in[h].sem, 16)
            gather(k, pool, k.table, s.rings * turns // SLOTS, SLOTS, KEPT)

        @block.scalar
        def _(act):
            act.sem_inc(k.kept_done.sem, 2)
            with act.Fori(0, KEPT // 2) as t:
                for h in range(2):
                    i = t * BODY + h * B
                    if h == 0:
                        for g in range(2):
                            act.wait_ge(k.kept_done.sem, 2 * t + (k.kept_done.base + g + 1))
                            act.sem_inc(k.act_turn.sem, 1)
                            nc.scalar.copy(k.index[g][:, :], k.tsrc[:, bass.ds(t * BODY + g * B, B)]).then_inc(
                                k.index_ready.sem, 1)
                    act.wait_ge(k.kept_in[h].sem, t * (16 * B) + (k.kept_in[h].base + 16 * B))
                    act.sem_inc(k.act_turn.sem, 1)
                    nc.scalar.copy(k.kept[:, bass.ds(i * D, B * D)], flat(k.rows[h][:, :, :])).then_inc(
                        k.kept_done.sem, 1)
            act.wait_ge(k.kept_done.sem, k.kept_done.at(2 + KEPT))
            act.sem_inc(k.rows_free.sem, SLOTS)
            act.wait_ge(k.dve_done.sem, k.dve_done.at(3))
            for n in range(2):
                last = nc.scalar.activation(k.s_tmp[n], k.s_tmp[n], ACT.Exp)
            last.then_inc(k.act_done.sem, 1)
            sweep_scalar(k, act, s)

        @block.sync
        def _(sp):
            sp.sem_inc(k.places_used.sem, 2)
            with sp.Fori(0, look) as t:
                for u in range(2):
                    sp.wait_ge(k.places_used.sem, 2 * t + (k.places_used.base + u + 1))
                    sp.dma_start(k.places[u], k.place_list[bass.ds((2 * t + u) * (B * P), B * P)].unsqueeze(
                        0).broadcast_to([L, B * P])).then_inc(k.places_in[u].sem, 16)
            for h in range(2):
                sp.wait_ge(k.kept_in[h].sem, k.kept_in[h].at(16 * B * KEPT // 2))
            feed_indices(k, sp, k.tsrc, KEPT * B, s.rings * turns // SLOTS, SLOTS)

        @block.tensor
        def _(pe):
            lookup_tensor(k, pe, look)
            weights_tensor(k, pe)
            pe.wait_ge(k.dve_done.sem, k.dve_done.at(4))
            sweep_tensor(k, pe, s)

        @block.vector
        def _(dve):
            lookup_vector(k, dve, look)
            weights_vector(k, dve)
            sweep_vector(k, dve, s)
    for h in range(2):
        k.kept_in[h].base += 16 * B * KEPT // 2
        k.places_in[h].base += 16 * look
    k.kept_done.base += 2 + KEPT
    k.index_ready.base += KEPT + s.rings * turns
    k.rows_free.base += SLOTS + s.rings * turns
    k.places_used.base += 2 + blocks
    k.hot.base += blocks
    k.looked.base += blocks
    k.seen.base += 2 + blocks
    k.look_step.base += 3 * blocks
    k.pe_done.base += 4
    k.dve_done.base += 4
    k.act_done.base += 1
    sweep_over(k, s)


def lookup_vector(k, dve, look):
    nc = k.nc

    def one_hots(t, u):
        dve.wait_ge(k.places_in[u].sem, 16 * t + (k.places_in[u].base + 16))
        dve.wait_ge(k.seen.sem, 2 * t + (k.seen.base + u + 1))
        nc.vector.tensor_scalar(k.place_hot[u], k.places[u], k.self_count[0:L, 0:1], None,
                                ALU.is_equal).then_inc(k.hot.sem, 1)
        dve.wait_ge(k.hot.sem, 2 * t + (k.hot.base + u + 1))
        dve.sem_inc(k.places_used.sem, 1)

    def pick(t, u):
        chunks = bass.ds(t * BODY + u * B, B)
        got = k.ps[:, 1024 * u:1024 * (u + 1)].rearrange("p (b e) -> p b e", e=128)
        at = 6 * t + (k.look_step.base + 3 * u)
        nc.vector.tensor_tensor(k.group_hot, col(k.group_of[:, chunks], G), row(k.count[:, 0:G], B),
                                ALU.is_equal).then_inc(k.look_step.sem, 1)
        dve.wait_ge(k.look_step.sem, at + 1)
        dve.wait_ge(k.looked.sem, 2 * t + (k.looked.base + u + 1))
        nc.vector.tensor_tensor(k.candidates.rearrange("p b (g e) -> p b g e", e=HEADS),
                                got[:, :, 0:G * HEADS].rearrange("p b (g e) -> p b g e", e=HEADS),
                                k.group_hot.unsqueeze(3).broadcast_to([P, B, G, HEADS]),
                                ALU.mult).then_inc(k.look_step.sem, 1)
        nc.vector.tensor_reduce(k.score_own[:, chunks, :],
                                got[:, :, G * HEADS:G * HEADS + 3 * HEADS].rearrange("p b (n e) -> p b e n", n=3),
                                AX.X, ALU.add).then_inc(k.seen.sem, 1)
        dve.wait_ge(k.look_step.sem, at + 2)
        nc.vector.tensor_reduce(k.score_src[:, chunks, :],
                                k.candidates.rearrange("p b (g e) -> p b e g", e=HEADS), AX.X,
                                ALU.add).then_inc(k.look_step.sem, 1)
        dve.wait_ge(k.look_step.sem, at + 3)

    dve.sem_inc(k.seen.sem, 2)
    one_hots(0, 0)
    with dve.Fori(0, look - 1) as t:
        one_hots(t, 1)
        pick(t, 0)
        one_hots(t + 1, 0)
        pick(t, 1)
    one_hots(look - 1, 1)
    pick(look - 1, 0)
    pick(look - 1, 1)


def lookup_tensor(k, pe, look):
    nc = k.nc
    with pe.Fori(0, look) as t:
        for u in range(2):
            p = 32 * TO_SCORES
            pe.reg_load(k.acc_regs, k.tgroup[p:p + 1, bass.ds(t * BODY + u * B, B)])
            at = [pe.snap(r, min_val=0, max_val=(G - 1) * 3 * HEADS) for r in k.acc_regs]
            pe.wait_ge(k.hot.sem, 2 * t + (k.hot.base + u + 1))
            pe.wait_ge(k.seen.sem, 2 * t + (k.seen.base + u + 1))
            for b in range(B):
                hot = k.place_hot[u][:, b * P:(b + 1) * P]
                to = 1024 * u + 128 * b
                for n in range(3):
                    nc.tensor.matmul(k.ps[:, to:to + G * HEADS], hot, k.scores_src[:, n, :], start=(n == 0),
                                     stop=(n == 2))
                last = nc.tensor.matmul(k.ps[:, to + G * HEADS:to + G * HEADS + 3 * HEADS], hot,
                                        k.scores_own[:, bass.ds(at[b], 3 * HEADS)], start=True, stop=True)
            last.then_inc(k.looked.sem, 1)


def weights_tensor(k, pe):
    nc = k.nc
    pe.wait_ge(k.look_step.sem, k.look_step.at(3 * (KD // B)))
    pe.wait_ge(k.seen.sem, k.seen.at(2 + KD // B))
    for n, x in enumerate((k.score_src, k.score_own)):
        v = x.rearrange("p (r j) e -> p e j r", j=4)
        for e in range(HEADS):
            for j in range(4):
                at = RL * (HEADS * n + e) + P * j
                last = nc.tensor.transpose(k.ps[0:ROWS, at:at + P], v[:, e, j, :], k.ident[:, :])
    last.then_inc(k.pe_done.sem, 1)
    pe.wait_ge(k.dve_done.sem, k.dve_done.at(1))
    for q in range(3):
        last = nc.tensor.transpose(k.ps[0:HEADS, P * q:P * q + ROWS], k.ends[:, q, :], k.ident[0:ROWS, 0:ROWS])
    last.then_inc(k.pe_done.sem, 1)
    pe.wait_ge(k.dve_done.sem, k.dve_done.at(2))
    for q in range(3):
        s = 1 if q == 1 else 0
        last = nc.tensor.transpose(k.ps[0:ROWS, 512 + HEADS * q:512 + HEADS * (q + 1)],
                                   k.carry_row[:, q, s:s + ROWS], k.ident[0:HEADS, 0:HEADS])
    last.then_inc(k.pe_done.sem, 1)
    pe.wait_ge(k.act_done.sem, k.act_done.at(1))
    for e in range(HEADS):
        for j in range(4):
            at = RL * (4 + e) + P * j
            last = nc.tensor.transpose(k.ps[:, at:at + ROWS], k.s_tmp[e // 2][:, e % 2, P * j:P * (j + 1)],
                                       k.ident[0:ROWS, 0:ROWS])
    last.then_inc(k.pe_done.sem, 1)


def weights_vector(k, dve):
    nc, ch = k.nc, k.dve_step
    src, own, fwd, bwd, tmp = k.s_src, k.s_own, k.s_fwd, k.s_bwd, k.s_tmp
    pairs = [slice(0, 2), slice(2, 4)]
    heads = range(HEADS)
    dve.wait_ge(k.pe_done.sem, k.pe_done.at(1))
    got = k.ps[0:ROWS, :].rearrange("p (e j) -> p e j", j=RL)
    ch(dve, nc.vector.tensor_tensor(src, got[:, 0:HEADS, :], row(k.m_pen[:, :], HEADS), ALU.add))
    ch(dve, nc.vector.tensor_tensor(own, got[:, HEADS:, :], row(k.m_first[:, :], HEADS), ALU.mult))
    for h in heads:
        nc.vector.tensor_tensor_scan(fwd[:, h, :], k.m_reset[:, :], src[:, h, :], -BIG, ALU.add, ALU.max)
        nc.vector.tensor_tensor_scan(bwd[:, h, ::-1], k.m_reset_b[:, ::-1], src[:, h, ::-1], -BIG, ALU.add, ALU.max)
        ch(dve, nc.vector.tensor_tensor_scan(tmp[h // 2][:, h % 2, :], k.m_keep[:, :], own[:, h, :], 0.0, ALU.mult,
                                             ALU.add))
    nc.vector.tensor_copy(k.ends[:, 0, :], fwd[:, :, RL - 1])
    nc.vector.tensor_copy(k.ends[:, 1, :], bwd[:, :, 0])
    for n in range(2):
        ch(dve, nc.vector.tensor_copy(k.ends[:, 2, pairs[n]], tmp[n][:, :, RL - 1]))
    dve.sem_inc(k.dve_done.sem, 1)
    nc.vector.memset(k.carry_row[:, 0, 0:1], -BIG)
    nc.vector.memset(k.carry_row[:, 1, ROWS:ROWS + 1], -BIG)
    ch(dve, nc.vector.memset(k.carry_row[:, 2, 0:1], 0.0))
    dve.wait_ge(k.pe_done.sem, k.pe_done.at(2))
    end = [k.ps[0:HEADS, P * q:P * q + ROWS] for q in range(3)]
    nc.vector.tensor_tensor_scan(k.carry_row[:, 0, 1:ROWS + 1], k.row_mask[:, 0, :], end[0], -BIG, ALU.add, ALU.max)
    nc.vector.tensor_tensor_scan(k.carry_row[:, 1, 0:ROWS][:, ::-1], k.row_mask[:, 1, ::-1], end[1][:, ::-1], -BIG,
                                 ALU.add, ALU.max)
    ch(dve, nc.vector.tensor_tensor_scan(k.carry_row[:, 2, 1:ROWS + 1], k.row_mask[:, 2, :], end[2], 0.0, ALU.mult,
                                         ALU.add))
    dve.sem_inc(k.dve_done.sem, 1)
    dve.wait_ge(k.pe_done.sem, k.pe_done.at(3))
    ch(dve, nc.vector.tensor_copy(k.carry[:, :], k.ps[0:ROWS, 512:512 + 3 * HEADS]))
    for h in heads:
        c = [k.carry[:, HEADS * q + h:HEADS * q + h + 1] for q in range(3)]
        nc.vector.scalar_tensor_tensor(fwd[:, h, :], k.m_seen[:, :], c[0], fwd[:, h, :], ALU.add, ALU.max)
        nc.vector.scalar_tensor_tensor(bwd[:, h, :], k.m_seen_b[:, :], c[1], bwd[:, h, :], ALU.add, ALU.max)
        ch(dve, nc.vector.scalar_tensor_tensor(own[:, h, :], k.m_open[:, :], c[2], tmp[h // 2][:, h % 2, :],
                                               ALU.mult, ALU.add))
    ch(dve, nc.vector.tensor_tensor(fwd, fwd, bwd, ALU.max))
    ch(dve, nc.vector.tensor_tensor(fwd, fwd, own, ALU.add))
    ch(dve, nc.vector.scalar_tensor_tensor(fwd, fwd, 0.2, fwd, ALU.mult, ALU.max))
    for n, pair in enumerate(pairs):
        ch(dve, nc.vector.tensor_tensor(tmp[n], src[:, pair, :], own[:, pair, :], ALU.add))
        ch(dve, nc.vector.scalar_tensor_tensor(tmp[n], tmp[n], 0.2, tmp[n], ALU.mult, ALU.max))
        ch(dve, nc.vector.tensor_tensor(tmp[n], tmp[n], fwd[:, pair, :], ALU.subtract))
    dve.sem_inc(k.dve_done.sem, 1)
    dve.wait_ge(k.pe_done.sem, k.pe_done.at(4))
    back = k.ps[:, RL * 4:].rearrange("p (e j r) -> p e j r", e=HEADS, j=4)
    ch(dve, nc.vector.tensor_copy(k.expo[:, :, :].rearrange("p (r j) e -> p e j r", j=4), back[:, :, :, 0:ROWS]))
    dve.sem_inc(k.dve_done.sem, 1)
    ch(dve, nc.vector.tensor_copy(k.spare, k.expo))
    in_parts = k.share[:, :].rearrange("p (c n e) -> p c n e", n=3, e=HEADS)
    thirds(k, k.spare, [in_parts[:, :, n, :] for n in range(3)], lambda ins: ch(dve, ins))


def scores_in_parts(k):
    nc = k.nc

    def steps(do):
        own = k.scores_own[:, :].rearrange("l (g n e) -> l g n e", n=3, e=HEADS)
        for n, parts in enumerate(([k.scores_src[:, part, :].rearrange("l (g e) -> l g e", e=HEADS)
                                    for part in range(3)], [own[:, :, part, :] for part in range(3)])):
            x = k.small_scores[:, :].rearrange("p (g e) -> p g e", e=HEADS)
            do(nc.vector.tensor_copy(x, k.h[:, :, D + HEADS * n:D + HEADS * (n + 1)]))
            thirds(k, x, parts, do)
    on_vector(k, steps)


def sums(k):
    return k.ps[0:L, 0:ACC].rearrange("p (g f) -> p g f", f=D)


def on_vector(k, steps):
    nc = k.nc
    with nc.Block() as block:
        @block.vector
        def _(dve):
            steps(lambda ins: k.dve_step(dve, ins))


def attention_result(k, i, relu):
    nc = k.nc

    def steps(do):
        do(nc.vector.tensor_reduce(k.r100[:, :].rearrange("p (g e) -> p g e", e=HEADS),
                                   k.ps[0:L, ACC:ACC + G * 3 * HEADS].rearrange("p (g n e) -> p g e n", n=3,
                                                                                e=HEADS), AX.X, ALU.add))
        do(nc.vector.reciprocal(k.r100[:, :], k.r100[:, :]))
        do(nc.vector.tensor_tensor(k.y[:, :, :].rearrange("p g (e c) -> p (g e) c", c=C),
                                   k.ps[0:L, 0:ACC].rearrange("p (a c) -> p a c", c=C), col(k.r100[:, :], C),
                                   ALU.mult))
        do(nc.vector.tensor_tensor(k.y[:, :, :], k.y[:, :, :], row(k.bias[i][0:L, :], G), ALU.add))
        if relu:
            do(nc.vector.tensor_scalar(k.y[:, :, :], k.y[:, :, :], 0.0, None, ALU.max))
    on_vector(k, steps)


def root(k, power, add_in, add_out):
    nc = k.nc
    with nc.Block() as block:
        @block.vector
        def _(dve):
            ch = k.dve_step
            ch(dve, nc.vector.tensor_scalar(k.r25[:, :], k.r25[:, :], power, add_in, ALU.mult, ALU.add))
            dve.sem_inc(k.dve_done.sem, 1)
            dve.wait_ge(k.act_done.sem, k.act_done.at(1))
            if add_out:
                ch(dve, nc.vector.tensor_scalar(k.r25[:, :], k.r25[:, :], add_out, None, ALU.add))
            ch(dve, nc.vector.reciprocal(k.r25[:, :], k.r25[:, :]))

        @block.scalar
        def _(act):
            act.wait_ge(k.dve_done.sem, k.dve_done.at(1))
            nc.scalar.activation(k.r25[:, :], k.r25[:, :], ACT.Sqrt).then_inc(k.act_done.sem, 1)
    k.dve_done.base += 1
    k.act_done.base += 1


def layer_norm(k, x, tmp, out):
    nc = k.nc

    def before(do):
        do(nc.vector.tensor_reduce(k.r25[:, :], x, AX.X, ALU.add))
        do(nc.vector.tensor_scalar(k.r25[:, :], k.r25[:, :], 1.0 / D, None, ALU.mult))
        do(nc.vector.tensor_tensor(x, x, col(k.r25[:, :], D), ALU.subtract))
        do(nc.vector.tensor_tensor(tmp, x, x, ALU.mult))
        do(nc.vector.tensor_reduce(k.r25[:, :], tmp, AX.X, ALU.add))
    on_vector(k, before)
    root(k, 1.0 / D, 1e-5, 0.0)
    on_vector(k, lambda do: do(nc.vector.tensor_tensor(out, x, col(k.r25[:, :], D), ALU.mult)))


def add_and_norm(k, what):
    nc = k.nc
    on_vector(k, lambda do: do(nc.vector.tensor_tensor(k.x[:, :, :], k.x[:, :, :], what, ALU.add)))
    layer_norm(k, k.x[:, :, :], k.z[:, :, :], k.x[:, :, :])


def mean_of_neighbours(k, out):
    nc = k.nc
    on_vector(k, lambda do: do(nc.vector.tensor_tensor(out, sums(k), col(k.degree[:, :], D), ALU.mult)))


def take_degree(k):
    nc = k.nc

    def steps(do):
        do(nc.vector.tensor_scalar(k.degree[:, :], k.ps[0:L, ACC:ACC + G], 1.0, None, ALU.max))
        do(nc.vector.reciprocal(k.degree[:, :], k.degree[:, :]))
    on_vector(k, steps)


def attention_layers(k):
    for i in range(4):
        products(k, k.y, [(k.w_gat[i][:, :], k.h)])
        store_table(k, [(k.table, k.h[:, :, 0:D])])
        scores_in_parts(k)
        attention(k)
        attention_result(k, i, i < 3)


def other_layers(k, out):
    nc = k.nc
    x, y, z, w = (t[:, :, :] for t in (k.x, k.y, k.z, k.w))
    add_and_norm(k, y)

    products(k, k.x, [(k.w_rel[:, 0:512], None), (k.w_rel[:, 512:1024], None), (k.w_self[:, :], k.w)])
    aggregate(k, k.table_rel, k.skind, k.sloc, k.sgroup, KS, True)
    take_degree(k)
    mean_of_neighbours(k, y)
    layer_norm(k, y, z, y)

    def relations(do):
        do(nc.vector.tensor_tensor(y, y, row(k.gamma[0:L, :], G), ALU.mult))
        do(nc.vector.tensor_tensor(y, y, row(k.beta[0:L, :], G), ALU.add))
        do(nc.vector.tensor_tensor(y, y, row(k.bias1[0:L, :], G), ALU.add))
        do(nc.vector.tensor_tensor(y, y, w, ALU.add))
    on_vector(k, relations)
    add_and_norm(k, y)

    store_table(k, [(k.table, x)])
    aggregate(k, k.table, k.sdst, k.sloc, k.sgroup, KS, False)
    mean_of_neighbours(k, y)
    products(k, k.x, [(k.w_l[:, :], k.w)])
    products(k, k.y, [(k.w_r[:, :], k.z)])

    def joined(do):
        do(nc.vector.tensor_tensor(w, w, row(k.bias2[0][0:L, :], G), ALU.add))
        do(nc.vector.tensor_tensor(w, w, z, ALU.add))
        do(nc.vector.tensor_tensor(w, w, row(k.bias2[1][0:L, :], G), ALU.add))
        do(nc.vector.tensor_scalar(w, w, 0.0, None, ALU.max))
        do(nc.vector.tensor_tensor(z, w, w, ALU.mult))
        do(nc.vector.tensor_reduce(k.r25[:, :], z, AX.X, ALU.add))
    on_vector(k, joined)
    root(k, 1.0, 0.0, 1e-6)
    on_vector(k, lambda do: do(nc.vector.tensor_tensor(w, w, col(k.r25[:, :], D), ALU.mult)))
    add_and_norm(k, w)

    store_table(k, [(k.table, x)])
    aggregate(k, k.table, k.tsrc, k.tself, k.tgroup, KD, True)
    take_degree(k)
    mean_of_neighbours(k, y)
    products(k, k.x, [(k.w_cat_t[:, 0, :], k.w)])
    products(k, k.y, [(k.w_cat_t[:, 1, :], k.z)])

    def ended(do):
        do(nc.vector.tensor_tensor(w, w, z, ALU.add))
        do(nc.vector.tensor_tensor(w, w, row(k.bias3[0:L, :], G), ALU.add))
    on_vector(k, ended)
    add_and_norm(k, w)
    store_table(k, [(out, x)])


def gnn_kernel(nc, p, out):
    k = Kit()
    k.nc = nc
    with ExitStack() as ctx:
        def sb(name, shape, dt=F32, c=ctx):
            return c.enter_context(nc.sbuf_tensor(name, shape, dt))

        def signal(name):
            return Signal(ctx.enter_context(nc.semaphore(name)))

        k.loaded, k.stored, k.tabled = signal("loaded"), signal("stored"), signal("tabled")
        k.dve_done, k.pe_done, k.act_done = signal("dve_done"), signal("pe_done"), signal("act_done")
        k.pool_done, k.pool_turn = signal("pool_done"), signal("pool_turn")
        k.act_turn = signal("act_turn")
        k.marks_free, k.marks_ready, k.sums_free = signal("marks_free"), signal("marks_ready"), signal("sums_free")
        k.turned, k.multiplied, k.taken = signal("turned"), signal("multiplied"), signal("taken")
        k.index_ready, k.rows_free = signal("index_ready"), signal("rows_free")
        k.parts_free, k.weighed, k.rounded = signal("parts_free"), signal("weighed"), signal("rounded")
        k.kept_done, k.places_used, k.hot = signal("kept_done"), signal("places_used"), signal("hot")
        k.looked, k.seen, k.look_step = signal("looked"), signal("seen"), signal("look_step")
        k.kept_in = [signal(f"kept_in{h}") for h in range(2)]
        k.places_in = [signal(f"places_in{h}") for h in range(2)]
        k.scattered = [signal(f"scattered{h}") for h in range(2)]
        k.fed = [signal(f"fed{h}") for h in range(RING)]
        k.gathered = [signal(f"gathered{h}") for h in range(RING)]
        k.pool_step = Chain(ctx.enter_context(nc.semaphore("pool_step")))
        k.dve_step = Chain(ctx.enter_context(nc.semaphore("dve_step")))
        k.ps = ctx.enter_context(nc.psum_tensor("ps", [P, 4096], F32))

        k.ones, k.zeros, k.count = sb("ones", [P, 512]), sb("zeros", [P, 512]), sb("count", [P, 512])
        k.ones16, k.count16 = sb("ones16", [P, 1], F16), sb("count16", [P, 512], F16)
        k.ident, k.before, k.before16 = sb("ident", [P, P]), sb("before", [P, P]), sb("before16", [P, P], F16)
        k.small = sb("small", [P, 16])
        k.tself, k.tloc = sb("tself", [P, KD], F16), sb("tloc", [P, KD], F16)
        k.tsrc, k.tgroup = sb("tsrc", [P, KD], I32), sb("tgroup", [P, KD], I32)
        k.sloc, k.sdst, k.skind = sb("sloc", [P, KS], F16), sb("sdst", [P, KS], I32), sb("skind", [P, KS], I32)
        k.sgroup = sb("sgroup", [P, KS], I32)
        k.place_list = nc.dram_tensor("place_list", [KD * P], BF16, kind="Internal").ap()
        k.acc_regs = [nc.tensor.alloc_register(f"to_acc{b}") for b in range(B)]
        k.sum_regs = [nc.tensor.alloc_register(f"to_sum{b}") for b in range(B)]

        constants(k)
        with ExitStack() as sorting:
            k.raw = sb("raw", [LP, 3, CE], I32, sorting)
            k.src, k.dst, k.kind, k.key, k.va, k.vb, k.pos, k.chunk, k.lane, k.tot, k.basis = (
                sb(name, [P, KD], F32, sorting) for name in ("src", "dst", "kind", "key", "va", "vb", "pos", "chunk",
                                                             "lane", "tot", "basis"))
            k.t0, k.t2, k.t3, k.t4, k.t5 = (sb(f"t{i}", [P, KD], F32, sorting) for i in (0, 2, 3, 4, 5))
            k.begin = [sb(f"begin{h}", [P, B, L], F32, sorting) for h in range(2)]
            k.marks = [sb(f"marks{h}", [P, B, L], F16, sorting) for h in range(2)]
            k.picked = [sb(f"picked{h}", [P, B, L], F32, sorting) for h in range(2)]
            k.by_source = nc.dram_tensor("by_source", [P * KS, 2], F32, kind="Internal").ap()
            k.row_of, k.pair = sb("row_of", [LP, CE], I32, sorting), sb("pair", [LP, CE, 2], F32, sorting)
            k.sorted_pair = sb("sorted_pair", [P, KS, 2], F32, sorting)
            k.at_row = [sb(f"at_row{h}", [LP, B], I32, sorting) for h in range(2)]
            k.at_pair = [sb(f"at_pair{h}", [LP, B, 2], F32, sorting) for h in range(2)]
            k.to_lane = [sb(f"to_lane{h}", [P, B, 2, P], F16, sorting) for h in range(2)]
            k.to_chunk = [sb(f"to_chunk{h}", [P, B, KD], F16, sorting) for h in range(2)]
            read_edges(k, p["src"], p["dst"], p["edge_type_8"])
            order_edges(k)

        k.bias = [sb(f"bias_gat{i}", [P, D]) for i in range(4)]
        k.w_gat = [sb(f"w_gat{i}", [P, D + 2 * HEADS]) for i in range(4)]
        k.one16 = sb("one16", [P, 1], BF16)
        k.m_first, k.m_pen, k.m_reset, k.m_keep, k.m_reset_b, k.m_seen, k.m_seen_b, k.m_open = (
            sb(f"m_{name}", [ROWS, RL]) for name in ("first", "pen", "reset", "keep", "reset_b", "seen", "seen_b",
                                                     "open"))
        k.row_mask = sb("row_mask", [HEADS, 3, ROWS])
        k.group_of, k.self_count = sb("group_of", [P, KD]), sb("self_count", [P, 1])
        with ExitStack() as preparing:
            k.w_t, k.a_col = sb("w_t", [P, 4, D], F32, preparing), sb("a_col", [P, 8], F32, preparing)
            k.a_wide, k.own = sb("a_wide", [P, 4, 2, HEADS], F32, preparing), sb("own", [P, HEADS], F32, preparing)
            k.m_last = sb("m_last", [ROWS, RL], F32, preparing)
            k.pen, k.town, k.node_of, k.place_of = (sb(n, [P, KD], F32, preparing) for n in (
                "pen", "town", "node_of", "place_of"))
            k.shift, k.place_row = sb("shift", [P, P], F32, preparing), sb("place_row", [ROWS, RL], BF16, preparing)
            load_attention(k, p)
            prepare_attention(k)
            transposed_lists(k)

        k.y = sb("y", [L, G, D])
        k.r25, k.r100, k.degree = sb("r25", [L, G]), sb("r100", [L, G * HEADS]), sb("degree", [L, G])
        k.index = [sb(f"index{h}", [P, B], I32) for h in range(RING)]
        k.parts = [sb(f"parts{u}", [P, 3, B * D], BF16) for u in range(2)]
        k.member = [sb(f"member{u}", [P, B, L], BF16) for u in range(2)]
        parts = [k.parts[u][:, :, :].rearrange("p n f -> p (n f)") for u in range(2)]
        k.xs = [parts[0].bitcast(F32)[0:L, D * b:D * (b + 1)] for b in range(TILES)]
        k.xt = [parts[1].bitcast(F32)[0:D, D * b:D * b + L] for b in range(TILES)]
        k.places = [parts[u][0:L, 0:B * P] for u in range(2)]
        k.place_hot = [parts[u][0:L, B * P:2 * B * P] for u in range(2)]
        k.group_hot = parts[0][:, 2 * B * P:2 * B * P + B * G].rearrange("p (b g) -> p b g", g=G)

        with ExitStack() as attending:
            k.h = sb("h", [L, G, D + 2 * HEADS], F32, attending)
            k.scores_src = sb("scores_src", [L, 3, G * HEADS], BF16, attending)
            k.scores_own = sb("scores_own", [L, G * 3 * HEADS], BF16, attending)
            k.small_scores = sb("small_scores", [L, G * HEADS], F32, attending)
            k.share = sb("share", [P, KD * 3 * HEADS], BF16, attending)
            k.kept = sb("kept", [P, KEPT * B * D], F32, attending)
            k.rows = [sb(f"rows{h}", [P, B, D], F32, attending) for h in range(SLOTS)]
            k.ends, k.carry = sb("ends", [ROWS, 3, HEADS], F32, attending), sb("carry", [ROWS, 12], F32, attending)
            k.carry_row = sb("carry_row", [HEADS, 3, ROWS + 2], F32, attending)
            both = sb("score", [P, 2 * KD * HEADS], F32, attending)
            k.score_src, k.score_own = (both[:, KD * HEADS * n:KD * HEADS * (n + 1)].rearrange(
                "p (c e) -> p c e", e=HEADS) for n in range(2))
            k.expo, k.spare = k.score_src, k.score_own
            k.candidates = k.share[:, :].bitcast(F32)[
                :, 0:B * G * HEADS].rearrange("p (b x) -> p b x", b=B)
            wide = HEADS * RL

            def rows_of(ap, at, heads):
                return ap[0:ROWS, at:at + heads * RL].rearrange("p (e j) -> p e j", e=heads)

            in_y, in_h = flat(k.y[:, :, :]), flat(k.h[:, :, :])
            k.s_src, k.s_own = rows_of(in_y, 0, HEADS), rows_of(in_h, 0, HEADS)
            k.s_tmp = [rows_of(in_y, wide, 2), rows_of(in_h, wide, 2)]
            k.s_fwd = rows_of(both, 0, HEADS)
            k.s_bwd = rows_of(k.share[:, :].bitcast(F32), 0, HEADS)
            k.table = nc.dram_tensor("table", [N, D], F32, kind="Internal").ap()
            load(k, [(k.y[:, :, :], p["x"].rearrange("(g l) f -> l g f", l=L))])
            attention_layers(k)

        k.x, k.z, k.w = (sb(n, [L, G, D]) for n in ("x", "z", "w"))
        k.rows = [sb(f"rows_of{h}", [P, B, D]) for h in range(RING)]
        k.stage = [[sb(f"stage{b}{j}", [L, 4 * D]) for j in range(2)] for b in range(TILES)]
        k.table_rel = nc.dram_tensor("table_rel", [REL * N, D], F32, kind="Internal").ap()
        k.gamma, k.beta, k.bias1 = sb("gamma", [P, D]), sb("beta", [P, D]), sb("bias_rel", [P, D])
        k.bias2, k.bias3 = [sb("bias_l", [P, D]), sb("bias_r", [P, D])], sb("bias_cat", [P, D])
        k.w_rel, k.w_self = sb("w_rel", [P, REL * D]), sb("w_self", [P, D])
        k.w_l, k.w_r, k.w_cat_t = sb("w_l", [P, D]), sb("w_r", [P, D]), sb("w_cat_t", [P, 2, D])
        k.w_base, k.alpha = sb("w_base", [P, BASES, D]), sb("alpha", [P, REL * BASES])
        k.w_cat = sb("w_cat", [P, 2 * D])
        load_others(k, p)
        prepare_others(k)
        other_layers(k, out)


_INS = ["x", "src", "dst", "edge_type_8"] + [f"L0_gnn_{n}{i}" for i in range(1, 5) for n in ("W", "as", "ad", "b")] + [
    "L1_gnn_weight", "L1_gnn_alpha", "L1_gnn_bias", "L1_gnn_weight_self_loop", "L1_gnn_ln_gamma", "L1_gnn_ln_beta",
    "L2_gnn_Wl", "L2_gnn_bl", "L2_gnn_Wr", "L2_gnn_br", "L3_gnn_W", "L3_gnn_b"]


def kernel(**inputs):
    import numpy as _np
    import concourse.bacc as _bacc
    from concourse import mybir as _mybir
    from concourse.bass_utils import run_bass_kernel_spmd as _run

    nc = _bacc.Bacc("TRN2", target_bir_lowering=False, num_devices=1)
    arrays, p = {}, {}
    for name in _INS:
        a = _np.ascontiguousarray(inputs[name])
        arrays[f"in_{name}_dram"] = a
        p[name] = nc.dram_tensor(f"in_{name}_dram", a.shape, _mybir.dt.from_np(a.dtype), kind="ExternalInput").ap()
    out = nc.dram_tensor("out_0_dram", (N, D), _mybir.dt.float32, kind="ExternalOutput").ap()
    gnn_kernel(nc, p, out)
    r = _run(nc, [arrays], core_ids=[0])
    return r.results[0]["out_0_dram"]
```

```python
import concourse.bass as bass
from concourse import mybir
from contextlib import ExitStack

F32 = mybir.dt.float32
F16 = mybir.dt.float16
BF16 = mybir.dt.bfloat16
I32 = mybir.dt.int32
ALU = mybir.AluOpType
ACT = mybir.ActivationFunctionType
AX = mybir.AxisListType

N = 3125
D = 128
L = 125
G = N // L
E = 50000
P = 128
HEADS, C = 4, 32
REL = 8
BASES = 4
LP = 125
CE = E // LP
B = 8
BODY = 2 * B
RING = 4


def up(n, m):
    return -(-n // m) * m


CIN = up(G + CE, BODY)
ES = E + N
CMID = up(up(ES, P) // P, BODY)
KD = up((ES + G * (P - 1)) // P, RING * B)
KS = up((E + G * (P - 1)) // P, RING * B)
ROWS, RL = KD // 4, 4 * P

ROUND = 12582912.0
HALF = 0.498
MID = float(N // 2)
SELF = 2000.0
BIG = 1e30
ACC = G * D
COLUMNS = ((D, 0), (3 * HEADS, ACC), (1, ACC), (3 * HEADS, 0))
TO_ACC, TO_WEIGHTS, TO_COUNT, TO_SCORES = range(4)
BESIDE = 26
KEPT = 26


class Signal:

    def __init__(self, sem):
        self.sem, self.base = sem, 0

    def at(self, n):
        return self.base + n


class Chain:

    def __init__(self, sem):
        self.sem, self.n = sem, 0

    def __call__(self, eng, ins):
        self.n += 1
        ins.then_inc(self.sem, 1)
        eng.wait_ge(self.sem, self.n)


class Kit:
    pass


def col(ap, n):
    return ap.unsqueeze(2).broadcast_to([ap.shape[0], ap.shape[1], n])


def row(ap, n):
    return ap.unsqueeze(1).broadcast_to([ap.shape[0], n, ap.shape[1]])


def constants(k):
    nc = k.nc
    with nc.Block() as block:
        @block.gpsimd
        def _(pool):
            ch = k.pool_step
            ch(pool, nc.gpsimd.memset(k.ones[:, :], 1.0))
            ch(pool, nc.gpsimd.memset(k.zeros[:, :], 0.0))
            ch(pool, nc.gpsimd.memset(k.ones16[:, :], 1.0))
            ch(pool, nc.gpsimd.iota(k.count[:, :], [[1, 512]], base=0, channel_multiplier=0,
                                    allow_small_or_imprecise_dtypes=True))
            ch(pool, nc.gpsimd.tensor_copy(k.count16[:, :], k.count[:, :]))
            ch(pool, nc.gpsimd.affine_select(out=k.ident[:, :], in_=k.ones[:, 0:P], compare_op=ALU.is_equal,
                                             fill=0.0, base=0, pattern=[[-1, P]], channel_multiplier=1))
            ch(pool, nc.gpsimd.affine_select(out=k.before[:, :], in_=k.ones[:, 0:P], compare_op=ALU.is_gt,
                                             fill=0.0, base=0, pattern=[[1, P]], channel_multiplier=-1))
            ch(pool, nc.gpsimd.tensor_copy(k.before16[:, :], k.before[:, :]))


def split(k, dve, node, group, local, n):
    nc, ch = k.nc, k.dve_step
    ch(dve, nc.vector.tensor_scalar(group, node, 1.0 / L, -0.496, ALU.mult, ALU.add))
    ch(dve, nc.vector.tensor_scalar(group, group, ROUND, -ROUND, ALU.add, ALU.add))
    ch(dve, nc.vector.scalar_tensor_tensor(local, group, -float(L), node, ALU.mult, ALU.add))


def read_edges(k, src, dst, kind):
    nc = k.nc
    with nc.Block() as block:
        @block.sync
        def _(sp):
            sp.dma_start(k.raw[:, 0, :], src.rearrange("(p c) -> p c", p=LP)).then_inc(k.loaded.sem, 16)
            sp.dma_start(k.raw[:, 1, :], dst.rearrange("(p c) -> p c", p=LP)).then_inc(k.loaded.sem, 16)
            sp.dma_start(k.raw[:, 2, :], kind.rearrange("(p c) -> p c", p=LP)).then_inc(k.loaded.sem, 16)
            for n in range(4):
                sp.dma_start(k.by_source.rearrange("(p c) v -> p (c v)", p=P)[:, n * KS // 2:(n + 1) * KS // 2],
                             k.zeros[:, 0:KS].bitcast(F32)).then_inc(k.stored.sem, 16)
            sp.wait_ge(k.stored.sem, k.stored.at(64))

        @block.gpsimd
        def _(pool):
            nc.gpsimd.iota(k.dst[0:LP, 0:G], [[L, G]], base=0, channel_multiplier=1,
                           allow_small_or_imprecise_dtypes=True).then_inc(k.pool_done.sem, 1)

        @block.vector
        def _(dve):
            ch = k.dve_step
            fill = slice(G + CE, CIN)
            real = slice(G, G + CE)
            dve.wait_ge(k.pool_done.sem, k.pool_done.at(1))
            dve.wait_ge(k.loaded.sem, k.loaded.at(48))
            nc.vector.memset(k.dst[0:LP, fill], 0.0)
            nc.vector.tensor_copy(k.dst[0:LP, real], k.raw[:, 1, :])
            nc.vector.tensor_copy(k.src[0:LP, real], k.raw[:, 0, :])
            ch(dve, nc.vector.tensor_copy(k.kind[0:LP, real], k.raw[:, 2, :]))
            out = slice(0, CE)
            split(k, dve, k.src[0:LP, real], k.key[0:LP, out], k.t0[0:LP, out], CE)
            ch(dve, nc.vector.memset(k.key[0:LP, CE:CMID], -1.0))
            ch(dve, nc.vector.scalar_tensor_tensor(k.t0[0:LP, out], k.kind[0:LP, real], 128.0, k.t0[0:LP, out],
                                                   ALU.mult, ALU.add))
            ch(dve, nc.vector.tensor_scalar(k.pair[:, :, 0], k.t0[0:LP, out], 1.0, None, ALU.add))
            ch(dve, nc.vector.tensor_copy(k.pair[:, :, 1], k.dst[0:LP, real]))
    k.loaded.base += 48
    k.stored.base += 64
    k.pool_done.base += 1


def target_keys(k):
    nc = k.nc
    fill = slice(G + CE, CIN)
    real = slice(G, G + CE)
    with nc.Block() as block:
        @block.vector
        def _(dve):
            ch = k.dve_step
            ch(dve, nc.vector.scalar_tensor_tensor(k.t0[0:LP, 0:CE], k.lane[0:LP, 0:CE], float(KS),
                                                   k.chunk[0:LP, 0:CE], ALU.mult, ALU.add))
            ch(dve, nc.vector.tensor_copy(k.row_of[:, :], k.t0[0:LP, 0:CE]))
            split(k, dve, k.dst[0:LP, 0:CIN], k.t0[0:LP, 0:CIN], k.key[0:LP, 0:CIN], CIN)
            ch(dve, nc.vector.memset(k.key[0:LP, fill], -1.0))
            nc.vector.tensor_scalar(k.va[0:LP, 0:CIN], k.dst[0:LP, 0:CIN], MID, None, ALU.subtract)
            nc.vector.tensor_scalar(k.vb[0:LP, real], k.src[0:LP, real], MID, None, ALU.subtract)
            ch(dve, nc.vector.memset(k.vb[0:LP, 0:G], SELF))
            ch(dve, nc.vector.memset(k.va[0:LP, fill], 0.0))
            ch(dve, nc.vector.memset(k.vb[0:LP, fill], 0.0))


def place(k, parts, cols, digits, width, padded, chunks=0, group_row=None):
    nc = k.nc
    turns = cols // (2 * width)
    key, tot, base = k.key, k.tot, k.basis

    def view(tile):
        return tile[:, 0:width * digits].rearrange("p (b d) -> p b d", d=digits)

    picked = [view(x) for x in k.picked]
    begin = [[view(x) for x in tiles] for tiles in k.begin]

    many = digits > P // 2

    def marks(t, h):
        size = width * digits
        where = bass.ds((2 * t + h) * size, size) if many else slice(h * size, (h + 1) * size)
        return k.marks[0:parts, where].rearrange("p (b d) -> p b d", d=digits)

    def one_hots(t, h):
        nc.vector.tensor_tensor(marks(t, h), col(key[0:parts, bass.ds((2 * t + h) * width, width)], digits),
                                row(k.count16[0:parts, 0:digits], width), ALU.is_equal).then_inc(
                                    k.marks_ready.sem, 1)

    with nc.Block() as block:
        @block.vector
        def _(dve):
            with dve.Fori(0, turns) as t:
                for h in range(2):
                    if not many:
                        dve.wait_ge(k.summed.sem, 2 * t + (k.summed.base + h + 1))
                    one_hots(t, h)

        @block.tensor
        def _(pe):
            pe.sem_inc(k.sums_free.sem, 2)
            pe.sem_inc(k.summed.sem, 2)
            with pe.Fori(0, turns) as t:
                for h in range(2):
                    pe.wait_ge(k.sums_free.sem, 2 * t + (k.sums_free.base + h + 1))
                    pe.wait_ge(k.marks_ready.sem, 2 * t + (k.marks_ready.base + h + 1))
                    for b in range(width):
                        last = nc.tensor.matmul(k.ps[0:digits, 512 * h + b:512 * h + b + 1], marks(t, h)[:, b, :],
                                                k.ones16[0:parts, 0:1], start=True, stop=True)
                    last.then_inc(k.summed.sem, 1)

        @block.scalar
        def _(act):
            with act.Fori(0, turns) as t:
                for h in range(2):
                    act.wait_ge(k.summed.sem, 2 * t + (k.summed.base + h + 3))
                    nc.scalar.copy(tot[0:digits, bass.ds((2 * t + h) * width, width)],
                                   k.ps[0:digits, 512 * h:512 * h + width]).then_inc(k.sums_free.sem, 1)
    k.summed.base += 2 + 2 * turns
    k.sums_free.base += 2 + 2 * turns
    k.marks_ready.base += 2 * turns

    with nc.Block() as block:
        @block.vector
        def _(dve):
            ch = k.dve_step
            ch(dve, nc.vector.memset(base[:, 0:cols], 0.0))
            ch(dve, nc.vector.tensor_tensor_scan(k.t0[0:digits, 0:cols], k.ones[0:digits, 0:cols],
                                                 tot[0:digits, 0:cols], 0.0, ALU.mult, ALU.add))
            size = k.small[0:digits, 0:1]
            ch(dve, nc.vector.tensor_copy(size, k.t0[0:digits, cols - 1:cols]))
            if padded:
                ch(dve, nc.vector.tensor_scalar(size, size, 1.0 / P, (P - 1.0) / P - HALF, ALU.mult, ALU.add))
                ch(dve, nc.vector.tensor_scalar(size, size, ROUND, -ROUND, ALU.add, ALU.add))
                ch(dve, nc.vector.tensor_scalar(size, size, float(P), None, ALU.mult))
            dve.sem_inc(k.dve_done.sem, 1)
            dve.wait_ge(k.pe_done.sem, k.pe_done.at(1))
            start = k.small[0:digits, 1:2]
            ch(dve, nc.vector.tensor_copy(start, k.ps[0:digits, 0:1]))
            ch(dve, nc.vector.scalar_tensor_tensor(base[0:digits, 0:cols], k.t0[0:digits, 0:cols], start,
                                                   tot[0:digits, 0:cols], ALU.add, ALU.subtract))
            whole = tot[:, 0:cols]
            ch(dve, nc.vector.tensor_scalar(whole, base[:, 0:cols], 1.0 / P, -HALF, ALU.mult, ALU.add))
            ch(dve, nc.vector.tensor_scalar(whole, whole, ROUND, -ROUND, ALU.add, ALU.add))
            ch(dve, nc.vector.tensor_scalar(whole, whole, float(P), None, ALU.mult))
            ch(dve, nc.vector.tensor_tensor(base[:, 0:cols], base[:, 0:cols], whole, ALU.subtract))
            if padded:
                end = k.small[0:digits, 2:3]
                ch(dve, nc.vector.tensor_tensor(end, start, size, ALU.add))
                ch(dve, nc.vector.tensor_scalar(end, end, 1.0 / P, None, ALU.mult))
                ch(dve, nc.vector.tensor_scalar(k.t0[0:digits, 0:chunks], k.count[0:digits, 0:chunks], end, None,
                                                ALU.is_ge))
                dve.sem_inc(k.dve_done.sem, 1)
                dve.wait_ge(k.pe_done.sem, k.pe_done.at(2))
                ch(dve, nc.vector.tensor_scalar(k.t0[0:1, 0:chunks], k.ps[0:1, 512:512 + chunks], float(G - 1), None,
                                                ALU.min))
                for n, (step, start) in enumerate(COLUMNS):
                    ch(dve, nc.vector.tensor_scalar(group_row[32 * n:32 * n + 1, :], k.t0[0:1, 0:chunks],
                                                    float(step), float(start), ALU.mult, ALU.add))

        @block.tensor
        def _(pe):
            pe.wait_ge(k.dve_done.sem, k.dve_done.at(1))
            nc.tensor.matmul(k.ps[0:digits, 0:1], k.before[0:digits, 0:digits], k.small[0:digits, 0:1],
                             start=True, stop=True).then_inc(k.pe_done.sem, 1)
            if padded:
                pe.wait_ge(k.dve_done.sem, k.dve_done.at(2))
                nc.tensor.matmul(k.ps[0:1, 512:512 + chunks], k.ones[0:digits, 0:1], k.t0[0:digits, 0:chunks],
                                 start=True, stop=True).then_inc(k.pe_done.sem, 1)
    k.dve_done.base += 2 if padded else 1
    k.pe_done.base += 2 if padded else 1

    H = width // 2
    pool_steps = 1 if many else 2

    def ranks(h, n):
        return k.ps[0:parts, 1024 * h + 512 * n:1024 * h + 512 * n + H * digits].rearrange("p (b d) -> p b d", b=H)

    def pick(dve, t, h):
        dve.wait_ge(k.marks_free.sem, 2 * t + (k.marks_free.base + h + 1))
        dve.wait_ge(k.pe_done.sem, 2 * t + (k.pe_done.base + h + 3))
        at = k.ps[0:parts, 1024 * h:1024 * (h + 1)].rearrange("p (n x) -> p n x", n=2)[
            :, :, 0:H * digits].rearrange("p n (b d) -> p n b d", b=H)
        nc.vector.tensor_tensor(
            picked[h][0:parts].rearrange("p (n b) d -> p n b d", n=2), at,
            marks(t, h).rearrange("p (n b) d -> p n b d", n=2), ALU.mult).then_inc(k.dve_done.sem, 1)
        dve.wait_ge(k.dve_done.sem, 2 * t + (k.dve_done.base + h + 3))
        nc.vector.tensor_reduce(k.pos[0:parts, bass.ds((2 * t + h) * width, width)], picked[h][0:parts],
                                AX.X, ALU.add).then_inc(k.marks_free.sem, 1)

    with nc.Block() as block:
        @block.vector
        def _(dve):
            dve.sem_inc(k.marks_free.sem, 2)
            dve.sem_inc(k.dve_done.sem, 2)
            if many:
                with dve.Fori(0, turns) as t:
                    for h in range(2):
                        pick(dve, t, h)
            else:
                one_hots(0, 0)
                with dve.Fori(0, turns - 1) as t:
                    for h in range(2):
                        dve.wait_ge(k.marks_free.sem, 2 * t + (k.marks_free.base + h + 2))
                        one_hots(t + h, 1 - h)
                        pick(dve, t, h)
                dve.wait_ge(k.marks_free.sem, k.marks_free.at(2 * turns))
                one_hots(turns - 1, 1)
                for h in range(2):
                    pick(dve, turns - 1, h)

        @block.gpsimd
        def _(pool):
            with pool.Fori(0, turns) as t:
                for h in range(2):
                    pool.wait_ge(k.pe_done.sem, 2 * t + (k.pe_done.base + h + 1))
                    for n, where in ((0, tot), (1, base))[2 - pool_steps:]:
                        nc.gpsimd.tensor_tensor(begin[h][n], col(where[:, bass.ds((2 * t + h) * width, width)], digits),
                                                row(k.ident[:, 0:digits], width), ALU.mult).then_inc(
                                                    k.pool_done.sem, 1)

        if many:
            @block.scalar
            def _(act):
                with act.Fori(0, turns) as t:
                    for h in range(2):
                        act.wait_ge(k.pe_done.sem, 2 * t + (k.pe_done.base + h + 1))
                        act.sem_inc(k.act_turn.sem, 1)
                        for b in range(width):
                            last = nc.scalar.activation(begin[h][0][:, b, :], k.ident[:, 0:digits], ACT.Copy,
                                                        scale=tot[:, bass.ds((2 * t + h) * width + b, 1)])
                        last.then_inc(k.act_done.sem, 1)

        @block.tensor
        def _(pe):
            pe.sem_inc(k.pe_done.sem, 2)
            with pe.Fori(0, turns) as t:
                for h in range(2):
                    pe.wait_ge(k.dve_done.sem, 2 * t + (k.dve_done.base + h + 1))
                    if not many:
                        pe.wait_ge(k.marks_ready.sem, 2 * t + (k.marks_ready.base + h + 1))
                    pe.wait_ge(k.pool_done.sem, 2 * pool_steps * t + (k.pool_done.base + pool_steps * (h + 1)))
                    if many:
                        pe.wait_ge(k.act_done.sem, 2 * t + (k.act_done.base + h + 1))
                    for n in range(2):
                        half = slice(n * H, (n + 1) * H)
                        nc.tensor.matmul(ranks(h, n), k.before16[0:parts, 0:parts], marks(t, h)[:, half, :],
                                         start=True, stop=False)
                        for m in range(2):
                            last = nc.tensor.matmul(ranks(h, n), k.ones16[:, 0:parts], begin[h][m][:, half, :],
                                                    start=False, stop=(m == 1))
                    last.then_inc(k.pe_done.sem, 1)
    if many:
        k.act_done.base += 2 * turns
    k.marks_free.base += 2 + 2 * turns
    if not many:
        k.marks_ready.base += 2 * turns
    k.pool_done.base += 2 * pool_steps * turns
    k.pe_done.base += 2 + 2 * turns
    k.dve_done.base += 2 + 2 * turns

    with nc.Block() as block:
        @block.vector
        def _(dve):
            ch = k.dve_step
            pos, chunk, lane = (x[0:parts, 0:cols] for x in (k.pos, k.chunk, k.lane))
            ch(dve, nc.vector.tensor_scalar(chunk, pos, 1.0 / P, -HALF, ALU.mult, ALU.add))
            ch(dve, nc.vector.tensor_scalar(chunk, chunk, ROUND, -ROUND, ALU.add, ALU.add))
            ch(dve, nc.vector.scalar_tensor_tensor(lane, chunk, -float(P), pos, ALU.mult, ALU.add))


def permute(k, parts, cols, chunks, out_a, out_b, first, last):
    nc = k.nc
    turns = cols // BODY
    scatters = (last - first) // 2
    with nc.Block() as block:
        @block.scalar
        def _(act):
            def stage(t, h):
                cols = bass.ds((t * 2 + (first + h)) * B, B)
                nc.scalar.copy(k.at_row[h][:, :], k.row_of[:, cols]).then_inc(k.index_ready.sem, 1)
                nc.scalar.copy(k.at_pair[h][:, :, :], k.pair[:, cols, :]).then_inc(k.index_ready.sem, 1)

            for h in range(2):
                stage(0, h)
            with act.Fori(0, scatters - 1) as t:
                for h in range(2):
                    act.wait_ge(k.scattered[h].sem, t * (16 * B) + (k.scattered[h].base + 16 * B))
                    act.sem_inc(k.act_turn.sem, 1)
                    stage(t + 1, h)

        @block.gpsimd
        def _(pool):
            with pool.Fori(0, scatters) as t:
                for h in range(2):
                    pool.wait_ge(k.index_ready.sem, 4 * t + (k.index_ready.base + 2 * h + 2))
                    pool.sem_inc(k.pool_turn.sem, 1)
                    for b in range(B):
                        nc.gpsimd.indirect_dma_start(
                            k.by_source, bass.IndirectOffsetOnAxis(ap=k.at_row[h][:, b:b + 1], axis=0),
                            k.at_pair[h][:, b, :], None).then_inc(k.scattered[h].sem, 16)
            for h in range(2):
                pool.wait_ge(k.scattered[h].sem, k.scattered[h].at(16 * B * scatters))

        @block.vector
        def _(dve):
            dve.sem_inc(k.marks_free.sem, 2)
            with dve.Fori(0, turns) as t:
                for h in range(2):
                    dve.wait_ge(k.marks_free.sem, 2 * t + (k.marks_free.base + h + 1))
                    for b in range(B):
                        i = t * BODY + (h * B + b)
                        lane, chunk = k.lane[0:parts, bass.ds(i, 1)], k.chunk[0:parts, bass.ds(i, 1)]
                        for n, v in enumerate((k.va, k.vb)):
                            nc.vector.tensor_scalar(k.to_lane[h][0:parts, b, n, :], k.count16[0:parts, 0:P], lane,
                                                    v[0:parts, bass.ds(i, 1)], ALU.is_equal, ALU.mult)
                        last = nc.vector.tensor_scalar(k.to_chunk[h][0:parts, b, 0:chunks],
                                                       k.count16[0:parts, 0:chunks], chunk, None, ALU.is_equal)
                    last.then_inc(k.marks_ready.sem, 1)
            dve.wait_ge(k.marks_free.sem, k.marks_free.at(2 + 2 * turns))
            k.dve_step(dve, nc.vector.tensor_copy(out_a, k.ps[:, 0:chunks]))
            k.dve_step(dve, nc.vector.tensor_copy(out_b, k.ps[:, 512:512 + chunks]))

        @block.tensor
        def _(pe):
            for n in range(2):
                nc.tensor.matmul(k.ps[:, 512 * n:512 * n + chunks], k.zeros[:, 0:P], k.zeros[:, 0:chunks],
                                 start=True, stop=False, skip_group_check=True)
            with pe.Fori(0, turns) as t:
                for h in range(2):
                    pe.wait_ge(k.marks_ready.sem, 2 * t + (k.marks_ready.base + h + 1))
                    for b in range(B):
                        for n in range(2):
                            last = nc.tensor.matmul(k.ps[:, 512 * n:512 * n + chunks], k.to_lane[h][0:parts, b, n, :],
                                                    k.to_chunk[h][0:parts, b, 0:chunks],
                                                    start=False, stop=False, skip_group_check=True)
                    last.then_inc(k.marks_free.sem, 1)
    k.marks_free.base += 2 + 2 * turns
    k.marks_ready.base += 2 * turns
    k.index_ready.base += 4 * scatters
    for h in range(2):
        k.scattered[h].base += 16 * B * scatters


def order_edges(k):
    nc = k.nc
    place(k, LP, CMID, G, 26, True, KS, k.sgroup)
    target_keys(k)
    place(k, LP, CIN, L, 8, False)
    permute(k, LP, CIN, CMID, k.va[:, 0:CMID], k.vb[:, 0:CMID], 0, BESIDE)
    with nc.Block() as block:
        @block.gpsimd
        def _(pool):
            nc.gpsimd.affine_select(out=k.t2[:, 0:CMID], in_=k.ones[:, 0:CMID], compare_op=ALU.is_gt, fill=0.0,
                                    base=ES, pattern=[[-P, CMID]],
                                    channel_multiplier=-1).then_inc(k.pool_done.sem, 1)

        @block.vector
        def _(dve):
            ch = k.dve_step
            m = slice(0, CMID)
            node, valid, group, local, own = k.t0[:, m], k.t2[:, m], k.key[:, m], k.t3[:, m], k.t4[:, m]
            ch(dve, nc.vector.tensor_scalar(node, k.va[:, m], MID, None, ALU.add))
            split(k, dve, node, group, local, CMID)
            dve.wait_ge(k.pool_done.sem, k.pool_done.at(1))
            ch(dve, nc.vector.tensor_scalar(own, k.vb[:, m], SELF, None, ALU.is_equal))
            ch(dve, nc.vector.tensor_tensor(k.t5[:, m], k.va[:, m], k.vb[:, m], ALU.subtract))
            ch(dve, nc.vector.tensor_tensor(k.t5[:, m], k.t5[:, m], own, ALU.mult))
            ch(dve, nc.vector.tensor_tensor(k.vb[:, m], k.vb[:, m], k.t5[:, m], ALU.add))
            ch(dve, nc.vector.scalar_tensor_tensor(k.va[:, m], own, 128.0, local, ALU.mult, ALU.add))
            ch(dve, nc.vector.scalar_tensor_tensor(k.va[:, m], k.va[:, m], 1.0, valid, ALU.add, ALU.mult))
            ch(dve, nc.vector.tensor_tensor(k.vb[:, m], k.vb[:, m], valid, ALU.mult))
            ch(dve, nc.vector.scalar_tensor_tensor(group, group, 1.0, valid, ALU.add, ALU.mult))
            ch(dve, nc.vector.tensor_scalar(group, group, -1.0, None, ALU.add))
    k.pool_done.base += 1
    place(k, P, CMID, G, 26, True, KD, k.tgroup)
    permute(k, P, CMID, KD, k.tself[:, :], k.t0[:, 0:KD], BESIDE, CE // B)
    with nc.Block() as block:
        @block.vector
        def _(dve):
            ch = k.dve_step
            ch(dve, nc.vector.tensor_scalar(k.t2[:, 0:KD], k.tself[:, :], 128.0, None, ALU.is_gt))
            ch(dve, nc.vector.scalar_tensor_tensor(k.tloc[:, :], k.t2[:, 0:KD], -128.0, k.tself[:, :],
                                                   ALU.mult, ALU.add))
            ch(dve, nc.vector.tensor_scalar(k.t0[:, 0:KD], k.t0[:, 0:KD], MID, None, ALU.add))
            ch(dve, nc.vector.tensor_copy(k.tsrc[:, :], k.t0[:, 0:KD]))
    with nc.Block() as block:
        @block.sync
        def _(sp):
            sp.dma_start(k.tself_list, k.tself[:, :]).then_inc(k.stored.sem, 16)
            for n in (TO_ACC, TO_COUNT):
                sp.dma_start(k.sgroup_list[n:n + 1, :], k.sgroup[32 * n:32 * n + 1, :]).then_inc(k.stored.sem, 16)
            sp.wait_ge(k.stored.sem, k.stored.at(48))
    k.stored.base += 48


def lists_by_source(k):
    nc = k.nc
    with nc.Block() as block:
        @block.vector
        def _(dve):
            ch = k.dve_step
            m = slice(0, KS)
            place_kind, target = k.sorted_pair[:, :, 0], k.sorted_pair[:, :, 1]
            ch(dve, nc.vector.tensor_scalar(k.kind_of[:, m], place_kind, 1.0 / 128, -HALF, ALU.mult, ALU.add))
            ch(dve, nc.vector.tensor_scalar(k.kind_of[:, m], k.kind_of[:, m], ROUND, -ROUND, ALU.add, ALU.add))
            ch(dve, nc.vector.scalar_tensor_tensor(k.sloc[:, :], k.kind_of[:, m], -128.0, place_kind, ALU.mult, ALU.add))
            ch(dve, nc.vector.tensor_copy(k.sdst[:, :], target))
            ch(dve, nc.vector.scalar_tensor_tensor(k.kind_of[:, m], k.kind_of[:, m], float(N), target, ALU.mult, ALU.add))
            ch(dve, nc.vector.tensor_copy(k.skind[:, :], k.kind_of[:, m]))



def load(k, loads):
    nc = k.nc
    with nc.Block() as block:
        @block.sync
        def _(sp):
            for to, what in loads:
                sp.dma_start(to, what).then_inc(k.loaded.sem, 16)
            sp.wait_ge(k.loaded.sem, k.loaded.at(16 * len(loads)))
    k.loaded.base += 16 * len(loads)


def to_all(pairs):
    return [(dst[:, :], src.unsqueeze(0).broadcast_to([P, D])) for dst, src in pairs]


def load_attention(k, p):
    loads = to_all([(k.bias[i], p[f"L0_gnn_b{i + 1}"]) for i in range(4)])
    loads += [(k.w_gat[i][:, 0:D], p[f"L0_gnn_W{i + 1}"]) for i in range(4)]
    for i in range(4):
        for n, name in enumerate(("as", "ad")):
            loads.append((k.a_col[:, 2 * i + n:2 * i + n + 1],
                          p[f"L0_gnn_{name}{i + 1}"].rearrange("h c -> (h c)").unsqueeze(1)))
    loads.append((k.tself[:, :], k.tself_list))
    load(k, loads)


def load_others(k, p):
    loads = to_all([(k.gamma, p["L1_gnn_ln_gamma"]), (k.beta, p["L1_gnn_ln_beta"]), (k.bias1, p["L1_gnn_bias"]),
                    (k.bias2[0], p["L2_gnn_bl"]), (k.bias2[1], p["L2_gnn_br"]), (k.bias3, p["L3_gnn_b"])])
    loads += [(k.x[:, :, :], p["x"].rearrange("(g l) f -> l g f", l=L)),
              (k.w_base[:, :, :], p["L1_gnn_weight"].rearrange("b i o -> i b o")),
              (k.alpha[:, :], p["L1_gnn_alpha"].rearrange("r b -> (r b)").unsqueeze(0).broadcast_to([P, REL * BASES])),
              (k.w_self[:, :], p["L1_gnn_weight_self_loop"]), (k.w_l[:, :], p["L2_gnn_Wl"]),
              (k.w_r[:, :], p["L2_gnn_Wr"]), (k.w_cat[:, :], p["L3_gnn_W"]),
              (k.tself[:, :], k.tself_list),
              (k.sorted_pair[:, :, :], k.by_source.rearrange("(p c) v -> p c v", p=P))]
    loads += [(k.sgroup[32 * n:32 * n + 1, :], k.sgroup_list[n:n + 1, :]) for n in (TO_ACC, TO_COUNT)]
    load(k, loads)


def prepare_attention(k):
    nc = k.nc
    with nc.Block() as block:
        @block.gpsimd
        def _(pool):
            ch = k.pool_step
            ch(pool, nc.gpsimd.memset(k.ones[:, :], 1.0))
            ch(pool, nc.gpsimd.affine_select(out=k.own[:, :], in_=k.ones[:, 0:HEADS], compare_op=ALU.is_ge, fill=0.0,
                                             base=0, pattern=[[-C, HEADS]], channel_multiplier=1))
            nc.gpsimd.affine_select(out=k.own[:, :], in_=k.own[:, :], compare_op=ALU.is_ge, fill=0.0, base=C - 1,
                                    pattern=[[C, HEADS]], channel_multiplier=-1).then_inc(k.pool_done.sem, 1)

        @block.tensor
        def _(pe):
            for i in range(4):
                last = nc.tensor.transpose(k.ps[:, 512 * i:512 * i + P], k.w_gat[i][:, 0:D], k.ident[:, :])
            last.then_inc(k.pe_done.sem, 1)
            pe.wait_ge(k.dve_done.sem, k.dve_done.at(1))
            for i in range(4):
                last = nc.tensor.matmul(k.ps[:, 512 * i + 256:512 * i + 256 + 2 * HEADS], k.w_t[:, i, :],
                                        k.a_wide[:, i, :, :].rearrange("p n h -> p (n h)"), start=True, stop=True)
            last.then_inc(k.pe_done.sem, 1)

        @block.vector
        def _(dve):
            ch = k.dve_step
            dve.wait_ge(k.pool_done.sem, k.pool_done.at(1))
            for i in range(4):
                for n in range(2):
                    ch(dve, nc.vector.tensor_scalar(k.a_wide[:, i, n, :], k.own[:, :],
                                                    k.a_col[:, 2 * i + n:2 * i + n + 1], None, ALU.mult))
            dve.wait_ge(k.pe_done.sem, k.pe_done.at(1))
            for i in range(4):
                ch(dve, nc.vector.tensor_copy(k.w_t[:, i, :], k.ps[:, 512 * i:512 * i + P]))
            dve.sem_inc(k.dve_done.sem, 1)
            dve.wait_ge(k.pe_done.sem, k.pe_done.at(2))
            for i in range(4):
                ch(dve, nc.vector.tensor_copy(k.w_gat[i][:, D:D + 2 * HEADS],
                                              k.ps[:, 512 * i + 256:512 * i + 256 + 2 * HEADS]))
    k.pool_done.base += 1
    k.pe_done.base += 2
    k.dve_done.base += 1


def prepare_others(k):
    nc = k.nc
    with nc.Block() as block:
        @block.tensor
        def _(pe):
            for n in range(2):
                last = nc.tensor.transpose(k.ps[:, 512 * n:512 * n + P], k.w_cat[:, n * D:(n + 1) * D],
                                           k.ident[:, :])
            last.then_inc(k.pe_done.sem, 1)

        @block.vector
        def _(dve):
            ch = k.dve_step
            for r in range(REL):
                w = k.w_rel[:, r * D:(r + 1) * D]
                for b in range(BASES):
                    a = k.alpha[:, r * BASES + b:r * BASES + b + 1]
                    if b == 0:
                        ch(dve, nc.vector.tensor_scalar(w, k.w_base[:, b, :], a, None, ALU.mult))
                    else:
                        ch(dve, nc.vector.scalar_tensor_tensor(w, k.w_base[:, b, :], a, w, ALU.mult, ALU.add))
            dve.wait_ge(k.pe_done.sem, k.pe_done.at(1))
            for n in range(2):
                ch(dve, nc.vector.tensor_copy(k.w_cat_t[:, n, :], k.ps[:, 512 * n:512 * n + P]))
    k.pe_done.base += 1


def transposed_lists(k):
    nc = k.nc
    first, last, pen = k.m_first, k.m_last, k.m_pen
    with nc.Block() as block:
        @block.sync
        def _(sp):
            sp.wait_ge(k.dve_done.sem, k.dve_done.at(2))
            sp.dma_start(k.place_list.rearrange("(r j) -> r j", j=RL), k.place_row[:, :]).then_inc(k.stored.sem, 16)
            sp.wait_ge(k.stored.sem, k.stored.at(16))

        @block.tensor
        def _(pe):
            pe.wait_ge(k.dve_done.sem, k.dve_done.at(1))
            for n, x in enumerate((k.town, k.pen, k.place_of)):
                v = x[:, :].rearrange("p (r j) -> p j r", j=4)
                for j in range(4):
                    at = 512 * n + P * j
                    done = nc.tensor.transpose(k.ps[0:ROWS, at:at + P], v[:, j, :], k.ident[:, :])
            done.then_inc(k.pe_done.sem, 1)
            pe.wait_ge(k.dve_done.sem, k.dve_done.at(3))
            nc.tensor.matmul(k.ps[0:ROWS, 1536:1537], k.shift[0:ROWS, 0:ROWS], first[:, 0:1], start=True,
                             stop=True).then_inc(k.pe_done.sem, 1)
            pe.wait_ge(k.dve_done.sem, k.dve_done.at(4))
            for n in range(2):
                done = nc.tensor.matmul(k.ps[0:HEADS, 2048 + P * n:2048 + P * n + ROWS],
                                        k.small[0:ROWS, n:n + 1].broadcast_to([ROWS, HEADS]),
                                        k.ident[0:ROWS, 0:ROWS], start=True, stop=True)
            done.then_inc(k.pe_done.sem, 1)

        @block.gpsimd
        def _(pool):
            nc.gpsimd.iota(k.self_count[:, :], [[0, 1]], base=0, channel_multiplier=1,
                           allow_small_or_imprecise_dtypes=True).then_inc(k.pool_done.sem, 1)
            nc.gpsimd.affine_select(out=k.shift[:, :], in_=k.ones[:, 0:P], compare_op=ALU.is_equal, fill=0.0,
                                    base=-1, pattern=[[-1, P]], channel_multiplier=1).then_inc(k.pool_done.sem, 1)

        @block.vector
        def _(dve):
            ch = k.dve_step
            ch(dve, nc.vector.memset(k.one16[:, :], 1.0))
            ch(dve, nc.vector.tensor_scalar(k.pen[:, :], k.tloc[:, :], 0.0, -BIG, ALU.is_equal, ALU.mult))
            ch(dve, nc.vector.tensor_scalar(k.town[:, :], k.tself[:, :], 128.0, None, ALU.is_gt))
            ch(dve, nc.vector.tensor_copy(k.node_of[:, :], k.tsrc[:, :]))
            split(k, dve, k.node_of[:, :], k.its_group[:, :], k.place_of[:, :], KD)
            ch(dve, nc.vector.tensor_copy(k.group_of[:, :], k.its_group[:, :]))
            dve.sem_inc(k.dve_done.sem, 1)
            dve.wait_ge(k.pe_done.sem, k.pe_done.at(1))
            ch(dve, nc.vector.tensor_copy(k.place_row[:, :], k.ps[0:ROWS, 1024:1536]))
            dve.sem_inc(k.dve_done.sem, 1)
            ch(dve, nc.vector.tensor_copy(first[:, :], k.ps[0:ROWS, 0:512]))
            ch(dve, nc.vector.tensor_copy(pen[:, :], k.ps[0:ROWS, 512:1024]))
            dve.wait_ge(k.pool_done.sem, k.pool_done.at(2))
            dve.sem_inc(k.dve_done.sem, 1)
            ch(dve, nc.vector.tensor_copy(last[:, 0:RL - 1], first[:, 1:RL]))
            dve.wait_ge(k.pe_done.sem, k.pe_done.at(2))
            ch(dve, nc.vector.tensor_copy(last[:, RL - 1:RL], k.ps[0:ROWS, 1536:1537]))
            ch(dve, nc.vector.tensor_reduce(k.small[0:ROWS, 0:1], first[:, :], AX.X, ALU.max))
            ch(dve, nc.vector.tensor_reduce(k.small[0:ROWS, 1:2], last[:, :], AX.X, ALU.max))
            dve.sem_inc(k.dve_done.sem, 1)
            ch(dve, nc.vector.tensor_scalar(k.m_reset[:, :], first[:, :], -BIG, None, ALU.mult))
            ch(dve, nc.vector.tensor_scalar(k.m_keep[:, :], first[:, :], -1.0, 1.0, ALU.mult, ALU.add))
            ch(dve, nc.vector.tensor_scalar(k.m_reset_b[:, :], last[:, :], -BIG, None, ALU.mult))
            one = k.ones[0:ROWS, 0:RL]
            ch(dve, nc.vector.tensor_tensor_scan(k.m_seen[:, :], one, first[:, :], 0.0, ALU.mult, ALU.max))
            ch(dve, nc.vector.tensor_tensor_scan(k.m_seen_b[:, ::-1], one, last[:, ::-1], 0.0, ALU.mult, ALU.max))
            ch(dve, nc.vector.tensor_scalar(k.m_open[:, :], k.m_seen[:, :], -1.0, 1.0, ALU.mult, ALU.add))
            ch(dve, nc.vector.tensor_scalar(k.m_seen[:, :], k.m_seen[:, :], -BIG, None, ALU.mult))
            ch(dve, nc.vector.tensor_scalar(k.m_seen_b[:, :], k.m_seen_b[:, :], -BIG, None, ALU.mult))
            dve.wait_ge(k.pe_done.sem, k.pe_done.at(3))
            has = [k.ps[0:HEADS, 2048 + P * n:2048 + P * n + ROWS] for n in range(2)]
            ch(dve, nc.vector.tensor_scalar(k.row_mask[:, 0, :], has[0], -BIG, None, ALU.mult))
            ch(dve, nc.vector.tensor_scalar(k.row_mask[:, 1, :], has[1], -BIG, None, ALU.mult))
            ch(dve, nc.vector.tensor_scalar(k.row_mask[:, 2, :], has[0], -1.0, 1.0, ALU.mult, ALU.add))
    k.stored.base += 16
    k.dve_done.base += 4
    k.pe_done.base += 3
    k.pool_done.base += 2


TILES = 5


def products(k, x, jobs):
    nc = k.nc
    turns, J = G // TILES, len(jobs)
    stores = sum(TILES for _, out in jobs if out is None)
    items = [(b, j) for b in range(TILES) for j in range(J)]

    def turned(b):
        at = 512 * (b // 4) + P * (b % 4)
        return k.ps[:, at:at + L]

    def result(n, width):
        at = 512 * (2 + n % 5)
        return k.ps[0:L, at:at + width]

    with nc.Block() as block:
        @block.scalar
        def _(act):
            with act.Fori(0, turns) as t:
                for b in range(TILES):
                    act.wait_ge(k.turned.sem, TILES * t + (k.turned.base + b + 1))
                    nc.scalar.copy(k.xs[b][:, :], x[:, bass.ds(t * TILES + b, 1), :].rearrange(
                        "p a f -> p (a f)")).then_inc(k.act_done.sem, 1)
                for b in range(TILES):
                    act.wait_ge(k.turned.sem, TILES * t + (k.turned.base + 2 * TILES))
                    act.wait_ge(k.multiplied.sem, TILES * J * t + (k.multiplied.base + J * b + J))
                    nc.scalar.copy(k.xt[b][:, :], turned(b)).then_inc(k.act_done.sem, 1)

        @block.tensor
        def _(pe):
            pe.sem_inc(k.turned.sem, TILES)
            pe.sem_inc(k.multiplied.sem, TILES * J)
            with pe.Fori(0, turns) as t:
                for b in range(TILES):
                    pe.wait_ge(k.act_done.sem, 2 * TILES * t + (k.act_done.base + b + 1))
                    nc.tensor.transpose(turned(b), k.xs[b][:, :], k.ident[0:L, 0:L]).then_inc(k.turned.sem, 1)
                for n, (b, j) in enumerate(items):
                    if j == 0:
                        pe.wait_ge(k.act_done.sem, 2 * TILES * t + (k.act_done.base + TILES + b + 1))
                    pe.wait_ge(k.taken.sem, TILES * J * t + (k.taken.base + n + 1))
                    nc.tensor.matmul(result(n, jobs[j][0].shape[1]), k.xt[b][:, :], jobs[j][0], start=True,
                                     stop=True).then_inc(k.multiplied.sem, 1)

        @block.vector
        def _(dve):
            dve.sem_inc(k.taken.sem, 5)
            if stores:
                dve.sem_inc(k.tabled.sem, 16 * stores)
            with dve.Fori(0, turns) as t:
                if stores:
                    dve.wait_ge(k.tabled.sem, t * (16 * stores) + (k.tabled.base + 16 * stores))
                for n, (b, j) in enumerate(items):
                    rhs, out = jobs[j]
                    width = rhs.shape[1]
                    to = k.stage[b][j][:, :] if out is None else \
                        out[:, bass.ds(t * TILES + b, 1), 0:width].rearrange("p a f -> p (a f)")
                    dve.wait_ge(k.multiplied.sem, TILES * J * t + (k.multiplied.base + TILES * J + n + 1))
                    nc.vector.tensor_copy(to, result(n, width)).then_inc(k.taken.sem, 1)

        if stores:
            @block.sync
            def _(sp):
                table = k.table_rel.rearrange("(r n) f -> n r f", n=N)
                with sp.Fori(0, turns) as t:
                    for n, (b, j) in enumerate(items):
                        if jobs[j][1] is None:
                            sp.wait_ge(k.taken.sem, TILES * J * t + (k.taken.base + 5 + n + 1))
                            sp.dma_start(table[bass.ds((t * TILES + b) * L, L), 4 * j:4 * j + 4, :],
                                         k.stage[b][j][:, :].rearrange("p (r f) -> p r f", r=4)
                                         ).then_inc(k.tabled.sem, 16)
                sp.wait_ge(k.tabled.sem, k.tabled.at(16 * stores * (turns + 1)))
    k.turned.base += TILES * (turns + 1)
    k.multiplied.base += TILES * J * (turns + 1)
    k.act_done.base += 2 * TILES * turns
    k.taken.base += TILES * J * turns + 5
    if stores:
        k.tabled.base += 16 * stores * (turns + 1)


def store_table(k, pairs):
    nc = k.nc
    with nc.Block() as block:
        @block.sync
        def _(sp):
            for to, what in pairs:
                sp.dma_start(to.rearrange("(g l) f -> l g f", l=L), what).then_inc(k.stored.sem, 16)
            sp.wait_ge(k.stored.sem, k.stored.at(16 * len(pairs)))
    k.stored.base += 16 * len(pairs)


def gather(k, pool, table, turns, ring, first):
    nc = k.nc
    with pool.Fori(0, turns) as t:
        for h in range(ring):
            pool.wait_ge(k.index_ready.sem, ring * t + (k.index_ready.base + first + h + 1))
            pool.wait_ge(k.rows_free.sem, ring * t + (k.rows_free.base + h + 1))
            pool.sem_inc(k.pool_turn.sem, 1)
            for b in range(B):
                nc.gpsimd.indirect_dma_start(
                    k.rows[h][:, b, :], None, table,
                    bass.IndirectOffsetOnAxis(ap=k.index[h][:, b:b + 1], axis=0)).then_inc(k.gathered[h].sem, 16)


def flat(ap):
    return ap.rearrange("p b f -> p (b f)")


def thirds(k, x, parts, do):
    nc = k.nc
    do(nc.vector.tensor_copy(parts[0], x))
    do(nc.vector.tensor_tensor(x, x, parts[0], ALU.subtract))
    do(nc.vector.tensor_copy(parts[1], x))
    do(nc.vector.tensor_tensor(parts[2], x, parts[1], ALU.subtract))




class Sweep:

    def __init__(self, k, body, turns, label, group, weigh, count, slots, kept_blocks=0):
        self.k, self.body, self.turns, self.label, self.group = k, body, turns, label, group
        self.weigh, self.count, self.slots, self.kept_blocks = weigh, count, slots, kept_blocks
        self.rings = sum(kind == "ring" for kind, _ in body)
        self.kepts = len(body) - self.rings
        assert self.rings % slots == 0 and len(body) % 2 == 0

    def chunk(self, t, n):
        kind, j = self.body[n]
        if kind == "kept":
            return t * (self.kepts * B) + j * B
        return t * (self.rings * B) + (self.kept_blocks + j) * B

    def rows(self, t, n):
        kind, j = self.body[n]
        if kind == "kept":
            return self.k.kept[:, bass.ds(self.chunk(t, n) * D, B * D)]
        return flat(self.k.rows[j % self.slots][:, :, :])

    def wait_rows(self, eng, t, n):
        kind, j = self.body[n]
        if kind == "ring":
            s = self.k.gathered[j % self.slots]
            per = self.rings // self.slots
            eng.wait_ge(s.sem, t * (16 * B * per) + (s.base + 16 * B * (j // self.slots + 1)))


def sweep_vector(k, dve, s):
    nc, N_ = k.nc, len(s.body)
    with dve.Fori(0, s.turns) as t:
        def last_part(n):
            u = n % 2
            dve.wait_ge(k.rounded.sem, t * (2 * N_) + (k.rounded.base + 2 * n + 2))
            nc.vector.tensor_tensor(k.parts[u][:, 2, :], s.rows(t, n), k.parts[u][:, 1, :],
                                    ALU.subtract).then_inc(k.marks_ready.sem, 1)
            if s.body[n][0] == "ring":
                dve.wait_ge(k.marks_ready.sem, t * N_ + (k.marks_ready.base + n + 1))
                dve.sem_inc(k.rows_free.sem, 1)

        for n in range(N_):
            u = n % 2
            i = s.chunk(t, n)
            s.wait_rows(dve, t, n)
            if s.weigh:
                x = s.rows(t, n).rearrange("p (a c) -> p a c", c=C)
                nc.vector.tensor_tensor(x, x, col(flat(k.expo[:, bass.ds(i, B), :]), C),
                                        ALU.mult).then_inc(k.weighed.sem, 1)
            if n:
                last_part(n - 1)
            dve.wait_ge(k.parts_free.sem, t * N_ + (k.parts_free.base + n + 1))
            nc.vector.tensor_tensor(k.member[u][:, :, :], col(s.label[:, bass.ds(i, B)], L),
                                    row(k.count16[:, 1:L + 1], B), ALU.is_equal)
            dve.wait_ge(k.rounded.sem, t * (2 * N_) + (k.rounded.base + 2 * n + 1))
            x = s.rows(t, n)
            nc.vector.tensor_tensor(x, x, k.parts[u][:, 0, :], ALU.subtract).then_inc(k.weighed.sem, 1)
        last_part(N_ - 1)


def sweep_scalar(k, act, s):
    nc, N_ = k.nc, len(s.body)
    with act.Fori(0, s.turns) as t:
        for n in range(N_):
            for part in range(2):
                if part == 0:
                    act.wait_ge(k.parts_free.sem, t * N_ + (k.parts_free.base + n + 1))
                if part == 0 and not s.weigh:
                    s.wait_rows(act, t, n)
                else:
                    steps = 2 if s.weigh else 1
                    act.wait_ge(k.weighed.sem, t * (steps * N_) + (k.weighed.base + steps * n + part + steps - 1))
                if s.body[n][0] == "kept":
                    act.sem_inc(k.act_turn.sem, 1)
                nc.scalar.copy(k.parts[n % 2][:, part, :], s.rows(t, n)).then_inc(k.rounded.sem, 1)


def sweep_tensor(k, pe, s):
    nc, N_ = k.nc, len(s.body)
    for n in range(7):
        last = nc.tensor.matmul(k.ps[:, 512 * n:512 * (n + 1)], k.zeros[:, 0:P], k.zeros[:, :], start=True,
                                stop=False, skip_group_check=True)
    last.then_inc(k.parts_free.sem, 2)
    with pe.Fori(0, s.turns) as t:
        for n in range(N_):
            u = n % 2
            i = s.chunk(t, n)
            pe.reg_load(k.acc_regs, s.group[0:1, bass.ds(i, B)])
            to_acc = [pe.snap(r, min_val=0, max_val=ACC - D) for r in k.acc_regs]
            if s.weigh or s.count:
                p = 32 * (TO_WEIGHTS if s.weigh else TO_COUNT)
                pe.reg_load(k.sum_regs, s.group[p:p + 1, bass.ds(i, B)])
                to_sum = [pe.snap(r, min_val=ACC, max_val=ACC + (G - 1) * 3 * HEADS) for r in k.sum_regs]
            pe.wait_ge(k.marks_ready.sem, t * N_ + (k.marks_ready.base + n + 1))
            for b in range(B):
                one = k.member[u][:, b, :]
                for part in range(3):
                    last = nc.tensor.matmul(k.ps[0:L, bass.ds(to_acc[b], D)], one,
                                            k.parts[u][:, part, b * D:(b + 1) * D], start=False, stop=False,
                                            skip_group_check=True)
                if s.weigh:
                    last = nc.tensor.matmul(k.ps[0:L, bass.ds(to_sum[b], 3 * HEADS)], one,
                                            k.share[:, bass.ds((i + b) * (3 * HEADS), 3 * HEADS)],
                                            start=False, stop=False, skip_group_check=True)
                if s.count:
                    last = nc.tensor.matmul(k.ps[0:L, bass.ds(to_sum[b], 1)], one, k.one16[:, 0:1],
                                            start=False, stop=False, skip_group_check=True)
            last.then_inc(k.parts_free.sem, 1)


def sweep_over(k, s):
    blocks = len(s.body) * s.turns
    k.parts_free.base += 2 + blocks
    k.marks_ready.base += blocks
    k.weighed.base += (2 if s.weigh else 1) * blocks
    k.rounded.base += 2 * blocks
    for h in range(s.slots):
        k.gathered[h].base += 16 * B * (s.rings * s.turns // s.slots)


def feed_indices(k, sp, index, start, turns, ring):
    def feed(t, h):
        sp.dma_start(k.index[h][:, :], index[:, bass.ds(t * (ring * B) + (start + h * B), B)]).then_inc(
            k.fed[h].sem, 16)
        sp.wait_ge(k.fed[h].sem, 16 * t + (k.fed[h].base + 16))
        sp.sem_inc(k.index_ready.sem, 1)

    for h in range(ring):
        feed(0, h)
    with sp.Fori(0, turns - 1) as t:
        for h in range(ring):
            sp.wait_ge(k.gathered[h].sem, t * (16 * B) + (k.gathered[h].base + 16 * B))
            feed(t + 1, h)
    for h in range(ring):
        k.fed[h].base += 16 * turns


def aggregate(k, table, index, label, group, chunks, count):
    nc = k.nc
    turns = chunks // (RING * B)
    s = Sweep(k, [("ring", h) for h in range(RING)], turns, label, group, False, count, RING)

    with nc.Block() as block:
        @block.sync
        def _(sp):
            sp.sem_inc(k.rows_free.sem, RING)
            feed_indices(k, sp, index, 0, turns, RING)

        @block.gpsimd
        def _(pool):
            gather(k, pool, table, turns, RING, 0)

        @block.scalar
        def _(act):
            sweep_scalar(k, act, s)

        @block.vector
        def _(dve):
            sweep_vector(k, dve, s)

        @block.tensor
        def _(pe):
            sweep_tensor(k, pe, s)
    sweep_over(k, s)
    k.rows_free.base += RING * (turns + 1)
    k.index_ready.base += RING * turns


SLOTS = 3
BODY_OF_ATTENTION = [("ring", n // 2) if n % 2 else ("kept", n // 2) for n in range(26)] + [("ring", 13), ("ring", 14)]


def attention(k):
    nc = k.nc
    turns = 2
    s = Sweep(k, BODY_OF_ATTENTION, turns, k.tloc, k.tgroup, True, False, SLOTS, KEPT)
    assert s.rings * turns + KEPT == KD // B and s.kepts * turns == KEPT
    look = KD // BODY // 2
    blocks = 2 * look

    with nc.Block() as block:
        @block.gpsimd
        def _(pool):
            keep_turns = KEPT // 2
            with pool.Fori(0, keep_turns) as t:
                for h in range(2):
                    pool.wait_ge(k.index_ready.sem, 2 * t + (k.index_ready.base + h + 1))
                    pool.sem_inc(k.pool_turn.sem, 1)
                    for b in range(B):
                        nc.gpsimd.indirect_dma_start(
                            k.rows[h][:, b, :], None, k.table,
                            bass.IndirectOffsetOnAxis(ap=k.index[h][:, b:b + 1], axis=0)).then_inc(
                                k.kept_in[h].sem, 16)
            gather(k, pool, k.table, s.rings * turns // SLOTS, SLOTS, KEPT)

        @block.scalar
        def _(act):
            def indices(t, h):
                nc.scalar.copy(k.index[h][:, :], k.tsrc[:, bass.ds((2 * t + h) * B, B)]).then_inc(
                    k.index_ready.sem, 1)

            def keep(t, h):
                act.wait_ge(k.kept_in[h].sem, t * (16 * B) + (k.kept_in[h].base + 16 * B))
                act.sem_inc(k.act_turn.sem, 1)
                nc.scalar.copy(k.kept[:, bass.ds((2 * t + h) * (B * D), B * D)], flat(k.rows[h][:, :, :])).then_inc(
                    k.kept_done.sem, 1)

            for h in range(2):
                indices(0, h)
            with act.Fori(0, KEPT // 2 - 1) as t:
                for h in range(2):
                    keep(t, h)
                    act.wait_ge(k.kept_done.sem, 2 * t + (k.kept_done.base + h + 1))
                    act.sem_inc(k.act_turn.sem, 1)
                    indices(t + 1, h)
            for h in range(2):
                keep(KEPT // 2 - 1, h)
            act.wait_ge(k.kept_done.sem, k.kept_done.at(KEPT))
            act.sem_inc(k.rows_free.sem, SLOTS)
            act.wait_ge(k.dve_done.sem, k.dve_done.at(3))
            for n in range(2):
                last = nc.scalar.activation(k.s_tmp[n], k.s_tmp[n], ACT.Exp)
            last.then_inc(k.act_done.sem, 1)
            sweep_scalar(k, act, s)

        @block.sync
        def _(sp):
            sp.sem_inc(k.places_used.sem, 2)
            with sp.Fori(0, look) as t:
                for u in range(2):
                    sp.wait_ge(k.places_used.sem, 2 * t + (k.places_used.base + u + 1))
                    sp.dma_start(k.places[u], k.place_list[bass.ds((2 * t + u) * (BODY * P), BODY * P)].unsqueeze(
                        0).broadcast_to([L, BODY * P])).then_inc(k.places_in[u].sem, 16)
            for h in range(2):
                sp.wait_ge(k.kept_in[h].sem, k.kept_in[h].at(16 * B * KEPT // 2))
            feed_indices(k, sp, k.tsrc, KEPT * B, s.rings * turns // SLOTS, SLOTS)

        @block.tensor
        def _(pe):
            lookup_tensor(k, pe, look)
            weights_tensor(k, pe)
            pe.wait_ge(k.dve_done.sem, k.dve_done.at(4))
            sweep_tensor(k, pe, s)

        @block.vector
        def _(dve):
            lookup_vector(k, dve, look)
            weights_vector(k, dve)
            sweep_vector(k, dve, s)
    for h in range(2):
        k.kept_in[h].base += 16 * B * KEPT // 2
        k.places_in[h].base += 16 * look
    k.kept_done.base += KEPT
    k.index_ready.base += KEPT + s.rings * turns
    k.rows_free.base += SLOTS + s.rings * turns
    k.places_used.base += 2 + blocks
    k.hot.base += blocks
    k.looked.base += blocks
    k.seen.base += 2 + blocks
    k.look_step.base += 3 * blocks
    k.pe_done.base += 4
    k.dve_done.base += 4
    k.act_done.base += 1
    sweep_over(k, s)


def lookup_vector(k, dve, look):
    nc = k.nc

    def one_hots(t, u):
        dve.wait_ge(k.places_in[u].sem, 16 * t + (k.places_in[u].base + 16))
        dve.wait_ge(k.seen.sem, 2 * t + (k.seen.base + u + 1))
        nc.vector.tensor_scalar(k.place_hot[u], k.places[u], k.self_count[0:L, 0:1], None,
                                ALU.is_equal).then_inc(k.hot.sem, 1)
        dve.wait_ge(k.hot.sem, 2 * t + (k.hot.base + u + 1))
        dve.sem_inc(k.places_used.sem, 1)

    def pick(t, u):
        chunks = bass.ds((2 * t + u) * BODY, BODY)
        got = k.ps[:, 2048 * u:2048 * (u + 1)].rearrange("p (b e) -> p b e", e=128)
        at = 6 * t + (k.look_step.base + 3 * u)
        nc.vector.tensor_tensor(k.group_hot, col(k.group_of[:, chunks], G), row(k.count16[:, 0:G], BODY),
                                ALU.is_equal).then_inc(k.look_step.sem, 1)
        dve.wait_ge(k.look_step.sem, at + 1)
        dve.wait_ge(k.looked.sem, 2 * t + (k.looked.base + u + 1))
        nc.vector.tensor_tensor(k.candidates.rearrange("p b (g e) -> p b g e", e=HEADS),
                                got[:, :, 0:G * HEADS].rearrange("p b (g e) -> p b g e", e=HEADS),
                                k.group_hot.unsqueeze(3).broadcast_to([P, BODY, G, HEADS]),
                                ALU.mult).then_inc(k.look_step.sem, 1)
        nc.vector.tensor_reduce(k.score_own[:, chunks, :],
                                got[:, :, G * HEADS:G * HEADS + 3 * HEADS].rearrange("p b (n e) -> p b e n", n=3),
                                AX.X, ALU.add).then_inc(k.seen.sem, 1)
        dve.wait_ge(k.look_step.sem, at + 2)
        nc.vector.tensor_reduce(k.score_src[:, chunks, :],
                                k.candidates.rearrange("p b (g e) -> p b e g", e=HEADS), AX.X,
                                ALU.add).then_inc(k.look_step.sem, 1)
        dve.wait_ge(k.look_step.sem, at + 3)

    dve.sem_inc(k.seen.sem, 2)
    one_hots(0, 0)
    with dve.Fori(0, look - 1) as t:
        one_hots(t, 1)
        pick(t, 0)
        one_hots(t + 1, 0)
        pick(t, 1)
    one_hots(look - 1, 1)
    pick(look - 1, 0)
    pick(look - 1, 1)


def lookup_tensor(k, pe, look):
    nc = k.nc
    with pe.Fori(0, look) as t:
        for u in range(2):
            p = 32 * TO_SCORES
            for n, regs in enumerate((k.acc_regs, k.sum_regs)):
                pe.reg_load(regs, k.tgroup[p:p + 1, bass.ds((2 * t + u) * BODY + n * B, B)])
            at = [pe.snap(r, min_val=0, max_val=(G - 1) * 3 * HEADS) for r in k.acc_regs + k.sum_regs]
            pe.wait_ge(k.hot.sem, 2 * t + (k.hot.base + u + 1))
            pe.wait_ge(k.seen.sem, 2 * t + (k.seen.base + u + 1))
            for b in range(BODY):
                hot = k.place_hot[u][:, b * P:(b + 1) * P]
                to = 2048 * u + 128 * b
                for n in range(3):
                    nc.tensor.matmul(k.ps[:, to:to + G * HEADS], hot, k.scores_src[:, n, :], start=(n == 0),
                                     stop=(n == 2))
                last = nc.tensor.matmul(k.ps[:, to + G * HEADS:to + G * HEADS + 3 * HEADS], hot,
                                        k.scores_own[:, bass.ds(at[b], 3 * HEADS)], start=True, stop=True)
            last.then_inc(k.looked.sem, 1)


def weights_tensor(k, pe):
    nc = k.nc
    pe.wait_ge(k.look_step.sem, k.look_step.at(3 * (KD // BODY)))
    pe.wait_ge(k.seen.sem, k.seen.at(2 + KD // BODY))
    for n, x in enumerate((k.score_src, k.score_own)):
        v = x.rearrange("p (r j) e -> p e j r", j=4)
        for e in range(HEADS):
            for j in range(4):
                at = RL * (HEADS * n + e) + P * j
                last = nc.tensor.transpose(k.ps[0:ROWS, at:at + P], v[:, e, j, :], k.ident[:, :])
    last.then_inc(k.pe_done.sem, 1)
    pe.wait_ge(k.dve_done.sem, k.dve_done.at(1))
    for q in range(3):
        last = nc.tensor.transpose(k.ps[0:HEADS, P * q:P * q + ROWS], k.ends[:, q, :], k.ident[0:ROWS, 0:ROWS])
    last.then_inc(k.pe_done.sem, 1)
    pe.wait_ge(k.dve_done.sem, k.dve_done.at(2))
    for q in range(3):
        s = 1 if q == 1 else 0
        last = nc.tensor.transpose(k.ps[0:ROWS, 512 + HEADS * q:512 + HEADS * (q + 1)],
                                   k.carry_row[:, q, s:s + ROWS], k.ident[0:HEADS, 0:HEADS])
    last.then_inc(k.pe_done.sem, 1)
    pe.wait_ge(k.act_done.sem, k.act_done.at(1))
    for e in range(HEADS):
        for j in range(4):
            at = RL * (4 + e) + P * j
            last = nc.tensor.transpose(k.ps[:, at:at + ROWS], k.s_tmp[e // 2][:, e % 2, P * j:P * (j + 1)],
                                       k.ident[0:ROWS, 0:ROWS])
    last.then_inc(k.pe_done.sem, 1)


def weights_vector(k, dve):
    nc, ch = k.nc, k.dve_step
    src, own, fwd, bwd, tmp = k.s_src, k.s_own, k.s_fwd, k.s_bwd, k.s_tmp
    pairs = [slice(0, 2), slice(2, 4)]
    heads = range(HEADS)
    dve.wait_ge(k.pe_done.sem, k.pe_done.at(1))
    got = k.ps[0:ROWS, :].rearrange("p (e j) -> p e j", j=RL)
    ch(dve, nc.vector.tensor_tensor(src, got[:, 0:HEADS, :], row(k.m_pen[:, :], HEADS), ALU.add))
    ch(dve, nc.vector.tensor_tensor(own, got[:, HEADS:, :], row(k.m_first[:, :], HEADS), ALU.mult))
    for h in heads:
        nc.vector.tensor_tensor_scan(fwd[:, h, :], k.m_reset[:, :], src[:, h, :], -BIG, ALU.add, ALU.max)
        nc.vector.tensor_tensor_scan(bwd[:, h, ::-1], k.m_reset_b[:, ::-1], src[:, h, ::-1], -BIG, ALU.add, ALU.max)
        ch(dve, nc.vector.tensor_tensor_scan(tmp[h // 2][:, h % 2, :], k.m_keep[:, :], own[:, h, :], 0.0, ALU.mult,
                                             ALU.add))
    nc.vector.tensor_copy(k.ends[:, 0, :], fwd[:, :, RL - 1])
    nc.vector.tensor_copy(k.ends[:, 1, :], bwd[:, :, 0])
    for n in range(2):
        ch(dve, nc.vector.tensor_copy(k.ends[:, 2, pairs[n]], tmp[n][:, :, RL - 1]))
    dve.sem_inc(k.dve_done.sem, 1)
    nc.vector.memset(k.carry_row[:, 0, 0:1], -BIG)
    nc.vector.memset(k.carry_row[:, 1, ROWS:ROWS + 1], -BIG)
    ch(dve, nc.vector.memset(k.carry_row[:, 2, 0:1], 0.0))
    dve.wait_ge(k.pe_done.sem, k.pe_done.at(2))
    end = [k.ps[0:HEADS, P * q:P * q + ROWS] for q in range(3)]
    nc.vector.tensor_tensor_scan(k.carry_row[:, 0, 1:ROWS + 1], k.row_mask[:, 0, :], end[0], -BIG, ALU.add, ALU.max)
    nc.vector.tensor_tensor_scan(k.carry_row[:, 1, 0:ROWS][:, ::-1], k.row_mask[:, 1, ::-1], end[1][:, ::-1], -BIG,
                                 ALU.add, ALU.max)
    ch(dve, nc.vector.tensor_tensor_scan(k.carry_row[:, 2, 1:ROWS + 1], k.row_mask[:, 2, :], end[2], 0.0, ALU.mult,
                                         ALU.add))
    dve.sem_inc(k.dve_done.sem, 1)
    dve.wait_ge(k.pe_done.sem, k.pe_done.at(3))
    ch(dve, nc.vector.tensor_copy(k.carry[:, :], k.ps[0:ROWS, 512:512 + 3 * HEADS]))
    for h in heads:
        c = [k.carry[:, HEADS * q + h:HEADS * q + h + 1] for q in range(3)]
        nc.vector.scalar_tensor_tensor(fwd[:, h, :], k.m_seen[:, :], c[0], fwd[:, h, :], ALU.add, ALU.max)
        nc.vector.scalar_tensor_tensor(bwd[:, h, :], k.m_seen_b[:, :], c[1], bwd[:, h, :], ALU.add, ALU.max)
        ch(dve, nc.vector.scalar_tensor_tensor(own[:, h, :], k.m_open[:, :], c[2], tmp[h // 2][:, h % 2, :],
                                               ALU.mult, ALU.add))
    ch(dve, nc.vector.tensor_tensor(fwd, fwd, bwd, ALU.max))
    ch(dve, nc.vector.tensor_tensor(fwd, fwd, own, ALU.add))
    ch(dve, nc.vector.scalar_tensor_tensor(fwd, fwd, 0.2, fwd, ALU.mult, ALU.max))
    for n, pair in enumerate(pairs):
        ch(dve, nc.vector.tensor_tensor(tmp[n], src[:, pair, :], own[:, pair, :], ALU.add))
        ch(dve, nc.vector.scalar_tensor_tensor(tmp[n], tmp[n], 0.2, tmp[n], ALU.mult, ALU.max))
        ch(dve, nc.vector.tensor_tensor(tmp[n], tmp[n], fwd[:, pair, :], ALU.subtract))
    dve.sem_inc(k.dve_done.sem, 1)
    dve.wait_ge(k.pe_done.sem, k.pe_done.at(4))
    back = k.ps[:, RL * 4:].rearrange("p (e j r) -> p e j r", e=HEADS, j=4)
    ch(dve, nc.vector.tensor_copy(k.expo[:, :, :].rearrange("p (r j) e -> p e j r", j=4), back[:, :, :, 0:ROWS]))
    dve.sem_inc(k.dve_done.sem, 1)
    ch(dve, nc.vector.tensor_copy(k.spare, k.expo))
    in_parts = k.share[:, :].rearrange("p (c n e) -> p c n e", n=3, e=HEADS)
    thirds(k, k.spare, [in_parts[:, :, n, :] for n in range(3)], lambda ins: ch(dve, ins))


def scores_in_parts(k):
    nc = k.nc

    def steps(do):
        own = k.scores_own[:, :].rearrange("l (g n e) -> l g n e", n=3, e=HEADS)
        for n, parts in enumerate(([k.scores_src[:, part, :].rearrange("l (g e) -> l g e", e=HEADS)
                                    for part in range(3)], [own[:, :, part, :] for part in range(3)])):
            x = k.small_scores[:, :].rearrange("p (g e) -> p g e", e=HEADS)
            do(nc.vector.tensor_copy(x, k.h[:, :, D + HEADS * n:D + HEADS * (n + 1)]))
            thirds(k, x, parts, do)
    on_vector(k, steps)


def sums(k):
    return k.ps[0:L, 0:ACC].rearrange("p (g f) -> p g f", f=D)


def on_vector(k, steps):
    nc = k.nc
    with nc.Block() as block:
        @block.vector
        def _(dve):
            steps(lambda ins: k.dve_step(dve, ins))


def attention_result(k, i, relu):
    nc = k.nc

    def steps(do):
        do(nc.vector.tensor_reduce(k.r100[:, :].rearrange("p (g e) -> p g e", e=HEADS),
                                   k.ps[0:L, ACC:ACC + G * 3 * HEADS].rearrange("p (g n e) -> p g e n", n=3,
                                                                                e=HEADS), AX.X, ALU.add))
        do(nc.vector.reciprocal(k.r100[:, :], k.r100[:, :]))
        do(nc.vector.tensor_tensor(k.y[:, :, :].rearrange("p g (e c) -> p (g e) c", c=C),
                                   k.ps[0:L, 0:ACC].rearrange("p (a c) -> p a c", c=C), col(k.r100[:, :], C),
                                   ALU.mult))
        do(nc.vector.tensor_tensor(k.y[:, :, :], k.y[:, :, :], row(k.bias[i][0:L, :], G), ALU.add))
        if relu:
            do(nc.vector.tensor_scalar(k.y[:, :, :], k.y[:, :, :], 0.0, None, ALU.max))
    on_vector(k, steps)


def root(k, power, add_in, add_out):
    nc = k.nc
    with nc.Block() as block:
        @block.vector
        def _(dve):
            ch = k.dve_step
            ch(dve, nc.vector.tensor_scalar(k.r25[:, :], k.r25[:, :], power, add_in, ALU.mult, ALU.add))
            dve.sem_inc(k.dve_done.sem, 1)
            dve.wait_ge(k.act_done.sem, k.act_done.at(1))
            if add_out:
                ch(dve, nc.vector.tensor_scalar(k.r25[:, :], k.r25[:, :], add_out, None, ALU.add))
            ch(dve, nc.vector.reciprocal(k.r25[:, :], k.r25[:, :]))

        @block.scalar
        def _(act):
            act.wait_ge(k.dve_done.sem, k.dve_done.at(1))
            nc.scalar.activation(k.r25[:, :], k.r25[:, :], ACT.Sqrt).then_inc(k.act_done.sem, 1)
    k.dve_done.base += 1
    k.act_done.base += 1


def layer_norm(k, x, tmp, out):
    nc = k.nc

    def before(do):
        do(nc.vector.tensor_reduce(k.r25[:, :], x, AX.X, ALU.add))
        do(nc.vector.tensor_scalar(k.r25[:, :], k.r25[:, :], 1.0 / D, None, ALU.mult))
        do(nc.vector.tensor_tensor(x, x, col(k.r25[:, :], D), ALU.subtract))
        do(nc.vector.tensor_tensor(tmp, x, x, ALU.mult))
        do(nc.vector.tensor_reduce(k.r25[:, :], tmp, AX.X, ALU.add))
    on_vector(k, before)
    root(k, 1.0 / D, 1e-5, 0.0)
    on_vector(k, lambda do: do(nc.vector.tensor_tensor(out, x, col(k.r25[:, :], D), ALU.mult)))


def add_and_norm(k, what):
    nc = k.nc
    on_vector(k, lambda do: do(nc.vector.tensor_tensor(k.x[:, :, :], k.x[:, :, :], what, ALU.add)))
    layer_norm(k, k.x[:, :, :], k.z[:, :, :], k.x[:, :, :])


def mean_of_neighbours(k, out):
    nc = k.nc
    on_vector(k, lambda do: do(nc.vector.tensor_tensor(out, sums(k), col(k.degree[:, :], D), ALU.mult)))


def take_degree(k):
    nc = k.nc

    def steps(do):
        do(nc.vector.tensor_scalar(k.degree[:, :], k.ps[0:L, ACC:ACC + G], 1.0, None, ALU.max))
        do(nc.vector.reciprocal(k.degree[:, :], k.degree[:, :]))
    on_vector(k, steps)


def attention_layers(k):
    for i in range(4):
        products(k, k.y, [(k.w_gat[i][:, :], k.h)])
        store_table(k, [(k.table, k.h[:, :, 0:D])])
        scores_in_parts(k)
        attention(k)
        attention_result(k, i, i < 3)


def other_layers(k, out):
    nc = k.nc
    x, y, z, w = (t[:, :, :] for t in (k.x, k.y, k.z, k.w))
    add_and_norm(k, y)

    products(k, k.x, [(k.w_rel[:, 0:512], None), (k.w_rel[:, 512:1024], None), (k.w_self[:, :], k.w)])
    aggregate(k, k.table_rel, k.skind, k.sloc, k.sgroup, KS, True)
    take_degree(k)
    mean_of_neighbours(k, y)
    layer_norm(k, y, z, y)

    def relations(do):
        do(nc.vector.tensor_tensor(y, y, row(k.gamma[0:L, :], G), ALU.mult))
        do(nc.vector.tensor_tensor(y, y, row(k.beta[0:L, :], G), ALU.add))
        do(nc.vector.tensor_tensor(y, y, row(k.bias1[0:L, :], G), ALU.add))
        do(nc.vector.tensor_tensor(y, y, w, ALU.add))
    on_vector(k, relations)
    add_and_norm(k, y)

    store_table(k, [(k.table, x)])
    aggregate(k, k.table, k.sdst, k.sloc, k.sgroup, KS, False)
    mean_of_neighbours(k, y)
    products(k, k.x, [(k.w_l[:, :], k.w)])
    products(k, k.y, [(k.w_r[:, :], k.z)])

    def joined(do):
        do(nc.vector.tensor_tensor(w, w, row(k.bias2[0][0:L, :], G), ALU.add))
        do(nc.vector.tensor_tensor(w, w, z, ALU.add))
        do(nc.vector.tensor_tensor(w, w, row(k.bias2[1][0:L, :], G), ALU.add))
        do(nc.vector.tensor_scalar(w, w, 0.0, None, ALU.max))
        do(nc.vector.tensor_tensor(z, w, w, ALU.mult))
        do(nc.vector.tensor_reduce(k.r25[:, :], z, AX.X, ALU.add))
    on_vector(k, joined)
    root(k, 1.0, 0.0, 1e-6)
    on_vector(k, lambda do: do(nc.vector.tensor_tensor(w, w, col(k.r25[:, :], D), ALU.mult)))
    add_and_norm(k, w)

    store_table(k, [(k.table, x)])
    aggregate(k, k.table, k.tsrc, k.tself, k.tgroup, KD, True)
    take_degree(k)
    mean_of_neighbours(k, y)
    products(k, k.x, [(k.w_cat_t[:, 0, :], k.w)])
    products(k, k.y, [(k.w_cat_t[:, 1, :], k.z)])

    def ended(do):
        do(nc.vector.tensor_tensor(w, w, z, ALU.add))
        do(nc.vector.tensor_tensor(w, w, row(k.bias3[0:L, :], G), ALU.add))
    on_vector(k, ended)
    add_and_norm(k, w)
    store_table(k, [(out, x)])


def gnn_kernel(nc, p, out):
    k = Kit()
    k.nc = nc
    with ExitStack() as ctx:
        def sb(name, shape, dt=F32, c=ctx):
            return c.enter_context(nc.sbuf_tensor(name, shape, dt))

        def signal(name):
            return Signal(ctx.enter_context(nc.semaphore(name)))

        k.loaded, k.stored, k.tabled = signal("loaded"), signal("stored"), signal("tabled")
        k.dve_done, k.pe_done, k.act_done = signal("dve_done"), signal("pe_done"), signal("act_done")
        k.pool_done, k.pool_turn = signal("pool_done"), signal("pool_turn")
        k.act_turn = signal("act_turn")
        k.marks_free, k.marks_ready, k.sums_free = signal("marks_free"), signal("marks_ready"), signal("sums_free")
        k.turned, k.multiplied, k.taken = signal("turned"), signal("multiplied"), signal("taken")
        k.index_ready, k.rows_free = signal("index_ready"), signal("rows_free")
        k.parts_free, k.weighed, k.rounded = signal("parts_free"), signal("weighed"), signal("rounded")
        k.kept_done, k.places_used, k.hot = signal("kept_done"), signal("places_used"), signal("hot")
        k.looked, k.seen, k.look_step = signal("looked"), signal("seen"), signal("look_step")
        k.kept_in = [signal(f"kept_in{h}") for h in range(2)]
        k.places_in = [signal(f"places_in{h}") for h in range(2)]
        k.summed = signal("summed")
        k.scattered = [signal(f"scattered{h}") for h in range(2)]
        k.fed = [signal(f"fed{h}") for h in range(RING)]
        k.gathered = [signal(f"gathered{h}") for h in range(RING)]
        k.pool_step = Chain(ctx.enter_context(nc.semaphore("pool_step")))
        k.dve_step = Chain(ctx.enter_context(nc.semaphore("dve_step")))
        k.ps = ctx.enter_context(nc.psum_tensor("ps", [P, 4096], F32))

        k.zeros, k.count16, k.ident = sb("zeros", [P, 512], BF16), sb("count16", [P, 512], F16), sb("ident", [P, P])
        k.small = sb("small", [P, 16])
        k.tloc = sb("tloc", [P, KD], F16)
        k.tsrc, k.tgroup = sb("tsrc", [P, KD], I32), sb("tgroup", [P, KD], I32)
        k.tself_list = nc.dram_tensor("tself_list", [P, KD], F16, kind="Internal").ap()
        k.sgroup_list = nc.dram_tensor("sgroup_list", [len(COLUMNS), KS], I32, kind="Internal").ap()
        k.by_source = nc.dram_tensor("by_source", [P * KS, 2], F32, kind="Internal").ap()
        k.place_list = nc.dram_tensor("place_list", [KD * P], BF16, kind="Internal").ap()
        k.acc_regs = [nc.tensor.alloc_register(f"to_acc{b}") for b in range(B)]
        k.sum_regs = [nc.tensor.alloc_register(f"to_sum{b}") for b in range(B)]

        with ExitStack() as sorting:
            k.ones, k.count = sb("ones", [P, 512], F32, sorting), sb("count", [P, 512], F32, sorting)
            k.ones16 = sb("ones16", [P, P], F16, sorting)
            k.before, k.before16 = sb("before", [P, P], F32, sorting), sb("before16", [P, P], F16, sorting)
            k.tself, k.sgroup = sb("tself", [P, KD], F16, sorting), sb("sgroup", [P, KS], I32, sorting)
            constants(k)
            k.raw = sb("raw", [LP, 3, CE], I32, sorting)
            k.src, k.dst, k.kind, k.key, k.va, k.vb, k.pos, k.chunk, k.lane, k.tot, k.basis = (
                sb(name, [P, KD], F32, sorting) for name in ("src", "dst", "kind", "key", "va", "vb", "pos", "chunk",
                                                             "lane", "tot", "basis"))
            k.t0, k.t2, k.t3, k.t4, k.t5 = (sb(f"t{i}", [P, KD], F32, sorting) for i in (0, 2, 3, 4, 5))
            k.begin = [[sb(f"begin{h}{n}", [P, B * L], F16, sorting) for n in range(2)] for h in range(2)]
            k.marks = sb("marks", [P, CIN * L], F16, sorting)
            k.picked = [sb(f"picked{h}", [P, B * L], F32, sorting) for h in range(2)]
            k.row_of, k.pair = sb("row_of", [LP, CE], I32, sorting), sb("pair", [LP, CE, 2], F32, sorting)
            k.at_row = [sb(f"at_row{h}", [LP, B], I32, sorting) for h in range(2)]
            k.at_pair = [sb(f"at_pair{h}", [LP, B, 2], F32, sorting) for h in range(2)]
            k.to_lane = [sb(f"to_lane{h}", [P, B, 2, P], F16, sorting) for h in range(2)]
            k.to_chunk = [sb(f"to_chunk{h}", [P, B, KD], F16, sorting) for h in range(2)]
            read_edges(k, p["src"], p["dst"], p["edge_type_8"])
            order_edges(k)

        k.bias = [sb(f"bias_gat{i}", [P, D]) for i in range(4)]
        k.w_gat = [sb(f"w_gat{i}", [P, D + 2 * HEADS]) for i in range(4)]
        k.one16 = sb("one16", [P, 1], BF16)
        k.m_first, k.m_pen, k.m_reset, k.m_keep, k.m_reset_b, k.m_seen, k.m_seen_b, k.m_open = (
            sb(f"m_{name}", [ROWS, RL], BF16) for name in ("first", "pen", "reset", "keep", "reset_b", "seen", "seen_b",
                                                     "open"))
        k.row_mask = sb("row_mask", [HEADS, 3, ROWS])
        k.group_of, k.self_count = sb("group_of", [P, KD], F16), sb("self_count", [P, 1])
        with ExitStack() as preparing:
            k.w_t, k.a_col = sb("w_t", [P, 4, D], F32, preparing), sb("a_col", [P, 8], F32, preparing)
            k.a_wide, k.own = sb("a_wide", [P, 4, 2, HEADS], F32, preparing), sb("own", [P, HEADS], F32, preparing)
            k.m_last = sb("m_last", [ROWS, RL], BF16, preparing)
            k.ones, k.tself = sb("ones_again", [P, RL], F32, preparing), sb("tself_again", [P, KD], F16, preparing)
            k.pen, k.town, k.node_of, k.place_of, k.its_group = (sb(n, [P, KD], F32, preparing) for n in (
                "pen", "town", "node_of", "place_of", "its_group"))
            k.shift, k.place_row = sb("shift", [P, P], BF16, preparing), sb("place_row", [ROWS, RL], BF16, preparing)
            load_attention(k, p)
            prepare_attention(k)
            transposed_lists(k)

        k.y = sb("y", [L, G, D])
        k.r25, k.r100, k.degree = sb("r25", [L, G]), sb("r100", [L, G * HEADS]), sb("degree", [L, G])
        k.index = [sb(f"index{h}", [P, B], I32) for h in range(RING)]
        k.parts = [sb(f"parts{u}", [P, 3, B * D], BF16) for u in range(2)]
        k.member = [sb(f"member{u}", [P, B, L], BF16) for u in range(2)]
        parts = [k.parts[u][:, :, :].rearrange("p n f -> p (n f)") for u in range(2)]
        k.xs = [parts[0].bitcast(F32)[0:L, D * b:D * (b + 1)] for b in range(TILES)]
        k.xt = [parts[1].bitcast(F32)[0:D, D * b:D * b + L] for b in range(TILES)]

        with ExitStack() as attending:
            k.h = sb("h", [L, G, D + 2 * HEADS], F32, attending)
            k.scores_src = sb("scores_src", [L, 3, G * HEADS], BF16, attending)
            k.scores_own = sb("scores_own", [L, G * 3 * HEADS], BF16, attending)
            k.small_scores = sb("small_scores", [L, G * HEADS], F32, attending)
            k.share = sb("share", [P, KD * 3 * HEADS], BF16, attending)
            k.kept = sb("kept", [P, KEPT * B * D], F32, attending)
            k.rows = [sb(f"rows{h}", [P, B, D], F32, attending) for h in range(SLOTS)]
            k.ends, k.carry = sb("ends", [ROWS, 3, HEADS], F32, attending), sb("carry", [ROWS, 12], F32, attending)
            k.carry_row = sb("carry_row", [HEADS, 3, ROWS + 2], F32, attending)
            both = sb("score", [P, 2 * KD * HEADS], F32, attending)
            k.score_src, k.score_own = (both[:, KD * HEADS * n:KD * HEADS * (n + 1)].rearrange(
                "p (c e) -> p c e", e=HEADS) for n in range(2))
            k.expo, k.spare = k.score_src, k.score_own
            k.candidates = k.share[:, :].bitcast(F32)[
                :, 0:BODY * G * HEADS].rearrange("p (b x) -> p b x", b=BODY)
            k.group_hot = parts[0][:, 0:BODY * G].rearrange("p (b g) -> p b g", g=G)
            k.places, k.place_hot = ([flat(x[:, :, :]).bitcast(BF16)[:, u * BODY * P:(u + 1) * BODY * P]
                                      for u in range(2)] for x in (k.h, k.y))
            wide = HEADS * RL

            def rows_of(ap, at, heads):
                return ap[0:ROWS, at:at + heads * RL].rearrange("p (e j) -> p e j", e=heads)

            in_y, in_h = flat(k.y[:, :, :]), flat(k.h[:, :, :])
            k.s_src, k.s_own = rows_of(in_y, 0, HEADS), rows_of(in_h, 0, HEADS)
            k.s_tmp = [rows_of(in_y, wide, 2), rows_of(in_h, wide, 2)]
            k.s_fwd = rows_of(both, 0, HEADS)
            k.s_bwd = rows_of(k.share[:, :].bitcast(F32), 0, HEADS)
            k.table = nc.dram_tensor("table", [N, D], F32, kind="Internal").ap()
            load(k, [(k.y[:, :, :], p["x"].rearrange("(g l) f -> l g f", l=L))])
            attention_layers(k)

        k.x, k.z, k.w = (sb(n, [L, G, D]) for n in ("x", "z", "w"))
        k.rows = [sb(f"rows_of{h}", [P, B, D]) for h in range(RING)]
        k.stage = [[sb(f"stage{b}{j}", [L, 4 * D]) for j in range(2)] for b in range(TILES)]
        k.table_rel = nc.dram_tensor("table_rel", [REL * N, D], F32, kind="Internal").ap()
        k.gamma, k.beta, k.bias1 = sb("gamma", [P, D]), sb("beta", [P, D]), sb("bias_rel", [P, D])
        k.bias2, k.bias3 = [sb("bias_l", [P, D]), sb("bias_r", [P, D])], sb("bias_cat", [P, D])
        k.w_rel, k.w_self = sb("w_rel", [P, REL * D]), sb("w_self", [P, D])
        k.w_l, k.w_r, k.w_cat_t = sb("w_l", [P, D]), sb("w_r", [P, D]), sb("w_cat_t", [P, 2, D])
        k.w_base, k.alpha = sb("w_base", [P, BASES, D]), sb("alpha", [P, REL * BASES])
        k.w_cat = sb("w_cat", [P, 2 * D])
        k.tself, k.sgroup = sb("tself_last", [P, KD], F16), sb("sgroup_last", [P, KS], I32)
        k.sloc, k.sdst, k.skind = sb("sloc", [P, KS], F16), sb("sdst", [P, KS], I32), sb("skind", [P, KS], I32)
        k.sorted_pair, k.kind_of = sb("sorted_pair", [P, KS, 2]), sb("kind_of", [P, KS])
        load_others(k, p)
        lists_by_source(k)
        prepare_others(k)
        other_layers(k, out)


_INS = ["x", "src", "dst", "edge_type_8"] + [f"L0_gnn_{n}{i}" for i in range(1, 5) for n in ("W", "as", "ad", "b")] + [
    "L1_gnn_weight", "L1_gnn_alpha", "L1_gnn_bias", "L1_gnn_weight_self_loop", "L1_gnn_ln_gamma", "L1_gnn_ln_beta",
    "L2_gnn_Wl", "L2_gnn_bl", "L2_gnn_Wr", "L2_gnn_br", "L3_gnn_W", "L3_gnn_b"]


def kernel(**inputs):
    import numpy as _np
    import concourse.bacc as _bacc
    from concourse import mybir as _mybir
    from concourse.bass_utils import run_bass_kernel_spmd as _run

    nc = _bacc.Bacc("TRN2", target_bir_lowering=False, num_devices=1)
    arrays, p = {}, {}
    for name in _INS:
        a = _np.ascontiguousarray(inputs[name])
        arrays[f"in_{name}_dram"] = a
        p[name] = nc.dram_tensor(f"in_{name}_dram", a.shape, _mybir.dt.from_np(a.dtype), kind="ExternalInput").ap()
    out = nc.dram_tensor("out_0_dram", (N, D), _mybir.dt.float32, kind="ExternalOutput").ap()
    gnn_kernel(nc, p, out)
    r = _run(nc, [arrays], core_ids=[0])
    return r.results[0]["out_0_dram"]
```
